# Optimizing a Trainium2 kernel written in Bass

```python
import numpy as np
import jax
import jax.numpy as jnp

def _softmax(x, axis=-1):
    return jax.nn.softmax(x, axis=axis)

def _gelu(x):
    return jax.nn.gelu(x, approximate=True)

def _silu(x):
    return jax.nn.silu(x)

def _sigmoid(x):
    return jax.nn.sigmoid(x)

def _layernorm(x, axis=-1, eps=1e-05):
    m = jnp.mean(x, axis=axis, keepdims=True)
    v = jnp.var(x, axis=axis, keepdims=True)
    return (x - m) / jnp.sqrt(v + eps)

def _scatter_add(tgt, idx, src, axis=0):
    return tgt.at[idx].add(src)

def _segment_sum(src, seg, n):
    return jax.ops.segment_sum(src, seg, n)
kernel_name = 'mk_hybrid_d2_jaxref_r8_ea5b22'

def setup_inputs(seed: int=0):
    np.random.seed(seed)
    _w = jnp.asarray

    def _L0_attn_a_setup():
        import jax, jax.numpy as jnp
        import numpy as np
        N_HEADS = 16
        BUCKETS = 32
        MAX_REL = 64
        ATT_SPAN = BUCKETS
        LN_EPS = 1e-07

        def make_log_bucket_position(relative_pos, bucket_size, max_position):
            sign = jnp.sign(relative_pos)
            mid = bucket_size // 2
            abs_pos = jnp.where((relative_pos < mid) & (relative_pos > -mid), mid - 1, jnp.abs(relative_pos))
            log_pos = jnp.ceil(jnp.log(abs_pos / mid) / jnp.log((max_position - 1) / mid) * (mid - 1)) + mid
            bucket_pos = jnp.where(abs_pos <= mid, abs_pos, log_pos * sign)
            return bucket_pos.astype(jnp.int32)

        def build_relative_position(q_size, k_size, bucket_size, max_position):
            rel = jnp.arange(q_size)[:, None] - jnp.arange(k_size)[None, :]
            rel = make_log_bucket_position(rel, bucket_size, max_position)
            return rel.astype(jnp.int32)
        key = jax.random.key(seed)
        ks = jax.random.split(key, 16)
        B, S, H = (4, 128, 128)
        std = 0.02
        inp = {'hidden_states': jax.random.normal(ks[0], (B, S, H), jnp.float32), 'attention_mask': jnp.ones((B, S), jnp.float32), 'rel_embeddings': jax.random.normal(ks[1], (2 * ATT_SPAN, H), jnp.float32) * std, 'Wq': jax.random.normal(ks[2], (H, H), jnp.float32) * std, 'bq': jnp.zeros((H,), jnp.float32), 'Wk': jax.random.normal(ks[3], (H, H), jnp.float32) * std, 'bk': jnp.zeros((H,), jnp.float32), 'Wv': jax.random.normal(ks[4], (H, H), jnp.float32) * std, 'bv': jnp.zeros((H,), jnp.float32), 'Wo': jax.random.normal(ks[5], (H, H), jnp.float32) * std, 'bo': jnp.zeros((H,), jnp.float32), 'ln_scale': jnp.ones((H,), jnp.float32), 'ln_bias': jnp.zeros((H,), jnp.float32)}
        return inp
    _L0_attn_a_in = _L0_attn_a_setup()

    def _L0_attn_b_setup():
        import jax, jax.numpy as jnp
        import numpy as np
        key = jax.random.key(seed)
        B, L, D, N = (2, 256, 128, 16)
        ks = jax.random.split(key, 8)
        s = 1.0 / np.sqrt(D)
        A_log = jnp.log(jnp.broadcast_to(jnp.arange(1, N + 1, dtype=jnp.float32), (D, N)))
        return {'x': jax.random.normal(ks[0], (B, L, D), jnp.float32), 'Wz': jax.random.normal(ks[1], (D, D), jnp.float32) * s, 'bz': jnp.zeros((D,), jnp.float32), 'Wx': jax.random.normal(ks[2], (D, D), jnp.float32) * s, 'bx': jnp.zeros((D,), jnp.float32), 'WB': jax.random.normal(ks[3], (D, N), jnp.float32) * s, 'bB': jnp.zeros((N,), jnp.float32), 'WC': jax.random.normal(ks[4], (D, N), jnp.float32) * s, 'bC': jnp.zeros((N,), jnp.float32), 'Wdt': jax.random.normal(ks[5], (D, D), jnp.float32) * s, 'bdt': jnp.zeros((D,), jnp.float32), 'A_log': A_log, 'Wout': jax.random.normal(ks[6], (D, D), jnp.float32) * s, 'bout': jnp.zeros((D,), jnp.float32)}
    _L0_attn_b_in = _L0_attn_b_setup()

    def _L0_ffn_setup():
        import jax, jax.numpy as jnp
        import numpy as np
        DIM = 128
        DEPTH = 2
        HEADS = 8
        DIM_HEAD = 64
        WINDOW = 64
        INNER = HEADS * DIM_HEAD
        HID = int(DIM * 4 * 2 / 3)
        B, N = (2, 1024)
        QK_SCALE = 8.0

        def shift_token(t):
            t1, t2 = jnp.split(t, 2, axis=-1)
            t2 = jnp.pad(t2, ((0, 0), (1, 0), (0, 0)))[:, :-1]
            return jnp.concatenate([t1, t2], axis=-1)

        def l2norm(t):
            return t / jnp.clip(jnp.linalg.norm(t, axis=-1, keepdims=True), 1e-12)

        def rotate_half(x):
            x1, x2 = jnp.split(x, 2, axis=-1)
            return jnp.concatenate([-x2, x1], axis=-1)

        def rotary_xpos(q, k):
            n = q.shape[-2]
            half_idx = jnp.arange(0, DIM_HEAD, 2, dtype=jnp.float32)
            inv_freq = 1.0 / 10000.0 ** (half_idx / DIM_HEAD)
            t = jnp.arange(n, dtype=jnp.float32)
            freqs = t[:, None] * inv_freq[None, :]
            freqs = jnp.concatenate([freqs, freqs], axis=-1)
            base = (half_idx + 0.4 * DIM_HEAD) / (1.4 * DIM_HEAD)
            power = (t - n // 2) / float(WINDOW // 2)
            scale = base[None, :] ** power[:, None]
            scale = jnp.concatenate([scale, scale], axis=-1)
            cos, sin = (jnp.cos(freqs), jnp.sin(freqs))
            q = q * cos * scale + rotate_half(q) * sin * scale
            k = k * cos / scale + rotate_half(k) * sin / scale
            return (q, k)

        def local_attention(q, k, v):
            b, h, n, d = q.shape
            w = n // WINDOW
            bq = q.reshape(b, h, w, WINDOW, d) * QK_SCALE
            bk = k.reshape(b, h, w, WINDOW, d)
            bv = v.reshape(b, h, w, WINDOW, d)

            def look_around(t):
                p = jnp.pad(t, ((0, 0), (0, 0), (1, 0), (0, 0), (0, 0)))
                return jnp.concatenate([p[:, :, :w], p[:, :, 1:]], axis=3)
            bk, bv = (look_around(bk), look_around(bv))
            bt = jnp.arange(n).reshape(w, WINDOW)
            btp = jnp.pad(bt, ((1, 0), (0, 0)), constant_values=-1)
            btk = jnp.concatenate([btp[:w], btp[1:]], axis=1)
            sim = jnp.einsum('bhwid,bhwjd->bhwij', bq, bk)
            i = bt[:, :, None]
            j = btk[:, None, :]
            mask = (i < j) | (i > j + WINDOW) | (j == -1)
            sim = jnp.where(mask, -jnp.finfo(sim.dtype).max, sim)
            attn = jax.nn.softmax(sim, axis=-1)
            out = jnp.einsum('bhwij,bhwjd->bhwid', attn, bv)
            return out.reshape(b, h, n, d)

        def _layer(x, wqkv, qs, ksc, wo, lg, lb, w1, b1, w2, b2):
            b, n, _ = x.shape
            h = shift_token(x)
            qkv = h @ wqkv
            q, k, v = jnp.split(qkv, 3, axis=-1)
            to_heads = lambda t: t.reshape(b, n, HEADS, DIM_HEAD).transpose(0, 2, 1, 3)
            q, k, v = (to_heads(q), to_heads(k), to_heads(v))
            q = l2norm(q) * qs
            k = l2norm(k) * ksc
            q, k = rotary_xpos(q, k)
            o = local_attention(q, k, v)
            o = o.transpose(0, 2, 1, 3).reshape(b, n, INNER)
            x = x + o @ wo
            h = shift_token(x)
            mu = h.mean(-1, keepdims=True)
            var = h.var(-1, keepdims=True)
            h = (h - mu) / jnp.sqrt(var + 1e-05) * lg + lb
            h = h @ w1 + b1
            a, g = jnp.split(h, 2, axis=-1)
            h = a * jax.nn.gelu(g, approximate=False)
            x = x + h @ w2 + b2
            return x
        key = jax.random.key(seed)
        ks = jax.random.split(key, 6)
        return {'x': jax.random.normal(ks[0], (B, N, DIM), jnp.float32), 'wqkv': jax.random.normal(ks[1], (DEPTH, DIM, 3 * INNER), jnp.float32) * 0.02, 'q_scale': jnp.ones((DEPTH, DIM_HEAD), jnp.float32), 'k_scale': jnp.ones((DEPTH, DIM_HEAD), jnp.float32), 'wo': jax.random.normal(ks[2], (DEPTH, INNER, DIM), jnp.float32) * 0.02, 'ln_g': jnp.ones((DEPTH, DIM), jnp.float32), 'ln_b': jnp.zeros((DEPTH, DIM), jnp.float32), 'w1': jax.random.normal(ks[3], (DEPTH, DIM, 2 * HID), jnp.float32) * 0.02, 'b1': jnp.zeros((DEPTH, 2 * HID), jnp.float32), 'w2': jax.random.normal(ks[4], (DEPTH, HID, DIM), jnp.float32) * 0.02, 'b2': jnp.zeros((DEPTH, DIM), jnp.float32)}
    _L0_ffn_in = _L0_ffn_setup()

    def _L1_attn_a_setup():
        import jax, jax.numpy as jnp
        import numpy as np
        D_MODEL = 128
        NUM_HEADS = 16
        D_HEAD = D_MODEL // NUM_HEADS
        LAMBDA_INIT = 0.8
        EPS = 1e-05
        key = jax.random.key(seed)
        ks = jax.random.split(key, 10)
        B, N = (2, 256)

        def xav(k, shape):
            fan_in, fan_out = (shape[0], shape[1])
            lim = np.sqrt(6.0 / (fan_in + fan_out))
            return jax.random.uniform(k, shape, jnp.float32, -lim, lim)
        return {'X': jax.random.normal(ks[0], (B, N, D_MODEL), jnp.float32), 'Wq': xav(ks[1], (D_MODEL, 2 * D_MODEL)), 'Wk': xav(ks[2], (D_MODEL, 2 * D_MODEL)), 'Wv': xav(ks[3], (D_MODEL, 2 * D_MODEL)), 'Wo': xav(ks[4], (2 * D_MODEL, D_MODEL)), 'lambda_q1': jax.random.normal(ks[5], (NUM_HEADS, D_HEAD), jnp.float32), 'lambda_k1': jax.random.normal(ks[6], (NUM_HEADS, D_HEAD), jnp.float32), 'lambda_q2': jax.random.normal(ks[7], (NUM_HEADS, D_HEAD), jnp.float32), 'lambda_k2': jax.random.normal(ks[8], (NUM_HEADS, D_HEAD), jnp.float32), 'rms_scale': jnp.ones((2 * D_HEAD,), jnp.float32)}
    _L1_attn_a_in = _L1_attn_a_setup()

    def _L1_attn_b_setup():
        import jax, jax.numpy as jnp
        import numpy as np
        DIM = 128
        DEPTH = 6
        LN_EPS = 1e-05

        def _layernorm(x, gamma, beta):
            mu = jnp.mean(x, axis=-1, keepdims=True)
            var = jnp.mean(jnp.square(x - mu), axis=-1, keepdims=True)
            return (x - mu) * jax.lax.rsqrt(var + LN_EPS) * gamma + beta
        key = jax.random.key(seed)
        ks = jax.random.split(key, 6)
        b, n, d = (4, 256, DIM)
        x = jax.random.normal(ks[0], (b, n, d), dtype=jnp.float32)
        w_qkv = jax.random.normal(ks[1], (DEPTH, d, 3 * d), dtype=jnp.float32) * 0.02
        w_out = jax.random.normal(ks[2], (DEPTH, d, d), dtype=jnp.float32) * 0.02
        b_out = jnp.zeros((DEPTH, d), dtype=jnp.float32)
        gamma = jnp.ones((DEPTH, d), dtype=jnp.float32)
        beta = jnp.zeros((DEPTH, d), dtype=jnp.float32)
        return {'x': x, 'w_qkv': w_qkv, 'w_out': w_out, 'b_out': b_out, 'gamma': gamma, 'beta': beta}
    _L1_attn_b_in = _L1_attn_b_setup()

    def _L1_ffn_setup():
        import jax, jax.numpy as jnp
        import numpy as np
        DIM = 128
        HIDDEN = 384
        SCALE = 1.0 / 127.0

        def _dequant(w_int, dtype):
            return w_int.astype(dtype) * jnp.asarray(SCALE, dtype)
        key = jax.random.key(seed)
        k_x, k_g, k_u, k_d = jax.random.split(key, 4)
        x = jax.random.normal(k_x, (4, 256, DIM), dtype=jnp.float32)
        w_gate = jax.random.randint(k_g, (HIDDEN, DIM), -127, 128, dtype=jnp.int32)
        w_up = jax.random.randint(k_u, (HIDDEN, DIM), -127, 128, dtype=jnp.int32)
        w_down = jax.random.randint(k_d, (DIM, HIDDEN), -127, 128, dtype=jnp.int32)
        return {'x': x, 'w_gate': w_gate, 'w_up': w_up, 'w_down': w_down}
    _L1_ffn_in = _L1_ffn_setup()
    _d = {'L0_attn_a_hidden_states': _L0_attn_a_in['hidden_states'], 'L0_attn_a_attention_mask': _L0_attn_a_in['attention_mask'], 'L0_attn_a_rel_embeddings': _L0_attn_a_in['rel_embeddings'], 'L0_attn_a_Wq': _L0_attn_a_in['Wq'], 'L0_attn_a_bq': _L0_attn_a_in['bq'], 'L0_attn_a_Wk': _L0_attn_a_in['Wk'], 'L0_attn_a_bk': _L0_attn_a_in['bk'], 'L0_attn_a_Wv': _L0_attn_a_in['Wv'], 'L0_attn_a_bv': _L0_attn_a_in['bv'], 'L0_attn_a_Wo': _L0_attn_a_in['Wo'], 'L0_attn_a_bo': _L0_attn_a_in['bo'], 'L0_attn_a_ln_scale': _L0_attn_a_in['ln_scale'], 'L0_attn_a_ln_bias': _L0_attn_a_in['ln_bias'], 'L0_attn_b_Wz': _L0_attn_b_in['Wz'], 'L0_attn_b_bz': _L0_attn_b_in['bz'], 'L0_attn_b_Wx': _L0_attn_b_in['Wx'], 'L0_attn_b_bx': _L0_attn_b_in['bx'], 'L0_attn_b_WB': _L0_attn_b_in['WB'], 'L0_attn_b_bB': _L0_attn_b_in['bB'], 'L0_attn_b_WC': _L0_attn_b_in['WC'], 'L0_attn_b_bC': _L0_attn_b_in['bC'], 'L0_attn_b_Wdt': _L0_attn_b_in['Wdt'], 'L0_attn_b_bdt': _L0_attn_b_in['bdt'], 'L0_attn_b_A_log': _L0_attn_b_in['A_log'], 'L0_attn_b_Wout': _L0_attn_b_in['Wout'], 'L0_attn_b_bout': _L0_attn_b_in['bout'], 'L0_ffn_wqkv': _L0_ffn_in['wqkv'], 'L0_ffn_q_scale': _L0_ffn_in['q_scale'], 'L0_ffn_k_scale': _L0_ffn_in['k_scale'], 'L0_ffn_wo': _L0_ffn_in['wo'], 'L0_ffn_ln_g': _L0_ffn_in['ln_g'], 'L0_ffn_ln_b': _L0_ffn_in['ln_b'], 'L0_ffn_w1': _L0_ffn_in['w1'], 'L0_ffn_b1': _L0_ffn_in['b1'], 'L0_ffn_w2': _L0_ffn_in['w2'], 'L0_ffn_b2': _L0_ffn_in['b2'], 'L1_attn_a_Wq': _L1_attn_a_in['Wq'], 'L1_attn_a_Wk': _L1_attn_a_in['Wk'], 'L1_attn_a_Wv': _L1_attn_a_in['Wv'], 'L1_attn_a_Wo': _L1_attn_a_in['Wo'], 'L1_attn_a_lambda_q1': _L1_attn_a_in['lambda_q1'], 'L1_attn_a_lambda_k1': _L1_attn_a_in['lambda_k1'], 'L1_attn_a_lambda_q2': _L1_attn_a_in['lambda_q2'], 'L1_attn_a_lambda_k2': _L1_attn_a_in['lambda_k2'], 'L1_attn_a_rms_scale': _L1_attn_a_in['rms_scale'], 'L1_attn_b_w_qkv': _L1_attn_b_in['w_qkv'], 'L1_attn_b_w_out': _L1_attn_b_in['w_out'], 'L1_attn_b_b_out': _L1_attn_b_in['b_out'], 'L1_attn_b_gamma': _L1_attn_b_in['gamma'], 'L1_attn_b_beta': _L1_attn_b_in['beta'], 'L1_ffn_w_gate': _L1_ffn_in['w_gate'], 'L1_ffn_w_up': _L1_ffn_in['w_up'], 'L1_ffn_w_down': _L1_ffn_in['w_down']}
    _x0 = _d['L0_attn_a_hidden_states']
    _d['L0_attn_a_hidden_states'] = jax.random.normal(jax.random.fold_in(jax.random.key(seed), 1), (2, 1024, 128), dtype=_x0.dtype)
    del _x0
    return _d

def reference(L0_attn_a_hidden_states, L0_attn_a_attention_mask, L0_attn_a_rel_embeddings, L0_attn_a_Wq, L0_attn_a_bq, L0_attn_a_Wk, L0_attn_a_bk, L0_attn_a_Wv, L0_attn_a_bv, L0_attn_a_Wo, L0_attn_a_bo, L0_attn_a_ln_scale, L0_attn_a_ln_bias, L0_attn_b_Wz, L0_attn_b_bz, L0_attn_b_Wx, L0_attn_b_bx, L0_attn_b_WB, L0_attn_b_bB, L0_attn_b_WC, L0_attn_b_bC, L0_attn_b_Wdt, L0_attn_b_bdt, L0_attn_b_A_log, L0_attn_b_Wout, L0_attn_b_bout, L0_ffn_wqkv, L0_ffn_q_scale, L0_ffn_k_scale, L0_ffn_wo, L0_ffn_ln_g, L0_ffn_ln_b, L0_ffn_w1, L0_ffn_b1, L0_ffn_w2, L0_ffn_b2, L1_attn_a_Wq, L1_attn_a_Wk, L1_attn_a_Wv, L1_attn_a_Wo, L1_attn_a_lambda_q1, L1_attn_a_lambda_k1, L1_attn_a_lambda_q2, L1_attn_a_lambda_k2, L1_attn_a_rms_scale, L1_attn_b_w_qkv, L1_attn_b_w_out, L1_attn_b_b_out, L1_attn_b_gamma, L1_attn_b_beta, L1_ffn_w_gate, L1_ffn_w_up, L1_ffn_w_down):

    def _L0_attn_a_ref(hidden_states, attention_mask, rel_embeddings, Wq, bq, Wk, bk, Wv, bv, Wo, bo, ln_scale, ln_bias):
        import jax, jax.numpy as jnp
        import numpy as np
        N_HEADS = 16
        BUCKETS = 32
        MAX_REL = 64
        ATT_SPAN = BUCKETS
        LN_EPS = 1e-07

        def make_log_bucket_position(relative_pos, bucket_size, max_position):
            sign = jnp.sign(relative_pos)
            mid = bucket_size // 2
            abs_pos = jnp.where((relative_pos < mid) & (relative_pos > -mid), mid - 1, jnp.abs(relative_pos))
            log_pos = jnp.ceil(jnp.log(abs_pos / mid) / jnp.log((max_position - 1) / mid) * (mid - 1)) + mid
            bucket_pos = jnp.where(abs_pos <= mid, abs_pos, log_pos * sign)
            return bucket_pos.astype(jnp.int32)

        def build_relative_position(q_size, k_size, bucket_size, max_position):
            rel = jnp.arange(q_size)[:, None] - jnp.arange(k_size)[None, :]
            rel = make_log_bucket_position(rel, bucket_size, max_position)
            return rel.astype(jnp.int32)
        B, S, H = hidden_states.shape
        nH = N_HEADS
        d = H // nH

        def split_heads(x):
            return jnp.transpose(x.reshape(B, S, nH, d), (0, 2, 1, 3))
        q = split_heads(hidden_states @ Wq + bq)
        k = split_heads(hidden_states @ Wk + bk)
        v = split_heads(hidden_states @ Wv + bv)
        scale_factor = 3
        scale = jnp.sqrt(jnp.asarray(d * scale_factor, hidden_states.dtype))
        scores = jnp.einsum('bhqd,bhkd->bhqk', q, k) / scale
        rel = build_relative_position(S, S, BUCKETS, MAX_REL)
        pos_k = (rel_embeddings @ Wk + bk).reshape(2 * ATT_SPAN, nH, d)
        pos_k = jnp.transpose(pos_k, (1, 0, 2))
        c2p_att = jnp.einsum('bhqd,hpd->bhqp', q, pos_k)
        c2p_pos = jnp.clip(rel + ATT_SPAN, 0, 2 * ATT_SPAN - 1)
        c2p = jnp.take_along_axis(c2p_att, jnp.broadcast_to(c2p_pos[None, None], (B, nH, S, S)), axis=-1)
        p2c_pos = jnp.clip(-rel + ATT_SPAN, 0, 2 * ATT_SPAN - 1)
        p2c_att = jnp.einsum('bhkd,hpd->bhkp', k, pos_k)
        p2c = jnp.take_along_axis(p2c_att, jnp.broadcast_to(p2c_pos[None, None], (B, nH, S, S)), axis=-1)
        p2c = jnp.swapaxes(p2c, -1, -2)
        scores = scores + (c2p + p2c) / scale
        probs = jax.nn.softmax(scores, axis=-1)
        ctx = jnp.einsum('bhqk,bhkd->bhqd', probs, v)
        ctx = jnp.transpose(ctx, (0, 2, 1, 3)).reshape(B, S, H)
        out = ctx @ Wo + bo + hidden_states
        mu = jnp.mean(out, axis=-1, keepdims=True)
        var = jnp.mean(jnp.square(out - mu), axis=-1, keepdims=True)
        out = (out - mu) * jax.lax.rsqrt(var + LN_EPS) * ln_scale + ln_bias
        return out

    def _L0_attn_b_ref(x, Wz, bz, Wx, bx, WB, bB, WC, bC, Wdt, bdt, A_log, Wout, bout):
        import jax, jax.numpy as jnp
        import numpy as np
        B, L, D = x.shape
        N = A_log.shape[1]
        z = jax.nn.sigmoid(x @ Wz + bz)
        x_ssm = x @ Wx + bx
        Bm = x @ WB + bB
        C = x @ WC + bC
        dt = jax.nn.softplus(x @ Wdt + bdt)
        A = -jnp.exp(A_log)
        A_bar = jnp.exp(dt[..., None] * A)
        x_db = x_ssm[..., None] * (dt[..., None] * Bm[..., None, :])
        a_scan = jnp.transpose(A_bar, (1, 0, 2, 3))
        x_scan = jnp.transpose(x_db, (1, 0, 2, 3))
        c_scan = jnp.transpose(C, (1, 0, 2))

        def ssm_step(h, inp):
            a_t, x_t, c_t = inp
            h_new = a_t * h + x_t
            y_t = jnp.einsum('bdn,bn->bd', h_new, c_t)
            return (h_new, y_t)
        h0 = jnp.zeros((B, D, N), x.dtype)
        _, y_ssm = jax.lax.scan(ssm_step, h0, (a_scan, x_scan, c_scan))
        y_ssm = jnp.transpose(y_ssm, (1, 0, 2))
        y = y_ssm * z
        return y @ Wout + bout

    def _L0_ffn_ref(x, wqkv, q_scale, k_scale, wo, ln_g, ln_b, w1, b1, w2, b2):
        import jax, jax.numpy as jnp
        import numpy as np
        DIM = 128
        DEPTH = 2
        HEADS = 8
        DIM_HEAD = 64
        WINDOW = 64
        INNER = HEADS * DIM_HEAD
        HID = int(DIM * 4 * 2 / 3)
        B, N = (2, 1024)
        QK_SCALE = 8.0

        def shift_token(t):
            t1, t2 = jnp.split(t, 2, axis=-1)
            t2 = jnp.pad(t2, ((0, 0), (1, 0), (0, 0)))[:, :-1]
            return jnp.concatenate([t1, t2], axis=-1)

        def l2norm(t):
            return t / jnp.clip(jnp.linalg.norm(t, axis=-1, keepdims=True), 1e-12)

        def rotate_half(x):
            x1, x2 = jnp.split(x, 2, axis=-1)
            return jnp.concatenate([-x2, x1], axis=-1)

        def rotary_xpos(q, k):
            n = q.shape[-2]
            half_idx = jnp.arange(0, DIM_HEAD, 2, dtype=jnp.float32)
            inv_freq = 1.0 / 10000.0 ** (half_idx / DIM_HEAD)
            t = jnp.arange(n, dtype=jnp.float32)
            freqs = t[:, None] * inv_freq[None, :]
            freqs = jnp.concatenate([freqs, freqs], axis=-1)
            base = (half_idx + 0.4 * DIM_HEAD) / (1.4 * DIM_HEAD)
            power = (t - n // 2) / float(WINDOW // 2)
            scale = base[None, :] ** power[:, None]
            scale = jnp.concatenate([scale, scale], axis=-1)
            cos, sin = (jnp.cos(freqs), jnp.sin(freqs))
            q = q * cos * scale + rotate_half(q) * sin * scale
            k = k * cos / scale + rotate_half(k) * sin / scale
            return (q, k)

        def local_attention(q, k, v):
            b, h, n, d = q.shape
            w = n // WINDOW
            bq = q.reshape(b, h, w, WINDOW, d) * QK_SCALE
            bk = k.reshape(b, h, w, WINDOW, d)
            bv = v.reshape(b, h, w, WINDOW, d)

            def look_around(t):
                p = jnp.pad(t, ((0, 0), (0, 0), (1, 0), (0, 0), (0, 0)))
                return jnp.concatenate([p[:, :, :w], p[:, :, 1:]], axis=3)
            bk, bv = (look_around(bk), look_around(bv))
            bt = jnp.arange(n).reshape(w, WINDOW)
            btp = jnp.pad(bt, ((1, 0), (0, 0)), constant_values=-1)
            btk = jnp.concatenate([btp[:w], btp[1:]], axis=1)
            sim = jnp.einsum('bhwid,bhwjd->bhwij', bq, bk)
            i = bt[:, :, None]
            j = btk[:, None, :]
            mask = (i < j) | (i > j + WINDOW) | (j == -1)
            sim = jnp.where(mask, -jnp.finfo(sim.dtype).max, sim)
            attn = jax.nn.softmax(sim, axis=-1)
            out = jnp.einsum('bhwij,bhwjd->bhwid', attn, bv)
            return out.reshape(b, h, n, d)

        def _layer(x, wqkv, qs, ksc, wo, lg, lb, w1, b1, w2, b2):
            b, n, _ = x.shape
            h = shift_token(x)
            qkv = h @ wqkv
            q, k, v = jnp.split(qkv, 3, axis=-1)
            to_heads = lambda t: t.reshape(b, n, HEADS, DIM_HEAD).transpose(0, 2, 1, 3)
            q, k, v = (to_heads(q), to_heads(k), to_heads(v))
            q = l2norm(q) * qs
            k = l2norm(k) * ksc
            q, k = rotary_xpos(q, k)
            o = local_attention(q, k, v)
            o = o.transpose(0, 2, 1, 3).reshape(b, n, INNER)
            x = x + o @ wo
            h = shift_token(x)
            mu = h.mean(-1, keepdims=True)
            var = h.var(-1, keepdims=True)
            h = (h - mu) / jnp.sqrt(var + 1e-05) * lg + lb
            h = h @ w1 + b1
            a, g = jnp.split(h, 2, axis=-1)
            h = a * jax.nn.gelu(g, approximate=False)
            x = x + h @ w2 + b2
            return x
        for l in range(DEPTH):
            x = _layer(x, wqkv[l], q_scale[l], k_scale[l], wo[l], ln_g[l], ln_b[l], w1[l], b1[l], w2[l], b2[l])
        return x

    def _L1_attn_a_ref(X, Wq, Wk, Wv, Wo, lambda_q1, lambda_k1, lambda_q2, lambda_k2, rms_scale):
        import jax, jax.numpy as jnp
        import numpy as np
        D_MODEL = 128
        NUM_HEADS = 16
        D_HEAD = D_MODEL // NUM_HEADS
        LAMBDA_INIT = 0.8
        EPS = 1e-05
        B, N, _ = X.shape
        H, Dh = (NUM_HEADS, D_HEAD)
        Q = (X @ Wq).reshape(B, N, H, 2 * Dh).transpose(0, 2, 1, 3)
        K = (X @ Wk).reshape(B, N, H, 2 * Dh).transpose(0, 2, 1, 3)
        V = (X @ Wv).reshape(B, N, H, 2 * Dh).transpose(0, 2, 1, 3)
        Q1, Q2 = (Q[..., :Dh], Q[..., Dh:])
        K1, K2 = (K[..., :Dh], K[..., Dh:])
        lam = jnp.exp(jnp.sum(lambda_q1 * lambda_k1, -1)) - jnp.exp(jnp.sum(lambda_q2 * lambda_k2, -1)) + LAMBDA_INIT
        scaling = 1.0 / np.sqrt(Dh)
        causal = jnp.tril(jnp.ones((N, N), bool))
        neg_inf = jnp.float32(-jnp.inf)
        A1 = jnp.einsum('bhqd,bhkd->bhqk', Q1, K1) * scaling
        A2 = jnp.einsum('bhqd,bhkd->bhqk', Q2, K2) * scaling
        A1 = jnp.where(causal, A1, neg_inf)
        A2 = jnp.where(causal, A2, neg_inf)
        attn = jax.nn.softmax(A1, axis=-1) - lam[None, :, None, None] * jax.nn.softmax(A2, axis=-1)
        O = jnp.einsum('bhqk,bhkd->bhqd', attn, V)
        rms = jnp.sqrt(jnp.mean(O * O, axis=-1, keepdims=True) + EPS)
        O = O / rms * rms_scale
        O = O * (1.0 - LAMBDA_INIT)
        O = O.transpose(0, 2, 1, 3).reshape(B, N, H * 2 * Dh)
        return O @ Wo

    def _L1_attn_b_ref(x, w_qkv, w_out, b_out, gamma, beta):
        import jax, jax.numpy as jnp
        import numpy as np
        DIM = 128
        DEPTH = 6
        LN_EPS = 1e-05

        def _layernorm(x, gamma, beta):
            mu = jnp.mean(x, axis=-1, keepdims=True)
            var = jnp.mean(jnp.square(x - mu), axis=-1, keepdims=True)
            return (x - mu) * jax.lax.rsqrt(var + LN_EPS) * gamma + beta
        depth = w_qkv.shape[0]
        for l in range(depth):
            residual = x
            h = _layernorm(x, gamma[l], beta[l])
            qkv = h @ w_qkv[l]
            q, k, v = jnp.split(qkv, 3, axis=-1)
            q = jax.nn.softmax(q, axis=1)
            k = jax.nn.softmax(k, axis=2)
            context = jnp.einsum('bic,bjc->bij', k, v)
            out = jnp.einsum('bic,bij->bjc', q, context)
            out = out @ w_out[l] + b_out[l]
            x = out + residual
        return x

    def _L1_ffn_ref(x, w_gate, w_up, w_down):
        import jax, jax.numpy as jnp
        import numpy as np
        DIM = 128
        HIDDEN = 384
        SCALE = 1.0 / 127.0

        def _dequant(w_int, dtype):
            return w_int.astype(dtype) * jnp.asarray(SCALE, dtype)
        wg = _dequant(w_gate, x.dtype)
        wu = _dequant(w_up, x.dtype)
        wd = _dequant(w_down, x.dtype)
        gate = jnp.einsum('bsd,hd->bsh', x, wg)
        up = jnp.einsum('bsd,hd->bsh', x, wu)
        h = jax.nn.silu(gate) * up
        return jnp.einsum('bsh,dh->bsd', h, wd)
    x = L0_attn_a_hidden_states
    x = x + _L0_attn_a_ref(_layernorm(x, axis=-1), L0_attn_a_attention_mask, L0_attn_a_rel_embeddings, L0_attn_a_Wq, L0_attn_a_bq, L0_attn_a_Wk, L0_attn_a_bk, L0_attn_a_Wv, L0_attn_a_bv, L0_attn_a_Wo, L0_attn_a_bo, L0_attn_a_ln_scale, L0_attn_a_ln_bias)
    x = x + _L0_ffn_ref(_layernorm(x, axis=-1), L0_ffn_wqkv, L0_ffn_q_scale, L0_ffn_k_scale, L0_ffn_wo, L0_ffn_ln_g, L0_ffn_ln_b, L0_ffn_w1, L0_ffn_b1, L0_ffn_w2, L0_ffn_b2)
    x = x + _L0_attn_b_ref(_layernorm(x, axis=-1), L0_attn_b_Wz, L0_attn_b_bz, L0_attn_b_Wx, L0_attn_b_bx, L0_attn_b_WB, L0_attn_b_bB, L0_attn_b_WC, L0_attn_b_bC, L0_attn_b_Wdt, L0_attn_b_bdt, L0_attn_b_A_log, L0_attn_b_Wout, L0_attn_b_bout)
    x = x + _L0_ffn_ref(_layernorm(x, axis=-1), L0_ffn_wqkv, L0_ffn_q_scale, L0_ffn_k_scale, L0_ffn_wo, L0_ffn_ln_g, L0_ffn_ln_b, L0_ffn_w1, L0_ffn_b1, L0_ffn_w2, L0_ffn_b2)
    x = x + _L1_attn_a_ref(_layernorm(x, axis=-1), L1_attn_a_Wq, L1_attn_a_Wk, L1_attn_a_Wv, L1_attn_a_Wo, L1_attn_a_lambda_q1, L1_attn_a_lambda_k1, L1_attn_a_lambda_q2, L1_attn_a_lambda_k2, L1_attn_a_rms_scale)
    x = x + _L1_ffn_ref(_layernorm(x, axis=-1), L1_ffn_w_gate, L1_ffn_w_up, L1_ffn_w_down)
    x = x + _L1_attn_b_ref(_layernorm(x, axis=-1), L1_attn_b_w_qkv, L1_attn_b_w_out, L1_attn_b_b_out, L1_attn_b_gamma, L1_attn_b_beta)
    x = x + _L1_ffn_ref(_layernorm(x, axis=-1), L1_ffn_w_gate, L1_ffn_w_up, L1_ffn_w_down)
    return x

_drawn_inputs = setup_inputs


def setup_inputs(seed=0):
    import zlib

    import numpy as np

    out = dict(_drawn_inputs(seed))
    spreads = {'L0_attn_a_bq': (0.0, 0.8),
     'L0_attn_a_bk': (0.0, 0.8),
     'L0_attn_a_bv': (0.0, 0.1),
     'L0_attn_a_bo': (0.0, 0.1),
     'L0_attn_a_ln_scale': (1.0, 0.2),
     'L0_attn_a_ln_bias': (0.0, 0.1),
     'L0_attn_b_bz': (0.0, 0.1),
     'L0_attn_b_bx': (0.0, 0.1),
     'L0_attn_b_bB': (0.0, 0.1),
     'L0_attn_b_bC': (0.0, 0.1),
     'L0_attn_b_bdt': (0.0, 0.1),
     'L0_attn_b_bout': (0.0, 0.1),
     'L0_ffn_q_scale': (1.0, 0.6),
     'L0_ffn_k_scale': (1.0, 0.6),
     'L0_ffn_ln_g': (1.0, 0.6),
     'L0_ffn_ln_b': (0.0, 0.8),
     'L0_ffn_b1': (0.0, 0.791),
     'L0_ffn_b2': (0.0, 0.1),
     'L1_attn_a_rms_scale': (1.0, 0.6),
     'L1_attn_b_b_out': (0.0, 2.0),
     'L1_attn_b_gamma': (1.0, 0.6),
     'L1_attn_b_beta': (0.0, 2.0)}
    factors = {'L0_attn_a_rel_embeddings': 8.0,
     'L0_attn_a_Wq': 8.0,
     'L0_attn_a_Wk': 8.0,
     'L0_attn_a_Wv': 8.0,
     'L0_ffn_w1': 3.026,
     'L0_ffn_w2': 2.979,
     'L1_attn_b_w_qkv': 24.906,
     'L1_attn_b_w_out': 24.997}
    for name, (base, spread) in spreads.items():
        noise = np.random.default_rng([zlib.crc32(name.encode()), seed]).standard_normal(out[name].shape)
        drawn = base * np.exp(spread * noise) if base else spread * noise
        out[name] = jnp.asarray(drawn.astype(out[name].dtype))
    for name, factor in factors.items():
        out[name] = (out[name] * factor).astype(out[name].dtype)
    return out
```

```python
import math
from contextlib import ExitStack, contextmanager

import numpy as np

import concourse.bass as bass
from concourse import mybir

F32 = mybir.dt.float32
BF16 = mybir.dt.bfloat16
I32 = mybir.dt.int32
ALU = mybir.AluOpType
ACT = mybir.ActivationFunctionType
AX = mybir.AxisListType

P = 128
D = 128
TOK = 2048
NT = TOK // P
NCH = TOK // 512


class Stage:

    def __init__(self, nc, tag):
        self.nc, self.tag, self.stack, self.sems = nc, tag, ExitStack(), []

    def sb(self, name, shape, dt=F32):
        return self.stack.enter_context(self.nc.sbuf_tensor(f"{self.tag}_{name}", shape, dt))

    def ps(self, name, shape, dt=F32):
        return self.stack.enter_context(self.nc.psum_tensor(f"{self.tag}_{name}", shape, dt))

    def sem(self, name):
        s = self.nc.alloc_semaphore(name=f"{self.tag}_{name}")
        self.sems.append(s)
        return s

    def dram(self, name, shape, dt=F32):
        return self.nc.dram_tensor(f"{self.tag}_{name}", shape, dt).ap()


@contextmanager
def stage(nc, tag):
    st = Stage(nc, tag)
    yield st
    nc.clear_and_free_semaphores(st.sems)
    nc.all_engine_barrier()
    st.stack.close()


def layer_norm(nc, st, x, out, eps, tag=""):
    stats = st.sb("stats" + tag, [P, NT, 6])
    mean = st.sb("mean" + tag, [P, NT])
    diff = st.sb("diff" + tag, [P, NT])
    ssq = st.sb("ssq" + tag, [P, NT])
    rstd = st.sb("rstd" + tag, [P, NT])
    stats_done = st.sem("stats_done" + tag)
    moments = st.sem("moments" + tag)
    std_ready = st.sem("std_ready" + tag)
    rstd_ready = st.sem("rstd_ready" + tag)
    normed = st.sem("normed" + tag)
    with nc.Block() as block:

        @block.vector
        def _(dve):
            with dve.Fori(0, NT) as t:
                dve.bn_stats(stats[:, t, :], x[:, t, :]).then_inc(stats_done, 1)
            dve.wait_ge(stats_done, NT)
            dve.tensor_tensor(mean[:], stats[:, :, 1], stats[:, :, 4], ALU.add).then_inc(moments, 1)
            dve.tensor_tensor(diff[:], stats[:, :, 1], stats[:, :, 4], ALU.subtract).then_inc(moments, 1)
            dve.tensor_tensor(ssq[:], stats[:, :, 2], stats[:, :, 5], ALU.add).then_inc(moments, 1)
            dve.wait_ge(moments, 3)
            dve.tensor_scalar(mean[:], mean[:], 0.5, None, ALU.mult).then_inc(moments, 1)
            dve.tensor_tensor(diff[:], diff[:], diff[:], ALU.mult).then_inc(moments, 1)
            dve.tensor_scalar(ssq[:], ssq[:], 1.0 / D, eps, ALU.mult, ALU.add).then_inc(moments, 1)
            dve.wait_ge(moments, 6)
            dve.scalar_tensor_tensor(ssq[:], diff[:], 0.25, ssq[:], ALU.mult, ALU.add).then_inc(moments, 1)
            dve.wait_ge(std_ready, 1)
            dve.reciprocal(rstd[:], ssq[:]).then_inc(rstd_ready, 1)
            dve.wait_ge(rstd_ready, 1)
            with dve.Fori(0, NT) as t:
                dve.tensor_scalar(out[:, t, :], x[:, t, :], mean[:, bass.ts(t, 1)], rstd[:, bass.ts(t, 1)],
                                  ALU.subtract, ALU.mult).then_inc(normed, 1)

        @block.scalar
        def _(act):
            act.wait_ge(moments, 7)
            act.activation(ssq[:], ssq[:], ACT.Sqrt).then_inc(std_ready, 1)


def transpose_all(nc, st, x, xT, ident, pt, tag=""):
    turned = st.sem("turned" + tag)
    kept = st.sem("kept" + tag)
    with nc.Block() as block:

        @block.tensor
        def _(pe):
            for c in range(NCH):
                if c >= 2:
                    pe.wait_ge(kept, c - 1)
                for j in range(4):
                    mm = pe.transpose(pt[:, c % 2, j * P:(j + 1) * P], x[:, 4 * c + j, :], ident[:])
                mm.then_inc(turned, 1)

        @block.vector
        def _(dve):
            for c in range(NCH):
                dve.wait_ge(turned, c + 1)
                dve.tensor_copy(xT[:, c * 512:(c + 1) * 512], pt[:, c % 2, :]).then_inc(kept, 1)


HEADS = 16
HD = D // HEADS
SEQ = 1024
BATCH = TOK // SEQ
QT = SEQ // P
BUCKETS = 32
NPOS = 2 * BUCKETS
Q_PARTS = (0, 0, 0, 1, 1, 2)
K_PARTS = (0, 1, 2, 0, 1, 0)
STACK = len(Q_PARTS) * HD
FARROWS = 9
KROWS = STACK + FARROWS


def log_bucket(r, bucket=BUCKETS, longest=64):
    mid = bucket // 2
    a = mid - 1 if abs(r) < mid else abs(r)
    if a <= mid:
        return a
    return int((math.ceil(math.log(a / mid) / math.log((longest - 1) / mid) * (mid - 1)) + mid) * (1 if r > 0 else -1))


def attn_a_constants():
    sel_c = np.zeros((NPOS, P + 3), np.float32)
    sel_p = np.zeros((NPOS, P + 3), np.float32)
    for j in range(P):
        f = log_bucket(64 - j)
        sel_c[min(max(f + BUCKETS, 0), NPOS - 1), j] += 1
        sel_p[min(max(BUCKETS - f, 0), NPOS - 1), j] += 1
    for s in (sel_c, sel_p):
        s[0, 0:P] -= 1
        s[NPOS - 1, P] -= 1
        s[0, P] += 1
        s[NPOS - 1, P + 1] = 1
        s[0, P + 2] = 1
    row, j = np.arange(P)[:, None] % 64, np.arange(P)[None, :]
    mask_c = (64 - j > row).astype(np.float32)
    mask_p = (row + j - 64 >= 64).astype(np.float32)
    heads = (np.arange(D)[:, None] // HD == np.arange(HEADS)[None, :]).astype(np.float32)
    return {"sel_c": sel_c, "sel_p": sel_p, "mask_c": mask_c, "mask_p": mask_p, "head_of": heads}


def attn_a(nc, x, d, cst):
    G = BATCH * HEADS
    inv_scale = 1.0 / math.sqrt(3 * HD)
    with stage(nc, "aa") as st:
        xn = st.sb("xn", [P, NT, D])
        ctx = st.sb("ctx", [P, QT, G, HD])
        vh = st.sb("vh", [P, QT, G, HD])
        ident = cst["ident"]
        qh = st.dram("qh", (G, KROWS, SEQ), BF16)
        kh = st.dram("kh", (2, G, KROWS, SEQ), BF16)
        tab = st.dram("tab", (G, STACK, 2 * (P + 1)), BF16)
        SKEW = P * (2 * P + 1)
        win = st.dram("win", (2, 2, QT, SKEW))
        attn_a_prepare(nc, x, d, cst, xn, vh, qh, kh, tab, win, inv_scale)
        attn_a_heads(nc, cst, ctx, vh, qh, kh, tab, win)
        attn_a_finish(nc, x, d, cst, xn, ctx)


def attn_a_prepare(nc, x, d, cst, xn, vh, qh, kh, tab, win, inv_scale):
    ident = cst["ident"]
    with stage(nc, "ap") as st:
        layer_norm(nc, st, x, xn, 1e-5)
        xT = st.sb("xT", [D, TOK])
        banks = st.ps("banks", [P, 8, 512])
        transpose_all(nc, st, xn, xT, ident, banks[:, 0:2, :])
        w = {n: st.sb(n, [D, D]) for n in ("Wq", "Wk", "Wv")}
        bq, bk = st.sb("bq", [D, 1]), st.sb("bk", [D, 1])
        bkrow, bvrow = st.sb("bkrow", [P, D]), st.sb("bvrow", [P, D])
        relT = st.sb("relT", [D, NPOS])
        sel = st.sb("sel", [NPOS, 2, P + 3])
        head_of = st.sb("head_of", [D, HEADS])
        posk = st.sb("posk", [NPOS, D])
        table = st.sb("table", [D, 2, P + 3])
        far_w = st.sb("far_w", [D, 2, 2, HEADS])
        tparts = st.sb("tparts", [D, 2, 3, P + 1], BF16)
        trest = st.sb("trest", [D, 2, P + 1])
        val = st.sb("val", [D, 2, TOK])
        rest = st.sb("rest", [D, 2, TOK])
        parts = st.sb("parts", [D, 2, 3, TOK], BF16)
        far = st.sb("far", [2 * HEADS, 2, TOK])
        far_rest = st.sb("far_rest", [2 * HEADS, 2, TOK])
        far_parts = st.sb("far_parts", [2 * HEADS, 2, 3, TOK], BF16)
        ones = st.sb("ones", [HEADS, 3, SEQ], BF16)
        zeros = st.sb("zeros", [HEADS, 3, SEQ], BF16)
        zwin = st.sb("zwin", [P, 2056])
        loaded = st.sem("loaded")
        filled = st.sem("filled")
        step = st.sem("step")
        mm_done = st.sem("mm_done")
        evac = st.sem("evac")
        copied = st.sem("copied")
        posk_ready = st.sem("posk_ready")
        table_mm, table_ready = st.sem("table_mm"), st.sem("table_ready")
        farw_ready = st.sem("farw_ready")
        far_mm, far_ready = st.sem("far_mm"), st.sem("far_ready")
        v_mm, v_ready = st.sem("v_mm"), st.sem("v_ready")
        t_done = st.sem("t_done")
        split_done, high_done, mid_done = st.sem("split_done"), st.sem("high_done"), st.sem("mid_done")
        fsplit, fhigh, fmid = st.sem("fsplit"), st.sem("fhigh"), st.sem("fmid")
        stored = st.sem("stored")
        with nc.Block() as block:

            @block.sync
            def _(sp):
                n = 0
                for name in ("Wq", "Wk", "Wv"):
                    sp.dma_start(w[name][:], d["L0_attn_a_" + name]).then_inc(loaded, 16)
                sp.dma_start(bq[:], d["L0_attn_a_bq"].rearrange("(p o) -> p o", o=1)).then_inc(loaded, 16)
                sp.dma_start(bk[:], d["L0_attn_a_bk"].rearrange("(p o) -> p o", o=1)).then_inc(loaded, 16)
                sp.dma_start(bkrow[:], d["L0_attn_a_bk"].rearrange("(o n) -> o n", o=1).to_broadcast([P, D])).then_inc(loaded, 16)
                sp.dma_start(bvrow[:], d["L0_attn_a_bv"].rearrange("(o n) -> o n", o=1).to_broadcast([P, D])).then_inc(loaded, 16)
                sp.dma_start(relT[:], d["relT"]).then_inc(loaded, 16)
                sp.dma_start(sel[:, 0, :], d["sel_c"]).then_inc(loaded, 16)
                sp.dma_start(sel[:, 1, :], d["sel_p"]).then_inc(loaded, 16)
                sp.dma_start(head_of[:], d["head_of"]).then_inc(loaded, 16)
                sp.wait_ge(filled, 3)
                for slot in range(2):
                    for side in range(2):
                        flat = win[slot, side].rearrange("t (p c) -> p t c", p=P)
                        sp.dma_start(flat, zwin[:, 0:QT * 257].rearrange("p (t c) -> p t c", t=QT)).then_inc(stored, 16)
                        n += 1
                for b in range(BATCH):
                    gs, ts = slice(b * HEADS, (b + 1) * HEADS), slice(b * SEQ, (b + 1) * SEQ)
                    sp.dma_start(qh[gs, STACK + 6:STACK + 9, :], ones[:]).then_inc(stored, 16)
                    sp.dma_start(kh[0, gs, STACK:STACK + 3, :], ones[:]).then_inc(stored, 16)
                    sp.dma_start(kh[0, gs, STACK + 3:STACK + 6, :], zeros[:]).then_inc(stored, 16)
                    sp.dma_start(kh[1, gs, STACK:STACK + 3, :], zeros[:]).then_inc(stored, 16)
                    sp.dma_start(kh[1, gs, STACK + 3:STACK + 6, :], ones[:]).then_inc(stored, 16)
                    n += 5
                sp.wait_ge(t_done, 4)
                for side, order in ((0, K_PARTS), (1, Q_PARTS)):
                    for r, part in enumerate(order):
                        for b in range(BATCH):
                            dst = tab[b * HEADS:(b + 1) * HEADS, r * HD:(r + 1) * HD, side * (P + 1):(side + 1) * (P + 1)]
                            sp.dma_start(dst, tparts[:, side, part, :]).then_inc(stored, 16)
                            n += 1
                sp.wait_ge(split_done, 2)
                for b in range(BATCH):
                    gs, ts = slice(b * HEADS, (b + 1) * HEADS), slice(b * SEQ, (b + 1) * SEQ)
                    for r in range(len(Q_PARTS)):
                        rows = slice(r * HD, (r + 1) * HD)
                        sp.dma_start(qh[gs, rows, :], parts[:, 0, Q_PARTS[r], ts]).then_inc(stored, 16)
                        sp.dma_start(kh[0, gs, rows, :], parts[:, 1, K_PARTS[r], ts]).then_inc(stored, 16)
                        sp.dma_start(kh[1, gs, rows, :], parts[:, 1, K_PARTS[r], ts]).then_inc(stored, 16)
                        n += 3
                sp.wait_ge(fsplit, 1)
                for b in range(BATCH):
                    gs, ts = slice(b * HEADS, (b + 1) * HEADS), slice(b * SEQ, (b + 1) * SEQ)
                    for sign in range(2):
                        sp.dma_start(qh[gs, STACK + 3 * sign:STACK + 3 * sign + 3, :], far_parts[sign * HEADS:(sign + 1) * HEADS, 0, :, ts]).then_inc(stored, 16)
                        sp.dma_start(kh[sign, gs, STACK + 6:STACK + 9, :], far_parts[sign * HEADS:(sign + 1) * HEADS, 1, :, ts]).then_inc(stored, 16)
                        n += 2
                sp.wait_ge(stored, 16 * n)

            @block.gpsimd
            def _(pool):
                pool.memset(zwin[:], 0.0).then_inc(filled, 1)
                pool.memset(ones[:], 1.0).then_inc(filled, 1)
                pool.memset(zeros[:], 0.0).then_inc(filled, 1)

            @block.tensor
            def _(pe):
                pe.wait_ge(loaded, 16 * 11)
                pe.matmul(banks[0:NPOS, 0, 0:D], relT[:], w["Wk"][:], start=True, stop=True).then_inc(mm_done, 1)
                pe.wait_ge(posk_ready, 1)
                for side in range(2):
                    mm = pe.matmul(banks[:, 1 + side, 0:P + 3], posk[:], sel[:, side, :], start=True, stop=True)
                mm.then_inc(table_mm, 1)
                for c in range(NCH):
                    for i, name in enumerate(("Wq", "Wk")):
                        if c >= 1:
                            pe.wait_ge(evac, 2 * (c - 1) + i + 1)
                        pe.matmul(banks[:, 3 + i, :], w[name][:], xT[:, c * 512:(c + 1) * 512], start=True,
                                  stop=True).then_inc(copied, 1)
                for c in range(NCH):
                    if c >= 1:
                        pe.wait_ge(v_ready, c)
                    for j in range(4):
                        t = 4 * c + j
                        mm = pe.matmul(banks[:, 5, j * P:(j + 1) * P], xT[:, t * P:(t + 1) * P], w["Wv"][:],
                                       start=True, stop=True)
                    mm.then_inc(v_mm, 1)
                pe.wait_ge(farw_ready, 4)
                for c in range(NCH):
                    pe.wait_ge(evac, 2 * c + 2)
                    for i in range(2):
                        if c >= 1:
                            pe.wait_ge(far_ready, 2 * (c - 1) + i + 1)
                        pe.matmul(banks[0:2 * HEADS, 6 + i, :], far_w[:, i, :, :].rearrange("p s h -> p (s h)"),
                                  val[:, i, c * 512:(c + 1) * 512], start=True, stop=True).then_inc(far_mm, 1)

            @block.vector
            def _(dve):
                dve.wait_ge(mm_done, 1)
                dve.tensor_tensor(posk[:], banks[0:NPOS, 0, 0:D], bkrow[0:NPOS, :], ALU.add).then_inc(posk_ready, 1)
                dve.wait_ge(table_mm, 1)
                dve.tensor_copy(table[:, 0, :], banks[:, 1, 0:P + 3]).then_inc(table_ready, 1)
                dve.tensor_scalar(table[:, 1, :], banks[:, 2, 0:P + 3], inv_scale, None, ALU.mult).then_inc(table_ready, 1)
                dve.wait_ge(table_ready, 2)
                for i in range(4):
                    dve.tensor_scalar(far_w[:, i // 2, i % 2, :], head_of[:], table[:, i // 2, P + 1 + i % 2:P + 2 + i % 2], None,
                                      ALU.mult).then_inc(farw_ready, 1)
                dve.tensor_copy(tparts[:, :, 0, :], table[:, :, 0:P + 1]).then_inc(t_done, 1)
                dve.wait_ge(t_done, 1)
                dve.tensor_tensor(trest[:], table[:, :, 0:P + 1], tparts[:, :, 0, :], ALU.subtract).then_inc(t_done, 1)
                dve.wait_ge(t_done, 2)
                dve.tensor_copy(tparts[:, :, 1, :], trest[:]).then_inc(t_done, 1)
                dve.wait_ge(t_done, 3)
                dve.tensor_tensor(tparts[:, :, 2, :], trest[:], tparts[:, :, 1, :], ALU.subtract).then_inc(t_done, 1)
                for c in range(NCH):
                    cs = slice(c * 512, (c + 1) * 512)
                    dve.wait_ge(copied, 2 * c + 1)
                    dve.tensor_scalar(val[:, 0, cs], banks[:, 3, :], bq[:, 0:1], inv_scale, ALU.add, ALU.mult).then_inc(evac, 1)
                    dve.wait_ge(copied, 2 * c + 2)
                    dve.tensor_scalar(val[:, 1, cs], banks[:, 4, :], bk[:, 0:1], None, ALU.add).then_inc(evac, 1)
                for i in range(2):
                    dve.wait_ge(high_done, i + 1)
                    dve.tensor_tensor(rest[:, i, :], val[:, i, :], parts[:, i, 0, :], ALU.subtract).then_inc(step, 1)
                for c in range(NCH):
                    dve.wait_ge(v_mm, c + 1)
                    b, k0 = 4 * c // QT, 4 * c % QT
                    dst = vh[:, k0:k0 + 4, b * HEADS:(b + 1) * HEADS, :].rearrange("p t g e -> p t (g e)")
                    src = banks[:, 5, :].rearrange("p (t n) -> p t n", t=4)
                    bv = bvrow[:].rearrange("p (o n) -> p o n", o=1).to_broadcast([P, 4, D])
                    dve.tensor_tensor(dst, src, bv, ALU.add).then_inc(v_ready, 1)
                for i in range(2):
                    dve.wait_ge(mid_done, i + 1)
                    dve.tensor_tensor(parts[:, i, 2, :], rest[:, i, :], parts[:, i, 1, :], ALU.subtract).then_inc(split_done, 1)
                for c in range(NCH):
                    for i in range(2):
                        dve.wait_ge(far_mm, 2 * c + i + 1)
                        dve.tensor_copy(far[:, i, c * 512:(c + 1) * 512], banks[0:2 * HEADS, 6 + i, :]).then_inc(far_ready, 1)
                dve.wait_ge(fhigh, 1)
                dve.tensor_tensor(far_rest[:], far[:], far_parts[:, :, 0, :], ALU.subtract).then_inc(step, 1)
                dve.wait_ge(fmid, 1)
                dve.tensor_tensor(far_parts[:, :, 2, :], far_rest[:], far_parts[:, :, 1, :], ALU.subtract).then_inc(fsplit, 1)

            @block.scalar
            def _(act):
                act.wait_ge(evac, 8)
                for i in range(2):
                    act.activation(parts[:, i, 0, :], val[:, i, :], ACT.Copy).then_inc(high_done, 1)
                for i in range(2):
                    act.wait_ge(step, i + 1)
                    act.activation(parts[:, i, 1, :], rest[:, i, :], ACT.Copy).then_inc(mid_done, 1)
                act.wait_ge(far_ready, 2 * NCH)
                act.activation(far_parts[:, :, 0, :], far[:], ACT.Copy).then_inc(fhigh, 1)
                act.wait_ge(step, 3)
                act.activation(far_parts[:, :, 1, :], far_rest[:], ACT.Copy).then_inc(fmid, 1)


def since(eng, sem, value):
    if not isinstance(value, int) or value > 0:
        eng.wait_ge(sem, value)


def attn_a_heads(nc, cst, ctx, vh, qh, kh, tab, win):
    ident = cst["ident"]
    G = BATCH * HEADS
    NSTEP = 2 * QT
    with stage(nc, "ah") as st:
        q_s = st.sb("q", [KROWS, 2, SEQ], BF16)
        kp_s = st.sb("kp", [KROWS, 2, SEQ], BF16)
        km_s = st.sb("km", [KROWS, 2, SEQ], BF16)
        tb_s = st.sb("tb", [STACK, 2, 2 * (P + 1)], BF16)
        band = st.sb("band", [P, 2, QT, P])
        cwin = st.sb("cwin", [P, 2, QT, 2 * P])
        pwin = st.sb("pwin", [P, 2, QT, 2 * P])
        prob = st.sb("prob", [P, 2, SEQ])
        probT = st.sb("probT", [P, 2, QT, P])
        negmax = st.sb("negmax", [P, 2])
        rowsum = st.sb("rowsum", [P, 4])
        rinv = st.sb("rinv", [P, 2])
        masks = st.sb("masks", [P, 2, P])
        scores = st.ps("scores", [P, 2, 2, 512])
        turned = st.ps("turned", [P, QT, P])
        bandp = st.ps("bandp", [P, 512])
        ctxp = st.ps("ctxp", [P, 512])
        mask_loaded = st.sem("mask_loaded")
        ops_loaded = [st.sem(f"ops_loaded{i}") for i in range(2)]
        win_stored = st.sem("win_stored")
        win_loaded = [st.sem(f"win_loaded{i}") for i in range(2)]
        band_mm, band_kept = st.sem("band_mm"), st.sem("band_kept")
        base_done, window_added = st.sem("base_done"), st.sem("window_added")
        max_ready, probs_ready = st.sem("max_ready"), st.sem("probs_ready")
        probs_turned, kept_a, kept_v = st.sem("probs_turned"), st.sem("kept_a"), st.sem("kept_v")
        pv_done, ctx_kept, rinv_ready = st.sem("pv_done"), st.sem("ctx_kept"), st.sem("rinv_ready")


        def passes(eng, run):
            run(0, True, False)
            with eng.Fori(1, G // 2 - 1) as i:
                run(i, False, False)
            run(G // 2 - 1, False, True)

        with nc.Block() as block:

            @block.sync
            def _(sp):
                def load_head(g, par):
                    sp.dma_start(q_s[:, par, :], qh[g]).then_inc(ops_loaded[par], 16)
                    sp.dma_start(kp_s[:, par, :], kh[0, g]).then_inc(ops_loaded[par], 16)
                    sp.dma_start(km_s[:, par, :], kh[1, g]).then_inc(ops_loaded[par], 16)
                    sp.dma_start(tb_s[:, par, :], tab[g]).then_inc(ops_loaded[par], 16)

                def window_trip(g, par):
                    sp.wait_ge(band_kept, 2 * QT * (g + 1))
                    for side in range(2):
                        dst = win[par, side].rearrange("t (p c) -> p t c", p=P)[:, :, 0:P]
                        sp.dma_start(dst, band[:, side, :, :]).then_inc(win_stored, 16)
                    sp.wait_ge(win_stored, 32 * (g + 1))
                    for side, buf in ((0, cwin), (1, pwin)):
                        src = win[par, side][:, 0:2 * P * P].rearrange("t (p c) -> p t c", p=P)
                        sp.dma_start(buf[:, par, :, :], src).then_inc(win_loaded[par], 16)

                def run(i, first, last):
                    for par in range(1 if last else 2):
                        g1 = 2 * i + par + 1
                        since(sp, window_added, QT * (g1 - 1))
                        load_head(g1, 1 - par)
                        window_trip(g1, 1 - par)

                sp.dma_start(masks[:, 0, :], cst["mask_c"]).then_inc(mask_loaded, 16)
                sp.dma_start(masks[:, 1, :], cst["mask_p"]).then_inc(mask_loaded, 16)
                load_head(0, 0)
                window_trip(0, 0)
                passes(sp, run)

            @block.tensor
            def _(pe):
                def band_tile(t, par):
                    ts = slice(t * P, (t + 1) * P)
                    pe.matmul(bandp[:, 0:P + 1], q_s[0:STACK, par, ts], tb_s[:, par, 0:P + 1], start=True, stop=True)
                    pe.matmul(bandp[:, P + 1:2 * P + 2], kp_s[0:STACK, par, ts], tb_s[:, par, P + 1:2 * P + 2],
                              start=True, stop=True).then_inc(band_mm, 1)

                def base(s):
                    par, t = s // QT, s % QT
                    lo = t * P
                    for bank in range(2):
                        b0, b1 = bank * 512, (bank + 1) * 512
                        todo = []
                        if max(lo + 64, b0) < b1:
                            a = max(lo + 64, b0)
                            todo.append((slice(0, P), a, b1, q_s[:, par, lo:lo + P], km_s[:, par, a:b1]))
                        if b0 < min(lo, b1):
                            a = min(lo, b1)
                            todo.append((slice(0, P), b0, a, q_s[:, par, lo:lo + P], kp_s[:, par, b0:a]))
                        if b0 <= lo < b1:
                            todo.append((slice(0, 64), lo, lo + 64, q_s[:, par, lo:lo + 64], km_s[:, par, lo:lo + 64]))
                            todo.append((slice(64, P), lo, lo + 64, q_s[:, par, lo + 64:lo + P],
                                         kp_s[:, par, lo:lo + 64]))
                        for kt, rows, cols in ((t - 1, slice(0, 64), slice(192, 256)), (t, slice(0, P), slice(64, 192)),
                                               (t + 1, slice(64, P), slice(0, 64))):
                            if 0 <= kt < QT and b0 <= kt * P < b1:
                                todo.append((rows, kt * P, kt * P + P, pwin[:, par, kt, cols], ident[:]))
                        for j, (rows, c0, c1, lhs, rhs) in enumerate(todo):
                            mm = pe.matmul(scores[rows, s % 2, bank, c0 - b0:c1 - b0], lhs, rhs, start=j == 0,
                                           stop=j == len(todo) - 1, skip_group_check=True)
                    mm.then_inc(base_done, 1)

                def turn(n, s):
                    pe.wait_ge(probs_ready, n + 1)
                    since(pe, kept_a, n)
                    since(pe, kept_v, n)
                    for kt in range(QT):
                        mm = pe.transpose(turned[:, kt, :], prob[:, s % 2, kt * P:(kt + 1) * P], ident[:])
                    mm.then_inc(probs_turned, 1)

                def times_v(n, s, g):
                    pe.wait_ge(kept_a, n + 1)
                    pe.wait_ge(kept_v, n + 1)
                    since(pe, ctx_kept, n)
                    for kt in range(QT):
                        mm = pe.matmul(ctxp[:, 0:HD], probT[:, s % 2, kt, :], vh[:, kt, bass.ts(g, 1), :],
                                       start=kt == 0, stop=kt == QT - 1)
                    mm.then_inc(pv_done, 1)

                def run(i, first, last):
                    for s in range(NSTEP):
                        n, par, t = NSTEP * i + s, s // QT, s % QT
                        if not (last and par == 1):
                            if t == 0:
                                pe.wait_ge(ops_loaded[1 - par], 64 * (i + 1 + par))
                            pe.wait_ge(band_kept, 2 * (n + QT))
                            band_tile(t, 1 - par)
                        if t == 0:
                            pe.wait_ge(win_loaded[par], 32 * (i + 1))
                        if not (first and s < 2):
                            pe.wait_ge(probs_ready, n - 1)
                        base(s)
                        if not (first and s < 2):
                            times_v(n - 2, s, (n - 2) // QT if isinstance(n, int) else 2 * i + (s - 2) // QT)
                        if not (first and s < 1):
                            turn(n - 1, s - 1)

                pe.wait_ge(ops_loaded[0], 64)
                for t in range(QT):
                    if t >= 1:
                        pe.wait_ge(band_kept, 2 * t)
                    band_tile(t, 0)
                passes(pe, run)
                n = QT * G
                times_v(n - 2, 0, G - 1)
                turn(n - 1, 1)
                times_v(n - 1, 1, G - 1)

            @block.vector
            def _(dve):
                def keep_band(t, tiles):
                    dve.wait_ge(band_mm, tiles)
                    for side in range(2):
                        o = side * (P + 1)
                        dve.scalar_tensor_tensor(band[:, side, t, :], masks[:, side, :], bandp[:, o + P:o + P + 1],
                                                 bandp[:, o:o + P], ALU.mult, ALU.add).then_inc(band_kept, 1)

                def keep_ctx(n, s, t, g):
                    dve.wait_ge(pv_done, n + 1)
                    dve.wait_ge(rinv_ready, n + 1)
                    dve.tensor_scalar(ctx[:, t, bass.ts(g, 1), :], ctxp[:, 0:HD], rinv[:, s % 2:s % 2 + 1], None,
                                      ALU.mult).then_inc(ctx_kept, 1)

                def invert(n, s):
                    dve.wait_ge(probs_ready, n + 1)
                    since(dve, ctx_kept, n - 1)
                    dve.reciprocal(rinv[:, s % 2:s % 2 + 1], rowsum[:, s % 4:s % 4 + 1]).then_inc(rinv_ready, 1)

                def keep_turned(n, s):
                    dve.wait_ge(probs_turned, n + 1)
                    since(dve, pv_done, n - 1)
                    dve.tensor_copy(probT[:, s % 2, QT // 2:QT, :], turned[:, QT // 2:QT, :]).then_inc(kept_v, 1)

                def run(i, first, last):
                    for s in range(NSTEP):
                        n, par, t = NSTEP * i + s, s // QT, s % QT
                        if not (last and par == 1):
                            if t == 0:
                                dve.wait_ge(win_stored, 32 * (2 * i + par + 1))
                            keep_band(t, n + QT + 1)
                        if t == 0:
                            dve.wait_ge(win_loaded[par], 32 * (i + 1))
                        lo, hi = max(t * P - 64, 0), min(t * P + 192, SEQ)
                        off = lo - (t * P - 64)
                        dve.wait_ge(base_done, n + 1)
                        row = scores[:, s % 2, :, :].rearrange("p b c -> p (b c)")
                        dve.tensor_tensor(row[:, lo:hi], row[:, lo:hi], cwin[:, par, t, off:off + hi - lo],
                                          ALU.add).then_inc(window_added, 1)
                        dve.wait_ge(window_added, n + 1)
                        dve.tensor_reduce(negmax[:, s % 2:s % 2 + 1], row, AX.X, ALU.max, negate=True).then_inc(max_ready, 1)
                        if not (first and s < 1):
                            invert(n - 1, s - 1)
                            keep_turned(n - 1, s - 1)
                        if not (first and s < 2):
                            keep_ctx(n - 2, s, (s - 2) % QT, (n - 2) // QT if isinstance(n, int) else 2 * i + (s - 2) // QT)

                dve.wait_ge(mask_loaded, 32)
                for t in range(QT):
                    keep_band(t, t + 1)
                passes(dve, run)
                n = QT * G
                invert(n - 1, NSTEP - 1)
                keep_turned(n - 1, NSTEP - 1)
                keep_ctx(n - 2, 0, QT - 2, G - 1)
                keep_ctx(n - 1, 1, QT - 1, G - 1)

            @block.scalar
            def _(act):
                def keep_turned(n, s):
                    act.wait_ge(probs_turned, n + 1)
                    since(act, pv_done, n - 1)
                    act.activation(probT[:, s % 2, 0:QT // 2, :], turned[:, 0:QT // 2, :], ACT.Copy).then_inc(kept_a, 1)

                def run(i, first, last):
                    for s in range(NSTEP):
                        n = NSTEP * i + s
                        if not (first and s < 1):
                            keep_turned(n - 1, s - 1)
                        act.wait_ge(max_ready, n + 1)
                        if not (first and s < 2):
                            act.wait_ge(probs_turned, n - 1)
                        if not (first and s < 4):
                            act.wait_ge(rinv_ready, n - 3)
                        act.activation(prob[:, s % 2, :], scores[:, s % 2, :, :].rearrange("p b c -> p (b c)"), ACT.Exp,
                                       bias=negmax[:, s % 2:s % 2 + 1],
                                       accum_out=rowsum[:, s % 4:s % 4 + 1]).then_inc(probs_ready, 1)

                passes(act, run)
                keep_turned(QT * G - 1, NSTEP - 1)


def attn_a_finish(nc, x, d, cst, xn, ctx):
    ident = cst["ident"]
    with stage(nc, "af") as st:
        wo = st.sb("wo", [D, D])
        rows = st.sb("rows", [P, 3, D])
        ctxT = st.sb("ctxT", [D, 2, P])
        y = st.sb("y", [P, NT, D])
        z = st.sb("z", [P, NT, D])
        banks = st.ps("banks", [P, 4, 512])
        loaded = st.sem("loaded")
        turned, kept, projected = st.sem("turned"), st.sem("kept"), st.sem("projected")
        summed, biased = st.sem("summed"), st.sem("biased")
        scaled, shifted, added = st.sem("scaled"), st.sem("shifted"), st.sem("added")
        with nc.Block() as block:

            @block.sync
            def _(sp):
                sp.dma_start(wo[:], d["L0_attn_a_Wo"]).then_inc(loaded, 16)
                for i, name in enumerate(("bo", "ln_scale", "ln_bias")):
                    src = d["L0_attn_a_" + name].rearrange("(o n) -> o n", o=1).to_broadcast([P, D])
                    sp.dma_start(rows[:, i, :], src).then_inc(loaded, 16)

            @block.tensor
            def _(pe):
                for t in range(NT):
                    b, qt = t // QT, t % QT
                    if t >= 2:
                        pe.wait_ge(kept, t - 1)
                    src = ctx[:, qt, b * HEADS:(b + 1) * HEADS, :].rearrange("p g e -> p (g e)")
                    pe.transpose(banks[:, t % 2, 0:P], src, ident[:]).then_inc(turned, 1)
                    if t == 0:
                        pe.wait_ge(loaded, 64)
                    pe.wait_ge(kept, t + 1)
                    if t >= 2:
                        pe.wait_ge(summed, t - 1)
                    pe.matmul(banks[:, 2 + t % 2, 0:D], ctxT[:, t % 2, :], wo[:], start=True, stop=True).then_inc(projected, 1)

            @block.scalar
            def _(act):
                for t in range(NT):
                    act.wait_ge(turned, t + 1)
                    if t >= 2:
                        act.wait_ge(projected, t - 1)
                    act.activation(ctxT[:, t % 2, :], banks[:, t % 2, 0:P], ACT.Copy).then_inc(kept, 1)

            @block.vector
            def _(dve):
                dve.wait_ge(loaded, 64)
                for t in range(NT):
                    dve.tensor_tensor(xn[:, t, :], xn[:, t, :], rows[:, 0, :], ALU.add).then_inc(biased, 1)
                for t in range(NT):
                    dve.wait_ge(projected, t + 1)
                    dve.wait_ge(biased, t + 1)
                    dve.tensor_tensor(y[:, t, :], banks[:, 2 + t % 2, 0:D], xn[:, t, :], ALU.add).then_inc(summed, 1)
        layer_norm(nc, st, y, z, 1e-7)
        with nc.Block() as block:

            @block.vector
            def _(dve):
                for t in range(NT):
                    dve.tensor_tensor(z[:, t, :], z[:, t, :], rows[:, 1, :], ALU.mult).then_inc(scaled, 1)
                for t in range(NT):
                    dve.wait_ge(scaled, t + 1)
                    dve.tensor_tensor(z[:, t, :], z[:, t, :], rows[:, 2, :], ALU.add).then_inc(shifted, 1)
                for t in range(NT):
                    dve.wait_ge(shifted, t + 1)
                    dve.tensor_tensor(x[:, t, :], x[:, t, :], z[:, t, :], ALU.add).then_inc(added, 1)


FF_DEPTH = 2
FF_HEADS = 8
FF_HD = 64
FF_WIN = 64
FF_INNER = FF_HEADS * FF_HD
FF_PAIRS = FF_INNER // P
HID = int(D * 4 * 2 / 3)
HID_CUT = [(0, 128), (128, 256), (256, HID)]
NEG = -1e30


def ffn_constants():
    f4 = np.float32
    half = np.arange(0, FF_HD, 2, dtype=f4)
    inv_freq = (f4(1.0) / np.power(f4(10000.0), half / f4(FF_HD))).astype(f4)
    t = np.arange(SEQ, dtype=f4)
    freqs = t[:, None] * inv_freq[None, :]
    base = ((half + f4(0.4 * FF_HD)) / f4(1.4 * FF_HD)).astype(f4)
    power = ((t - SEQ // 2) / f4(FF_WIN // 2)).astype(f4)
    scale = np.power(base[None, :], power[:, None]).astype(f4)
    cos, sin = np.cos(freqs), np.sin(freqs)
    two = lambda a: np.concatenate([a, a], axis=-1)
    signed = np.concatenate([-sin, sin], axis=-1)
    tabs = np.stack([two(cos * scale), signed * two(scale), two(cos / scale), signed / two(scale)]).astype(f4)
    rot = tabs.reshape(4, QT, P, FF_HD).transpose(2, 0, 1, 3)
    m, i = np.arange(P)[None, :], (np.arange(P) % FF_WIN)[:, None]
    allowed = (m <= i + FF_WIN) & (m >= i)
    first = allowed & ((m >= FF_WIN) | (np.arange(P)[:, None] >= FF_WIN))
    mask = np.where(np.stack([allowed, first], axis=1), 0.0, NEG).astype(f4)
    shift = np.zeros((P, 2, P), f4)
    shift[np.arange(P - 1), 0, np.arange(1, P)] = 1
    shift[P - 1, 1, 0] = 1
    return {"rot": np.ascontiguousarray(rot), "local_mask": mask, "shift": shift}


def ffn(nc, x, d, cst, tag):
    with stage(nc, tag) as st:
        u = st.sb("u", [P, NT, D])
        layer_norm(nc, st, x, u, 1e-5)
        with nc.Fori(0, FF_DEPTH) as layer:
            ffn_attention(nc, u, d, cst, layer, tag + "a")
            ffn_glu(nc, u, d, cst, layer, tag + "g")
        added = st.sem("added")
        with nc.Block() as block:

            @block.vector
            def _(dve):
                dve.tensor_tensor(x[:], x[:], u[:], ALU.add).then_inc(added, 1)


def row_of(ap, n):
    return ap.rearrange("(o n) -> o n", o=1).to_broadcast([n, ap.shape[0]])


def ffn_attention(nc, u, d, cst, layer, tag):
    ident, shift = cst["ident"], cst["shift"]
    PAD = FF_WIN
    with stage(nc, tag) as st:
        qT = st.sb("qT", [P, FF_PAIRS, TOK])
        kT = st.sb("kT", [P, FF_PAIRS, PAD + TOK])
        v_own = st.sb("v_own", [P, NT, FF_HEADS, FF_HD + 1])
        v_prev = st.sb("v_prev", [P, NT, FF_HEADS, FF_HD + 1])
        ffn_qkv(nc, u, d, cst, layer, tag + "q", qT, kT, v_own, v_prev)
        ffn_windows(nc, u, d, cst, layer, tag + "w", qT, kT, v_own, v_prev)


def ffn_qkv(nc, u, d, cst, layer, tag, qT, kT, v_own, v_prev):
    ident, shift = cst["ident"], cst["shift"]
    with stage(nc, tag) as st:
        w = st.sb("w", [D, 3 * FF_INNER])
        srow = st.sb("srow", [P, 2, FF_HD])
        rot = st.sb("rot", [P, 4, QT, FF_HD])
        hT = st.sb("hT", [D, 2, FF_WIN + P])
        sq = st.sb("sq", [P, 2, FF_HEADS, FF_HD])
        norm = st.sb("norm", [P, 2, FF_HEADS])
        rn = st.sb("rn", [P, 2, FF_HEADS])
        tc = st.sb("tc", [P, 2, FF_HEADS, FF_HD])
        ts_ = st.sb("ts", [P, 2, FF_HEADS, FF_HD])
        banks = st.ps("banks", [P, 8, 512])
        loaded, table_ready = st.sem("loaded"), st.sem("table_ready")
        shifted, h_kept, pad_zero = st.sem("shifted"), st.sem("h_kept"), st.sem("pad_zero")
        qk_done, v_done, v_kept = st.sem("qk_done"), st.sem("v_done"), st.sem("v_kept")
        squared, summed, rooted, clipped, inverted = (st.sem(n) for n in ("squared", "summed", "rooted", "clipped", "inverted"))
        by_cos, by_sin, rotated, scaled = st.sem("by_cos"), st.sem("by_sin"), st.sem("rotated"), st.sem("scaled")
        turned, kept = st.sem("turned"), st.sem("kept")
        QB, KB, V0, V1, HB, TB = 0, 1, 2, 3, 4, 6
        with nc.Block() as block:

            @block.sync
            def _(sp):
                sp.dma_start(w[:], d["L0_ffn_wqkv"][layer]).then_inc(loaded, 16)
                sp.dma_start(srow[:, 0, :], d["L0_ffn_q_scale"][bass.ts(layer, 1), :].to_broadcast([P, FF_HD])).then_inc(loaded, 16)
                sp.dma_start(srow[:, 1, :], d["L0_ffn_k_scale"][bass.ts(layer, 1), :].to_broadcast([P, FF_HD])).then_inc(loaded, 16)
                sp.dma_start(rot[:], d["rot"]).then_inc(loaded, 16)

            @block.tensor
            def _(pe):
                def turn(t):
                    pe.wait_ge(scaled, 2 * t + 2)
                    if t >= 1:
                        pe.wait_ge(kept, 2 * t)
                    for i in range(2):
                        flat = tc[:, i, :, :].rearrange("p h e -> p (h e)")
                        for c in range(FF_PAIRS):
                            mm = pe.transpose(banks[:, TB + i, c * P:(c + 1) * P], flat[:, c * P:(c + 1) * P], ident[:])
                    mm.then_inc(turned, 1)

                pe.wait_ge(pad_zero, 4)
                for t in range(NT):
                    if t >= 1:
                        pe.wait_ge(h_kept, 2 * t)
                    first = t % QT == 0
                    pe.matmul(banks[0:64, HB, 0:P], u[:, t, 0:64], ident[:], start=True, stop=True)
                    mm = pe.matmul(banks[64:P, HB, 0:P], u[:, t, 64:D], shift[:, 0, :], start=True, stop=first)
                    if not first:
                        mm = pe.matmul(banks[64:P, HB, 0:P], u[:, t - 1, 64:D], shift[:, 1, :], start=False, stop=True)
                    mm.then_inc(shifted, 1)
                    if t == 0:
                        pe.wait_ge(loaded, 64)
                    pe.wait_ge(h_kept, 2 * t + 2)
                    own, prev = hT[:, t % 2, FF_WIN:FF_WIN + P], hT[:, t % 2, 0:P]
                    if t >= 1:
                        pe.wait_ge(by_sin, 2 * t)
                        pe.wait_ge(squared, t)
                    pe.matmul(banks[:, QB, :], own, w[:, 0:FF_INNER], start=True, stop=True)
                    pe.matmul(banks[:, KB, :], own, w[:, FF_INNER:2 * FF_INNER], start=True, stop=True).then_inc(qk_done, 1)
                    if t >= 1:
                        pe.wait_ge(v_kept, 2 * t)
                    pe.matmul(banks[:, V0, :], own, w[:, 2 * FF_INNER:], start=True, stop=True)
                    pe.matmul(banks[:, V1, :], prev, w[:, 2 * FF_INNER:], start=True, stop=True).then_inc(v_done, 1)
                    if t >= 1:
                        turn(t - 1)
                turn(NT - 1)

            @block.scalar
            def _(act):
                def keep(t):
                    act.wait_ge(turned, t + 1)
                    src = banks[:, TB, :].rearrange("p (c n) -> p c n", c=FF_PAIRS)
                    act.activation(qT[:, :, t * P:(t + 1) * P], src, ACT.Copy).then_inc(kept, 1)
                    src = banks[:, TB + 1, :].rearrange("p (c n) -> p c n", c=FF_PAIRS)
                    act.activation(kT[:, :, PAD_K + t * P:PAD_K + (t + 1) * P], src, ACT.Copy).then_inc(kept, 1)

                PAD_K = FF_WIN
                act.wait_ge(pad_zero, 4)
                for t in range(NT):
                    act.wait_ge(shifted, t + 1)
                    if t >= 2:
                        act.wait_ge(v_done, t - 1)
                    if t >= 1:
                        act.wait_ge(h_kept, 2 * t)
                        act.activation(hT[:, t % 2, 0:FF_WIN], hT[:, (t - 1) % 2, P:P + FF_WIN], ACT.Copy).then_inc(h_kept, 1)
                    else:
                        act.activation(hT[:, 0, 0:FF_WIN], ident[:, 0:FF_WIN], ACT.Copy, scale=0.0).then_inc(h_kept, 1)
                    act.activation(hT[:, t % 2, FF_WIN:FF_WIN + P], banks[:, HB, 0:P], ACT.Copy).then_inc(h_kept, 1)
                    act.wait_ge(qk_done, t + 1)
                    if t >= 1:
                        act.wait_ge(summed, t)
                    act.activation(sq[:].rearrange("p i h e -> p i (h e)"), banks[:, QB:QB + 2, :], ACT.Square).then_inc(squared, 1)
                    act.wait_ge(summed, t + 1)
                    act.activation(norm[:], norm[:], ACT.Sqrt).then_inc(rooted, 1)
                    act.wait_ge(v_done, t + 1)
                    for bank, buf in ((V0, v_own), (V1, v_prev)):
                        src = banks[:, bank, :].rearrange("p (h e) -> p h e", h=FF_HEADS)
                        act.activation(buf[:, t, :, 0:FF_HD], src, ACT.Copy).then_inc(v_kept, 1)
                    if t >= 1:
                        keep(t - 1)
                keep(NT - 1)

            @block.vector
            def _(dve):
                dve.wait_ge(loaded, 64)
                half = FF_HD // 2
                for i in range(2):
                    cosrow = srow[:, i, :].rearrange("p (o e) -> p o e", o=1).to_broadcast([P, QT, FF_HD])
                    dve.tensor_tensor(rot[:, 2 * i, :, :], rot[:, 2 * i, :, :], cosrow, ALU.mult).then_inc(table_ready, 1)
                    for a, b in ((0, half), (half, 0)):
                        sinrow = srow[:, i, b:b + half].rearrange("p (o e) -> p o e", o=1).to_broadcast([P, QT, half])
                        dve.tensor_tensor(rot[:, 2 * i + 1, :, a:a + half], rot[:, 2 * i + 1, :, a:a + half], sinrow,
                                          ALU.mult).then_inc(table_ready, 1)
                dve.wait_ge(table_ready, 6)
                for t in range(NT):
                    dve.wait_ge(squared, t + 1)
                    if t >= 1:
                        dve.wait_ge(clipped, t)
                    dve.tensor_reduce(norm[:], sq[:], AX.X, ALU.add).then_inc(summed, 1)
                    if t >= 1:
                        dve.wait_ge(turned, t)
                    for i in range(2):
                        src = banks[:, QB + i, :].rearrange("p (h e) -> p h e", h=FF_HEADS)
                        cosb = rot[:, 2 * i, t % QT, :].rearrange("p (o e) -> p o e", o=1).to_broadcast([P, FF_HEADS, FF_HD])
                        dve.tensor_tensor(tc[:, i, :, :], src, cosb, ALU.mult).then_inc(by_cos, 1)
                        for a, b in ((0, half), (half, 0)):
                            sinb = rot[:, 2 * i + 1, t % QT, a:a + half].rearrange("p (o e) -> p o e", o=1)
                            mm = dve.tensor_tensor(ts_[:, i, :, a:a + half], src[:, :, b:b + half],
                                                   sinb.to_broadcast([P, FF_HEADS, half]), ALU.mult)
                            if a == 0:
                                mm.then_inc(by_cos, 1)
                        mm.then_inc(by_sin, 1)
                    dve.wait_ge(rooted, t + 1)
                    dve.tensor_scalar(rn[:], norm[:], 1e-12, None, ALU.max).then_inc(clipped, 1)
                    dve.wait_ge(clipped, t + 1)
                    dve.reciprocal(rn[:], rn[:]).then_inc(inverted, 1)
                    dve.wait_ge(inverted, t + 1)
                    for i in range(2):
                        dve.wait_ge(by_sin, 2 * t + i + 1)
                        dve.wait_ge(by_cos, 4 * t + 2 * i + 2)
                        dve.tensor_tensor(tc[:, i, :, :], tc[:, i, :, :], ts_[:, i, :, :], ALU.add).then_inc(rotated, 1)
                    for i in range(2):
                        dve.wait_ge(rotated, 2 * t + i + 1)
                        rnb = rn[:, i, :].rearrange("p (h o) -> p h o", o=1).to_broadcast([P, FF_HEADS, FF_HD])
                        dve.tensor_tensor(tc[:, i, :, :], tc[:, i, :, :], rnb, ALU.mult).then_inc(scaled, 1)

            @block.gpsimd
            def _(pool):
                pool.memset(kT[:, :, 0:FF_WIN], 0.0).then_inc(pad_zero, 1)
                pool.memset(v_own[:, :, :, FF_HD:FF_HD + 1], 1.0).then_inc(pad_zero, 1)
                pool.memset(v_prev[:, :, :, FF_HD:FF_HD + 1], 1.0).then_inc(pad_zero, 1)
                pool.memset(sq[:], 0.0).then_inc(pad_zero, 1)


def ffn_windows(nc, u, d, cst, layer, tag, qT, kT, v_own, v_prev):
    ident = cst["ident"]
    HB = FF_HEADS // 2
    with stage(nc, tag) as st:
        wo = st.sb("wo", [P, FF_PAIRS, D])
        mask = st.sb("mask", [P, 2, P])
        maskb = st.sb("maskb", [P, 2, P], BF16)
        identb = st.sb("identb", [P, P], BF16)
        mx = st.sb("mx", [P, 2, FF_HEADS])
        less = st.sb("less", [P, 2, FF_HEADS, P])
        prob = st.sb("prob", [P, 2, FF_HEADS, P])
        probT = st.sb("probT", [P, FF_HEADS, P])
        rinv = st.sb("rinv", [P, FF_HEADS])
        o = st.sb("o", [P, FF_HEADS, FF_HD])
        oT = st.sb("oT", [P, FF_PAIRS, P])
        scores = st.ps("scores", [P, 2, 512])
        turned = st.ps("turned", [P, 2, 512])
        outp = st.ps("outp", [P, 2, 512])
        oTp = st.ps("oTp", [P, 512])
        projp = st.ps("projp", [P, 512])
        loaded, cast = st.sem("loaded"), st.sem("cast")
        scored, max_ready, lessened, probs_ready = (st.sem(n) for n in ("scored", "max_ready", "lessened", "probs_ready"))
        probs_turned, t_kept, pv_done, inverted, o_ready = (st.sem(n) for n in ("probs_turned", "t_kept", "pv_done", "inverted", "o_ready"))
        o_turned, oT_kept, projected, added = (st.sem(n) for n in ("o_turned", "oT_kept", "projected", "added"))
        with nc.Block() as block:

            @block.sync
            def _(sp):
                sp.dma_start(wo[:], d["L0_ffn_wo"][layer].rearrange("(c p) n -> p c n", p=P)).then_inc(loaded, 16)
                sp.dma_start(mask[:], d["local_mask"]).then_inc(loaded, 16)

            @block.tensor
            def _(pe):
                def score(t):
                    if t >= 1:
                        pe.wait_ge(lessened, 2 * t)
                    which = 1 if t % QT == 0 else 0
                    for b in range(2):
                        for h4 in range(HB):
                            pe.matmul(scores[:, b, h4 * P:(h4 + 1) * P], identb[:], maskb[:, which, :],
                                      start=h4 == 0, stop=False, skip_group_check=True)
                        for h4 in range(HB):
                            rows, pair = slice(b * 64, b * 64 + 64), h4
                            for w in range(2):
                                k0 = t * P + w * FF_WIN
                                mm = pe.matmul(scores[w * 64:w * 64 + 64, b, h4 * P:(h4 + 1) * P],
                                               qT[rows, pair, t * P + w * 64:t * P + w * 64 + 64],
                                               kT[rows, pair, k0:k0 + P], start=False,
                                               stop=h4 == HB - 1, skip_group_check=True)
                    mm.then_inc(scored, 1)

                def turn(t):
                    pe.wait_ge(probs_ready, t + 1)
                    if t >= 1:
                        pe.wait_ge(t_kept, t)
                    for h in range(FF_HEADS):
                        mm = pe.transpose(turned[:, h // HB, h % HB * P:(h % HB + 1) * P], prob[:, t % 2, h, :], ident[:])
                    mm.then_inc(probs_turned, 1)

                def times_v(t):
                    pe.wait_ge(t_kept, t + 1)
                    if t >= 1:
                        pe.wait_ge(o_ready, 2 * t)
                    for h in range(FF_HEADS):
                        slot = h % 2 * HB + h // 2
                        for w, v in ((0, v_prev), (1, v_own)):
                            mm = pe.matmul(outp[w * 64:w * 64 + 64, h // HB, h % HB * 65:h % HB * 65 + 65],
                                           probT[:, slot, w * 64:w * 64 + 64], v[:, t, h, :], start=True, stop=True)
                    mm.then_inc(pv_done, 1)

                def project(t):
                    pe.wait_ge(o_ready, 2 * t + 2)
                    if t >= 1:
                        pe.wait_ge(oT_kept, t)
                    of = o[:].rearrange("p h e -> p (h e)")
                    for c in range(FF_PAIRS):
                        mm = pe.transpose(oTp[:, c * P:(c + 1) * P], of[:, c * P:(c + 1) * P], ident[:])
                    mm.then_inc(o_turned, 1)
                    pe.wait_ge(oT_kept, t + 1)
                    if t >= 1:
                        pe.wait_ge(added, t)
                    for c in range(FF_PAIRS):
                        mm = pe.matmul(projp[:, 0:D], oT[:, c, :], wo[:, c, :], start=c == 0, stop=c == FF_PAIRS - 1)
                    mm.then_inc(projected, 1)

                pe.wait_ge(cast, 2)
                pe.wait_ge(loaded, 32)
                for t in range(NT + 2):
                    if t < NT:
                        score(t)
                    if 2 <= t:
                        project(t - 2)
                    if 1 <= t <= NT:
                        turn(t - 1)
                        times_v(t - 1)

            @block.scalar
            def _(act):
                def keep(t):
                    act.wait_ge(probs_turned, t + 1)
                    if t >= 1:
                        act.wait_ge(pv_done, t)
                    act.activation(probT[:], turned[:].rearrange("p b (h n) -> p (b h) n", h=HB), ACT.Copy).then_inc(t_kept, 1)

                def keep_o(t):
                    act.wait_ge(o_turned, t + 1)
                    if t >= 1:
                        act.wait_ge(projected, t)
                    act.activation(oT[:].rearrange("p c n -> p (c n)"), oTp[:], ACT.Copy).then_inc(oT_kept, 1)

                for t in range(NT + 2):
                    if t < NT:
                        act.wait_ge(lessened, 2 * t + 2)
                        if t >= 2:
                            act.wait_ge(probs_turned, t - 1)
                        act.activation(prob[:, t % 2, :, :], less[:, t % 2, :, :], ACT.Exp, scale=8.0).then_inc(probs_ready, 1)
                    if 2 <= t:
                        keep_o(t - 2)
                    if 1 <= t <= NT:
                        keep(t - 1)

            @block.vector
            def _(dve):
                dve.wait_ge(loaded, 32)
                dve.tensor_copy(maskb[:], mask[:]).then_inc(cast, 1)
                dve.tensor_copy(identb[:], ident[:]).then_inc(cast, 1)

                def normalise(t):
                    dve.wait_ge(pv_done, t + 1)
                    sums = outp[:, :, 0:HB * 65].rearrange("p b (h e) -> p b h e", e=65)
                    if t >= 1:
                        dve.wait_ge(o_ready, 2 * t)
                        dve.wait_ge(o_turned, t)
                    dve.reciprocal(rinv[:].rearrange("p (b h o) -> p b h o", b=2, o=1), sums[:, :, :, 64:65]).then_inc(inverted, 1)
                    dve.wait_ge(inverted, t + 1)
                    for b in range(2):
                        rb = rinv[:, b * HB:(b + 1) * HB].rearrange("p (h o) -> p h o", o=1).to_broadcast([P, HB, FF_HD])
                        dve.tensor_tensor(o[:, b * HB:(b + 1) * HB, :], sums[:, b, :, 0:FF_HD], rb, ALU.mult).then_inc(o_ready, 1)

                def add(t):
                    dve.wait_ge(projected, t + 1)
                    dve.tensor_tensor(u[:, t, :], u[:, t, :], projp[:, 0:D], ALU.add).then_inc(added, 1)

                for t in range(NT + 2):
                    if t < NT:
                        dve.wait_ge(scored, t + 1)
                        sv = scores[:].rearrange("p b (h n) -> p b h n", h=HB)
                        mxv = mx[:, t % 2, :].rearrange("p (b h) -> p b h", b=2)
                        dve.tensor_reduce(mxv, sv, AX.X, ALU.max).then_inc(max_ready, 1)
                        dve.wait_ge(max_ready, t + 1)
                        if t >= 2:
                            dve.wait_ge(probs_ready, t - 1)
                        for b in range(2):
                            mb = mx[:, t % 2, b * HB:(b + 1) * HB].rearrange("p (h o) -> p h o", o=1).to_broadcast([P, HB, P])
                            dve.tensor_tensor(less[:, t % 2, b * HB:(b + 1) * HB, :], sv[:, b], mb, ALU.subtract).then_inc(lessened, 1)
                    if 2 <= t:
                        add(t - 2)
                    if 1 <= t <= NT:
                        normalise(t - 1)


def ffn_glu(nc, u, d, cst, layer, tag):
    ident, shift = cst["ident"], cst["shift"]
    with stage(nc, tag) as st:
        h = st.sb("h", [P, NT, D])
        hT = st.sb("hT", [D, TOK])
        w1 = st.sb("w1", [D, 2 * HID])
        w2 = st.sb("w2", [P, 3, D])
        b1 = st.sb("b1", [P, 6])
        b2 = st.sb("b2", [P, D])
        affine = st.sb("affine", [D, 2])
        act_g = st.sb("act_g", [P, 2, 3, 512])
        hid = st.sb("hid", [P, 2, 3, 512])
        banks = st.ps("banks", [P, 8, 512])
        loaded = st.sem("loaded")
        shifted, kept, biased = st.sem("shifted"), st.sem("kept"), st.sem("biased")
        turned, hT_ready = st.sem("turned"), st.sem("hT_ready")
        a_done, g_done, gelu_done, hid_done = (st.sem(n) for n in ("a_done", "g_done", "gelu_done", "hid_done"))
        down_done, added = st.sem("down_done"), st.sem("added")
        with nc.Block() as block:

            @block.sync
            def _(sp):
                sp.dma_start(w1[:], d["L0_ffn_w1"][layer]).then_inc(loaded, 16)
                for j, (a, b) in enumerate(HID_CUT):
                    sp.dma_start(w2[0:b - a, j, :], d["L0_ffn_w2"][layer][a:b, :]).then_inc(loaded, 16)
                    for i in range(2):
                        src = d["L0_ffn_b1"][layer][i * HID + a:i * HID + b].rearrange("(p o) -> p o", o=1)
                        sp.dma_start(b1[0:b - a, 3 * i + j:3 * i + j + 1], src).then_inc(loaded, 16)
                sp.dma_start(b2[:], d["L0_ffn_b2"][bass.ts(layer, 1), :].to_broadcast([P, D])).then_inc(loaded, 16)
                sp.dma_start(affine[:, 0:1], d["L0_ffn_ln_g"][layer].rearrange("(p o) -> p o", o=1)).then_inc(loaded, 16)
                sp.dma_start(affine[:, 1:2], d["L0_ffn_ln_b"][layer].rearrange("(p o) -> p o", o=1)).then_inc(loaded, 16)
                sp.wait_ge(loaded, 16 * 13)

            @block.tensor
            def _(pe):
                for t in range(NT):
                    if t >= 2:
                        pe.wait_ge(kept, t - 1)
                    first = t % QT == 0
                    mm = pe.matmul(banks[:, t % 2, 0:64], shift[:, 0, :], u[:, t, 64:D], start=True, stop=first)
                    if not first:
                        mm = pe.matmul(banks[:, t % 2, 0:64], shift[:, 1, :], u[:, t - 1, 64:D], start=False, stop=True)
                    mm.then_inc(shifted, 1)

            @block.scalar
            def _(act):
                act.activation(h[:, :, 0:64], u[:, :, 0:64], ACT.Copy)

            @block.vector
            def _(dve):
                for t in range(NT):
                    dve.wait_ge(shifted, t + 1)
                    dve.tensor_copy(h[:, t, 64:D], banks[:, t % 2, 0:64]).then_inc(kept, 1)
        layer_norm(nc, st, h, h, 1e-5)
        with nc.Block() as block:

            @block.tensor
            def _(pe):
                def turn(c):
                    for j in range(4):
                        mm = pe.transpose(banks[:, 6, j * P:(j + 1) * P], h[:, 4 * c + j, :], ident[:])
                    mm.then_inc(turned, 1)

                def down(c):
                    pe.wait_ge(hid_done, 3 * c + 3)
                    for i in range(4):
                        for j, (a, b) in enumerate(HID_CUT):
                            mm = pe.matmul(banks[:, 7, i * P:(i + 1) * P], hid[0:b - a, c % 2, j, i * P:(i + 1) * P],
                                           w2[0:b - a, j, :], start=j == 0, stop=j == 2)
                    mm.then_inc(down_done, 1)

                turn(0)
                for c in range(NCH):
                    pe.wait_ge(hT_ready, c + 1)
                    if c + 1 < NCH:
                        turn(c + 1)
                    for j, (a, b) in enumerate(HID_CUT):
                        if c >= 1:
                            pe.wait_ge(gelu_done, 3 * (c - 1) + j + 1)
                        pe.matmul(banks[0:b - a, 3 + j, :], w1[:, HID + a:HID + b], hT[:, c * 512:(c + 1) * 512],
                                  start=True, stop=True).then_inc(g_done, 1)
                        if c >= 1:
                            pe.wait_ge(hid_done, 3 * (c - 1) + j + 1)
                        pe.matmul(banks[0:b - a, j, :], w1[:, a:b], hT[:, c * 512:(c + 1) * 512],
                                  start=True, stop=True).then_inc(a_done, 1)
                    if c >= 1:
                        if c >= 2:
                            pe.wait_ge(added, c - 1)
                        down(c - 1)
                pe.wait_ge(added, NCH - 1)
                down(NCH - 1)

            @block.scalar
            def _(act):
                for c in range(NCH):
                    for j, (a, b) in enumerate(HID_CUT):
                        act.wait_ge(g_done, 3 * c + j + 1)
                        if c >= 2:
                            act.wait_ge(hid_done, 3 * (c - 2) + j + 1)
                        act.activation(act_g[0:b - a, c % 2, j, :], banks[0:b - a, 3 + j, :], ACT.Gelu,
                                       bias=b1[0:b - a, 3 + j:4 + j]).then_inc(gelu_done, 1)

            @block.vector
            def _(dve):
                b2v = b2[:].rearrange("p (o n) -> p o n", o=1).to_broadcast([P, NT, D])
                dve.tensor_tensor(u[:], u[:], b2v, ALU.add).then_inc(biased, 1)

                def keep_h(c):
                    dve.wait_ge(turned, c + 1)
                    dve.tensor_scalar(hT[:, c * 512:(c + 1) * 512], banks[:, 6, :], affine[:, 0:1], affine[:, 1:2],
                                      ALU.mult, ALU.add).then_inc(hT_ready, 1)

                def add(c):
                    dve.wait_ge(down_done, c + 1)
                    dve.wait_ge(biased, 1)
                    y = banks[:, 7, :].rearrange("p (t n) -> p t n", t=4)
                    dve.tensor_tensor(u[:, 4 * c:4 * c + 4, :], u[:, 4 * c:4 * c + 4, :], y, ALU.add).then_inc(added, 1)

                keep_h(0)
                for c in range(NCH):
                    if c + 1 < NCH:
                        keep_h(c + 1)
                    for j, (a, b) in enumerate(HID_CUT):
                        dve.wait_ge(a_done, 3 * c + j + 1)
                        dve.wait_ge(gelu_done, 3 * c + j + 1)
                        if c >= 2:
                            dve.wait_ge(down_done, c - 1)
                        dve.scalar_tensor_tensor(hid[0:b - a, c % 2, j, :], banks[0:b - a, j, :], b1[0:b - a, j:j + 1],
                                                 act_g[0:b - a, c % 2, j, :], ALU.add, ALU.mult).then_inc(hid_done, 1)
                    if c >= 1:
                        add(c - 1)
                add(NCH - 1)


NSTATE = 16


def attn_b(nc, x, d, cst):
    ident = cst["ident"]
    with stage(nc, "ab") as st:
        xn = st.sb("xn", [P, NT, D])
        layer_norm(nc, st, x, xn, 1e-5)
        xT = st.sb("xT", [D, TOK])
        banks = st.ps("banks", [P, 8, 512])
        transpose_all(nc, st, xn, xT, ident, banks[:, 0:2, :])
        z = st.sb("z", [D, TOK])
        dt = st.sb("dt", [D, TOK])
        dtx = st.sb("dtx", [D, TOK])
        y = st.sb("y", [D, TOK])
        attn_b_prepare(nc, d, xT, banks, z, dt, dtx)
        attn_b_scan(nc, d, xT, banks, dt, dtx, y)
        attn_b_finish(nc, x, d, banks, z, y)


def attn_b_prepare(nc, d, xT, banks, z, dt, dtx):
    with stage(nc, "bp") as st:
        w = st.sb("w", [D, 3, D])
        b = st.sb("b", [D, 3])
        pos = st.sb("pos", [D, TOK])
        loaded, projected = st.sem("loaded"), st.sem("projected")
        gate, dt_in, magnitude, decayed, plus_one, logged = (st.sem(n) for n in (
            "gate", "dt_in", "magnitude", "decayed", "plus_one", "logged"))
        positive, dt_ready, xs_ready, dtx_ready = (st.sem(n) for n in ("positive", "dt_ready", "xs_ready", "dtx_ready"))
        with nc.Block() as block:

            @block.sync
            def _(sp):
                for i, name in enumerate(("z", "dt", "x")):
                    sp.dma_start(w[:, i, :], d["L0_attn_b_W" + name]).then_inc(loaded, 16)
                    sp.dma_start(b[:, i:i + 1], d["L0_attn_b_b" + name].rearrange("(p o) -> p o", o=1)).then_inc(loaded, 16)

            @block.tensor
            def _(pe):
                pe.wait_ge(loaded, 96)
                for c in range(NCH):
                    for i, used in enumerate((gate, dt_in, xs_ready)):
                        if c >= 2:
                            pe.wait_ge(used, c - 1)
                        pe.matmul(banks[:, 2 * i + c % 2, :], w[:, i, :], xT[:, c * 512:(c + 1) * 512], start=True,
                                  stop=True).then_inc(projected, 1)

            @block.scalar
            def _(act):
                for c in range(NCH):
                    act.wait_ge(projected, 3 * c + 1)
                    act.activation(z[:, c * 512:(c + 1) * 512], banks[:, c % 2, :], ACT.Sigmoid, bias=b[:, 0:1]).then_inc(gate, 1)
                act.wait_ge(positive, 1)
                act.activation(dt[:], dt[:], ACT.Abs).then_inc(magnitude, 1)
                act.wait_ge(magnitude, 1)
                act.activation(dt[:], dt[:], ACT.Exp, scale=-1.0).then_inc(decayed, 1)
                act.wait_ge(plus_one, 1)
                act.activation(dt[:], dt[:], ACT.Ln).then_inc(logged, 1)

            @block.vector
            def _(dve):
                for c in range(NCH):
                    cs = slice(c * 512, (c + 1) * 512)
                    dve.wait_ge(projected, 3 * c + 2)
                    dve.tensor_scalar(dt[:, cs], banks[:, 2 + c % 2, :], b[:, 1:2], None, ALU.add).then_inc(dt_in, 1)
                    dve.wait_ge(projected, 3 * c + 3)
                    dve.tensor_scalar(dtx[:, cs], banks[:, 4 + c % 2, :], b[:, 2:3], None, ALU.add).then_inc(xs_ready, 1)
                dve.wait_ge(dt_in, NCH)
                dve.tensor_scalar(pos[:], dt[:], 0.0, None, ALU.max).then_inc(positive, 1)
                dve.wait_ge(decayed, 1)
                dve.tensor_scalar(dt[:], dt[:], 1.0, None, ALU.add).then_inc(plus_one, 1)
                dve.wait_ge(logged, 1)
                dve.tensor_tensor(dt[:], dt[:], pos[:], ALU.add).then_inc(dt_ready, 1)
                dve.wait_ge(dt_ready, 1)
                dve.wait_ge(xs_ready, NCH)
                dve.tensor_tensor(dtx[:], dtx[:], dt[:], ALU.mult).then_inc(dtx_ready, 1)


def attn_b_scan(nc, d, xT, banks, dt, dtx, y):
    with stage(nc, "bs") as st:
        wrow = st.sb("wrow", [D, 2, NSTATE])
        wrep = st.sb("wrep", [D, 2, NSTATE, D])
        brow = st.sb("brow", [D, 2, NSTATE])
        a = st.sb("a", [D, NSTATE])
        decay = st.sb("decay", [D, 2, SEQ])
        inp = st.sb("inp", [D, 2, SEQ])
        h = st.sb("h", [D, 2, SEQ])
        hc = st.sb("hc", [D, 2, SEQ])
        loaded, repeated, a_exp, a_ready = (st.sem(n) for n in ("loaded", "repeated", "a_exp", "a_ready"))
        b_done, c_done, decay_ready, inp_ready, scanned, hc_ready, y_added, y_zero = (st.sem(n) for n in (
            "b_done", "c_done", "decay_ready", "inp_ready", "scanned", "hc_ready", "y_added", "y_zero"))
        N = BATCH * NSTATE
        with nc.Block() as block:

            @block.sync
            def _(sp):
                for i, name in enumerate("BC"):
                    sp.dma_start(wrow[:, i, :], d["L0_attn_b_W" + name]).then_inc(loaded, 16)
                    sp.dma_start(brow[:, i, :], row_of(d["L0_attn_b_b" + name], D)).then_inc(loaded, 16)
                sp.dma_start(a[:], d["L0_attn_b_A_log"]).then_inc(loaded, 16)

            @block.tensor
            def _(pe):
                pe.wait_ge(repeated, 2)

                def project(i, k, bank, sem):
                    for c in range(2):
                        tok = (k // NSTATE) * SEQ + c * 512
                        mm = pe.matmul(banks[:, bank + c, :], wrep[:, i, k % NSTATE, :], xT[:, tok:tok + 512],
                                       start=True, stop=True)
                    mm.then_inc(sem, 1)

                for k in range(N):
                    if k >= 2:
                        pe.wait_ge(inp_ready, k - 1)
                    project(0, k, 2 * (k % 2), b_done)
                    if k >= 2:
                        pe.wait_ge(hc_ready, k - 1)
                    project(1, k, 4 + 2 * (k % 2), c_done)

            @block.scalar
            def _(act):
                act.wait_ge(loaded, 80)
                act.activation(a[:], a[:], ACT.Exp).then_inc(a_exp, 1)
                act.wait_ge(a_ready, 1)
                for k in range(N):
                    if k >= 2:
                        act.wait_ge(scanned, k - 1)
                    tok = (k // NSTATE) * SEQ
                    act.activation(decay[:, k % 2, :], dt[:, tok:tok + SEQ], ACT.Exp,
                                   scale=a[:, k % NSTATE:k % NSTATE + 1]).then_inc(decay_ready, 1)

            @block.vector
            def _(dve):
                dve.wait_ge(loaded, 80)
                for i in range(2):
                    src = wrow[:, i, :].rearrange("p (n o) -> p n o", o=1).to_broadcast([D, NSTATE, D])
                    dve.tensor_copy(wrep[:, i, :, :], src).then_inc(repeated, 1)
                dve.wait_ge(a_exp, 1)
                dve.tensor_scalar(a[:], a[:], -1.0, None, ALU.mult).then_inc(a_ready, 1)

                def feed(k):
                    tok, n = (k // NSTATE) * SEQ, k % NSTATE
                    dve.wait_ge(b_done, k + 1)
                    bank = 2 * (k % 2)
                    if k >= 2:
                        dve.wait_ge(scanned, k - 1)
                    dve.scalar_tensor_tensor(inp[:, k % 2, :], banks[:, bank:bank + 2, :].rearrange("p b c -> p (b c)"),
                                             brow[:, 0, n:n + 1], dtx[:, tok:tok + SEQ], ALU.add, ALU.mult).then_inc(inp_ready, 1)

                def scan(k):
                    dve.wait_ge(decay_ready, k + 1)
                    dve.wait_ge(inp_ready, k + 1)
                    if k >= 2:
                        dve.wait_ge(hc_ready, k - 1)
                    dve.tensor_tensor_scan(h[:, k % 2, :], decay[:, k % 2, :], inp[:, k % 2, :], 0.0, ALU.mult,
                                           ALU.add).then_inc(scanned, 1)

                def weigh(k):
                    n = k % NSTATE
                    dve.wait_ge(c_done, k + 1)
                    dve.wait_ge(scanned, k + 1)
                    if k >= 2:
                        dve.wait_ge(y_added, k - 1)
                    bank = 4 + 2 * (k % 2)
                    dve.scalar_tensor_tensor(hc[:, k % 2, :], banks[:, bank:bank + 2, :].rearrange("p b c -> p (b c)"),
                                             brow[:, 1, n:n + 1], h[:, k % 2, :], ALU.add, ALU.mult).then_inc(hc_ready, 1)

                feed(0)
                for k in range(N):
                    scan(k)
                    if k + 1 < N:
                        feed(k + 1)
                    weigh(k)

            @block.gpsimd
            def _(pool):
                pool.memset(y[:], 0.0).then_inc(y_zero, 1)
                pool.wait_ge(y_zero, 1)
                for k in range(N):
                    tok = (k // NSTATE) * SEQ
                    pool.wait_ge(hc_ready, k + 1)
                    if k >= 1:
                        pool.wait_ge(y_added, k)
                    pool.tensor_tensor(y[:, tok:tok + SEQ], y[:, tok:tok + SEQ], hc[:, k % 2, :], ALU.add).then_inc(y_added, 1)


def attn_b_finish(nc, x, d, banks, z, y):
    with stage(nc, "bf") as st:
        w = st.sb("w", [D, D])
        b = st.sb("b", [P, D])
        loaded, gated, biased, projected, added = (st.sem(n) for n in ("loaded", "gated", "biased", "projected", "added"))
        with nc.Block() as block:

            @block.sync
            def _(sp):
                sp.dma_start(w[:], d["L0_attn_b_Wout"]).then_inc(loaded, 16)
                sp.dma_start(b[:], row_of(d["L0_attn_b_bout"], P)).then_inc(loaded, 16)

            @block.tensor
            def _(pe):
                pe.wait_ge(loaded, 32)
                for c in range(NCH):
                    pe.wait_ge(gated, c + 1)
                    for j in range(4):
                        t = 4 * c + j
                        mm = pe.matmul(banks[:, c, j * P:(j + 1) * P], y[:, t * P:(t + 1) * P], w[:], start=True, stop=True)
                    mm.then_inc(projected, 1)

            @block.vector
            def _(dve):
                for c in range(NCH):
                    cs = slice(c * 512, (c + 1) * 512)
                    dve.tensor_tensor(y[:, cs], y[:, cs], z[:, cs], ALU.mult).then_inc(gated, 1)
                dve.wait_ge(loaded, 32)
                bv = b[:].rearrange("p (o n) -> p o n", o=1).to_broadcast([P, NT, D])
                dve.tensor_tensor(x[:], x[:], bv, ALU.add).then_inc(biased, 1)
                dve.wait_ge(biased, 1)
                for c in range(NCH):
                    dve.wait_ge(projected, c + 1)
                    src = banks[:, c, :].rearrange("p (t n) -> p t n", t=4)
                    dve.tensor_tensor(x[:, 4 * c:4 * c + 4, :], x[:, 4 * c:4 * c + 4, :], src, ALU.add).then_inc(added, 1)


DF_HD = 8
DF_V = 2 * DF_HD
LAMBDA_INIT = 0.8
DF_STACK = len(Q_PARTS) * DF_HD


def diff(nc, x, d, cst):
    G = BATCH * HEADS
    with stage(nc, "df") as st:
        qh = st.dram("qh", (2 * G, DF_STACK, SEQ), BF16)
        kh = st.dram("kh", (2 * G, DF_STACK, SEQ), BF16)
        ctx = st.sb("ctx", [P, QT, G, DF_V])
        vh = st.sb("vh", [P, QT, G, DF_V])
        neglam = st.sb("neglam", [P, G])
        diff_prepare(nc, x, d, cst, qh, kh, vh, neglam)
        diff_heads(nc, cst, d, ctx, vh, qh, kh, neglam)
        diff_finish(nc, x, d, cst, ctx)


def diff_prepare(nc, x, d, cst, qh, kh, vh, neglam):
    ident = cst["ident"]
    WD = HEADS * DF_V
    with stage(nc, "dp") as st:
        banks = st.ps("banks", [P, 8, 512])
        w = st.sb("w", [D, 3, WD])
        lamrow = st.sb("lamrow", [P, 4, HEADS * DF_HD])
        lamprod = st.sb("lamprod", [P, 2, HEADS * DF_HD])
        lam = st.sb("lam", [P, 2, HEADS])
        xT = st.sb("xT", [D, TOK])
        xn = st.sb("xn", [P, NT, D])
        layer_norm(nc, st, x, xn, 1e-5)
        transpose_all(nc, st, xn, xT, ident, banks[:, 0:2, :])
        val = st.sb("val", [P, 2, TOK])
        rest = st.sb("rest", [P, 2, TOK])
        parts = st.sb("parts", [P, 2, 3, TOK], BF16)
        loaded, projected, evac = st.sem("loaded"), st.sem("projected"), st.sem("evac")
        high, less, mid, split = (st.sem(n) for n in ("high", "less", "mid", "split"))
        v_mm, v_ready, stored = st.sem("v_mm"), st.sem("v_ready"), [st.sem(f"stored{i}") for i in range(2)]
        lam_step, lam_exp = st.sem("lam_step"), st.sem("lam_exp")
        UNITS, NW = 4, BATCH * 6
        with nc.Block() as block:

            @block.sync
            def _(sp):
                for i, name in enumerate("qkv"):
                    sp.dma_start(w[:, i, :], d["L1_attn_a_W" + name]).then_inc(loaded, 16)
                for i, name in enumerate(("q1", "k1", "q2", "k2")):
                    src = d["L1_attn_a_lambda_" + name].rearrange("(o h) e -> o (h e)", o=1).to_broadcast([P, HEADS * DF_HD])
                    sp.dma_start(lamrow[:, i, :], src).then_inc(loaded, 16)
                for r in range(UNITS):
                    sp.wait_ge(split, r + 1)
                    dst_all, order = ((qh, Q_PARTS), (kh, K_PARTS))[r // 2]
                    for b in range(BATCH):
                        g0 = b * HEADS + r % 2 * 8
                        for j, part in enumerate(order):
                            dst = dst_all[2 * g0:2 * g0 + 16, j * DF_HD:(j + 1) * DF_HD, :]
                            sp.dma_start(dst, parts[:, r % 2, part, b * SEQ:(b + 1) * SEQ]).then_inc(stored[r % 2], 16)
                for i in range(2):
                    sp.wait_ge(stored[i], 16 * NW * 2)

            @block.tensor
            def _(pe):
                pe.wait_ge(loaded, 7 * 16)
                for r in range(UNITS):
                    for c in range(NCH):
                        if r >= 1 or c >= 2:
                            pe.wait_ge(evac, NCH * r + c - 1)
                        lhs = w[:, r // 2, r % 2 * P:(r % 2 + 1) * P]
                        pe.matmul(banks[:, c % 2, :], lhs, xT[:, c * 512:(c + 1) * 512], start=True,
                                  stop=True).then_inc(projected, 1)
                for t in range(NT // 2):
                    if t >= 2:
                        pe.wait_ge(v_ready, t - 1)
                    for j in range(2):
                        mm = pe.matmul(banks[:, 2 + t % 2, j * WD:(j + 1) * WD], xT[:, (2 * t + j) * P:(2 * t + j + 1) * P],
                                       w[:, 2, :], start=True, stop=True)
                    mm.then_inc(v_mm, 1)

            @block.scalar
            def _(act):
                act.wait_ge(lam_step, 3)
                act.activation(lam[:], lam[:], ACT.Exp).then_inc(lam_exp, 1)
                for r in range(UNITS):
                    act.wait_ge(evac, NCH * (r + 1))
                    if r >= 2:
                        act.wait_ge(stored[r % 2], 16 * NW)
                    act.activation(parts[:, r % 2, 0, :], val[:, r % 2, :], ACT.Copy).then_inc(high, 1)
                    act.wait_ge(less, r + 1)
                    act.activation(parts[:, r % 2, 1, :], rest[:, r % 2, :], ACT.Copy).then_inc(mid, 1)

            @block.vector
            def _(dve):
                dve.wait_ge(loaded, 7 * 16)
                for i in range(2):
                    dve.tensor_tensor(lamprod[:, i, :], lamrow[:, 2 * i, :], lamrow[:, 2 * i + 1, :], ALU.mult).then_inc(lam_step, 1)
                dve.wait_ge(lam_step, 2)
                dve.tensor_reduce(lam[:], lamprod[:].rearrange("p i (h e) -> p i h e", e=DF_HD), AX.X, ALU.add).then_inc(lam_step, 1)
                for r in range(UNITS):
                    for c in range(NCH):
                        dve.wait_ge(projected, NCH * r + c + 1)
                        if r >= 2 and c == 0:
                            dve.wait_ge(split, r - 1)
                        factor = 1.0 / math.sqrt(DF_HD) if r < 2 else 1.0
                        dve.tensor_scalar(val[:, r % 2, c * 512:(c + 1) * 512], banks[:, c % 2, :], factor, None,
                                          ALU.mult).then_inc(evac, 1)
                    dve.wait_ge(high, r + 1)
                    dve.tensor_tensor(rest[:, r % 2, :], val[:, r % 2, :], parts[:, r % 2, 0, :], ALU.subtract).then_inc(less, 1)
                    dve.wait_ge(mid, r + 1)
                    dve.tensor_tensor(parts[:, r % 2, 2, :], rest[:, r % 2, :], parts[:, r % 2, 1, :], ALU.subtract).then_inc(split, 1)
                for t in range(NT // 2):
                    dve.wait_ge(v_mm, t + 1)
                    b, k0 = 2 * t // QT, 2 * t % QT
                    dst = vh[:, k0:k0 + 2, b * HEADS:(b + 1) * HEADS, :].rearrange("p t g e -> p t (g e)")
                    dve.tensor_copy(dst, banks[:, 2 + t % 2, :].rearrange("p (t n) -> p t n", t=2)).then_inc(v_ready, 1)
                dve.wait_ge(lam_exp, 1)
                for b in range(BATCH):
                    dve.tensor_tensor(neglam[:, b * HEADS:(b + 1) * HEADS], lam[:, 1, :], lam[:, 0, :], ALU.subtract).then_inc(lam_step, 1)
                dve.wait_ge(lam_step, 5)
                dve.tensor_scalar(neglam[:], neglam[:], LAMBDA_INIT, None, ALU.subtract).then_inc(lam_step, 1)


def diff_heads(nc, cst, d, ctx, vh, qh, kh, neglam):
    ident = cst["ident"]
    G = BATCH * HEADS
    NSTEP = 2 * QT
    M2 = 64
    with stage(nc, "dh") as st:
        q_s = st.sb("q", [P, 2, SEQ], BF16)
        k_s = st.sb("k", [P, 2, SEQ], BF16)
        mask = st.sb("mask", [P, P])
        maskb = st.sb("maskb", [P, P], BF16)
        identb = st.sb("identb", [P, P], BF16)
        prob = st.sb("prob", [P, 2, 2, SEQ])
        both = st.sb("both", [P, 2, SEQ])
        probT = st.sb("probT", [P, 2, QT, P])
        negmax = st.sb("negmax", [P, 2, 2])
        rowsum = st.sb("rowsum", [P, 4, 2])
        rinv = st.sb("rinv", [P, 4, 2])
        coef = st.sb("coef", [P, 2])
        scores = st.ps("scores", [P, 2, 2, 512])
        turned = st.ps("turned", [P, QT, P])
        ctxp = st.ps("ctxp", [P, 2, 512])
        mask_loaded, cast = st.sem("mask_loaded"), st.sem("cast")
        ops_loaded = [st.sem(f"ops_loaded{i}") for i in range(2)]
        scored = [st.sem(f"scored{m}") for m in range(2)]
        max_ready = [st.sem(f"max_ready{m}") for m in range(2)]
        probs_ready = [st.sem(f"probs_ready{m}") for m in range(2)]
        inverted, coef_ready, combined = st.sem("inverted"), st.sem("coef_ready"), st.sem("combined")
        probs_turned, kept_a, kept_v = st.sem("probs_turned"), st.sem("kept_a"), st.sem("kept_v")
        pv_done, ctx_kept = st.sem("pv_done"), st.sem("ctx_kept")

        def passes(eng, run):
            run(0, True, False)
            with eng.Fori(1, G // 2 - 1) as i:
                run(i, False, False)
            run(G // 2 - 1, False, True)

        def late(i, s):
            return QT * i + (s // QT) * (QT // 2) + max(0, s % QT - QT // 2)

        with nc.Block() as block:

            @block.sync
            def _(sp):
                def load_head(g, par):
                    for m in range(2):
                        rows = slice(m * M2, m * M2 + DF_STACK)
                        sp.dma_start(q_s[rows, par, :], qh[2 * g + m]).then_inc(ops_loaded[par], 16)
                        sp.dma_start(k_s[rows, par, :], kh[2 * g + m]).then_inc(ops_loaded[par], 16)

                def run(i, first, last):
                    for par in range(1 if last else 2):
                        g1 = 2 * i + par + 1
                        since(sp, scored[1], QT * (g1 - 1))
                        load_head(g1, 1 - par)

                sp.dma_start(mask[:], d["causal"]).then_inc(mask_loaded, 16)
                load_head(0, 0)
                passes(sp, run)

            @block.tensor
            def _(pe):
                def score(n, s, first):
                    par, t = s // QT, s % QT
                    width = (t + 1) * P
                    for m in range(2):
                        if not (first and s < 1):
                            pe.wait_ge(probs_ready[m], n)
                        rows = slice(m * M2, m * M2 + DF_STACK)
                        for bank in range((width + 511) // 512):
                            b0, b1 = bank * 512, min(width, bank * 512 + 512)
                            diag = b1 == width
                            mm = pe.matmul(scores[:, m, bank, 0:b1 - b0], q_s[rows, par, t * P:(t + 1) * P],
                                           k_s[rows, par, b0:b1], start=True, stop=not diag, skip_group_check=True)
                            if diag:
                                mm = pe.matmul(scores[:, m, bank, b1 - P - b0:b1 - b0], identb[:], maskb[:],
                                               start=False, stop=True, skip_group_check=True)
                        mm.then_inc(scored[m], 1)

                def turn(n, i, s):
                    t = s % QT
                    pe.wait_ge(combined, n + 1)
                    since(pe, kept_a, n)
                    since(pe, kept_v, late(i, s))
                    for kt in range(t + 1):
                        mm = pe.transpose(turned[:, kt, :], both[:, s % 2, kt * P:(kt + 1) * P], ident[:])
                    mm.then_inc(probs_turned, 1)

                def times_v(n, i, s, g):
                    t = s % QT
                    pe.wait_ge(kept_a, n + 1)
                    since(pe, kept_v, late(i, s + 1))
                    since(pe, ctx_kept, n - 1)
                    for kt in range(t + 1):
                        mm = pe.matmul(ctxp[:, s % 2, 0:DF_V], probT[:, s % 2, kt, :], vh[:, kt, bass.ts(g, 1), :],
                                       start=kt == 0, stop=kt == t)
                    mm.then_inc(pv_done, 1)

                def run(i, first, last):
                    for s in range(NSTEP):
                        n, par, t = NSTEP * i + s, s // QT, s % QT
                        if t == 0:
                            pe.wait_ge(ops_loaded[par], 64 * (i + 1))
                        score(n, s, first)
                        if not (first and s < 2):
                            j, r = (i, s - 2) if s >= 2 else (i - 1, s - 2 + NSTEP)
                            times_v(n - 2, j, r, 2 * j + r // QT)
                        if not (first and s < 1):
                            j, r = (i, s - 1) if s >= 1 else (i - 1, s - 1 + NSTEP)
                            turn(n - 1, j, r)

                pe.wait_ge(cast, 2)
                passes(pe, run)
                n, j = QT * G, G // 2 - 1
                times_v(n - 2, j, NSTEP - 2, G - 1)
                turn(n - 1, j, NSTEP - 1)
                times_v(n - 1, j, NSTEP - 1, G - 1)

            @block.vector
            def _(dve):
                dve.wait_ge(mask_loaded, 16)
                dve.tensor_copy(maskb[:], mask[:]).then_inc(cast, 1)
                dve.tensor_copy(identb[:], ident[:]).then_inc(cast, 1)

                def combine(n, s, g):
                    width = (s % QT + 1) * P
                    dve.wait_ge(probs_ready[1], n + 1)
                    since(dve, ctx_kept, n - 3)
                    dve.reciprocal(rinv[:, s % 4, :], rowsum[:, s % 4, :]).then_inc(inverted, 1)
                    dve.wait_ge(inverted, n + 1)
                    since(dve, combined, n - 1)
                    dve.scalar_tensor_tensor(coef[:, s % 2:s % 2 + 1], rinv[:, s % 4, 1:2], rowsum[:, s % 4, 0:1],
                                             neglam[:, bass.ts(g, 1)], ALU.mult, ALU.mult).then_inc(coef_ready, 1)
                    dve.wait_ge(coef_ready, n + 1)
                    since(dve, probs_turned, n - 1)
                    dve.scalar_tensor_tensor(both[:, s % 2, 0:width], prob[:, s % 2, 1, 0:width], coef[:, s % 2:s % 2 + 1],
                                             prob[:, s % 2, 0, 0:width], ALU.mult, ALU.add).then_inc(combined, 1)

                def keep_turned(n, s):
                    t = s % QT
                    if t >= QT // 2:
                        dve.wait_ge(probs_turned, n + 1)
                        since(dve, pv_done, n - 1)
                        dve.tensor_copy(probT[:, s % 2, QT // 2:t + 1, :], turned[:, QT // 2:t + 1, :]).then_inc(kept_v, 1)

                def keep_ctx(n, s, g):
                    dve.wait_ge(pv_done, n + 1)
                    dve.tensor_scalar(ctx[:, s % QT, bass.ts(g, 1), :], ctxp[:, s % 2, 0:DF_V], rinv[:, s % 4, 0:1],
                                      None, ALU.mult).then_inc(ctx_kept, 1)

                def run(i, first, last):
                    for s in range(NSTEP):
                        n, width = NSTEP * i + s, (s % QT + 1) * P

                        def before(k):
                            return (s - k, 2 * i + (s - k) // QT)

                        for m in range(2):
                            dve.wait_ge(scored[m], n + 1)
                            row = scores[:, m, :, :].rearrange("p b c -> p (b c)")[:, 0:width]
                            dve.tensor_reduce(negmax[:, s % 2, m:m + 1], row, AX.X, ALU.max, negate=True).then_inc(max_ready[m], 1)
                        if not (first and s < 1):
                            combine(n - 1, *before(1))
                        if not (first and s < 2):
                            keep_turned(n - 2, s - 2)
                        if not (first and s < 3):
                            keep_ctx(n - 3, *before(3))

                passes(dve, run)
                n, s = QT * G, NSTEP
                combine(n - 1, s - 1, G - 1)
                keep_turned(n - 2, s - 2)
                keep_ctx(n - 3, s - 3, G - 1)
                keep_turned(n - 1, s - 1)
                keep_ctx(n - 2, s - 2, G - 1)
                keep_ctx(n - 1, s - 1, G - 1)

            @block.scalar
            def _(act):
                def keep_turned(n, s):
                    hi = min(s % QT + 1, QT // 2)
                    act.wait_ge(probs_turned, n + 1)
                    since(act, pv_done, n - 1)
                    act.activation(probT[:, s % 2, 0:hi, :], turned[:, 0:hi, :], ACT.Copy).then_inc(kept_a, 1)

                def run(i, first, last):
                    for s in range(NSTEP):
                        n, width = NSTEP * i + s, (s % QT + 1) * P
                        if not (first and s < 2):
                            keep_turned(n - 2, s - 2)
                        for m in range(2):
                            act.wait_ge(max_ready[m], n + 1)
                            if m == 0 and not (first and s < 2):
                                act.wait_ge(combined, n - 1)
                            if m == 0 and not (first and s < 4):
                                act.wait_ge(coef_ready, n - 3)
                            row = scores[:, m, :, :].rearrange("p b c -> p (b c)")[:, 0:width]
                            act.activation(prob[:, s % 2, m, 0:width], row, ACT.Exp, bias=negmax[:, s % 2, m:m + 1],
                                           accum_out=rowsum[:, s % 4, m:m + 1]).then_inc(probs_ready[m], 1)

                passes(act, run)
                n, s = QT * G, NSTEP
                keep_turned(n - 2, s - 2)
                keep_turned(n - 1, s - 1)


def diff_finish(nc, x, d, cst, ctx):
    ident = cst["ident"]
    G = BATCH * HEADS
    with stage(nc, "dz") as st:
        sq = st.sb("sq", [P, QT, G, DF_V])
        ms = st.sb("ms", [P, QT, G])
        srow = st.sb("srow", [P, DF_V])
        wo = st.sb("wo", [P, 2, D])
        oT = st.sb("oT", [P, 2, 2, P])
        banks = st.ps("banks", [P, 4, 512])
        loaded, squared, summed, meaned, rooted, inverted, s_ready, scaled, weighted = (st.sem(n) for n in (
            "loaded", "squared", "summed", "meaned", "rooted", "inverted", "s_ready", "scaled", "weighted"))
        turned, kept, projected, added = (st.sem(n) for n in ("turned", "kept", "projected", "added"))
        with nc.Block() as block:

            @block.sync
            def _(sp):
                sp.dma_start(wo[:], d["L1_attn_a_Wo"].rearrange("(c p) n -> p c n", p=P)).then_inc(loaded, 16)
                sp.dma_start(srow[:], row_of(d["L1_attn_a_rms_scale"], P)).then_inc(loaded, 16)

            @block.scalar
            def _(act):
                act.activation(sq[:], ctx[:], ACT.Square).then_inc(squared, 1)
                act.wait_ge(meaned, 1)
                act.activation(ms[:], ms[:], ACT.Sqrt).then_inc(rooted, 1)
                for t in range(NT):
                    act.wait_ge(turned, t + 1)
                    if t >= 2:
                        act.wait_ge(projected, t - 1)
                    act.activation(oT[:, t % 2, :, :], banks[:, t % 2, 0:2 * P].rearrange("p (c n) -> p c n", c=2),
                                   ACT.Copy).then_inc(kept, 1)

            @block.vector
            def _(dve):
                dve.wait_ge(loaded, 32)
                dve.tensor_scalar(srow[:], srow[:], 1.0 - LAMBDA_INIT, None, ALU.mult).then_inc(s_ready, 1)
                dve.wait_ge(squared, 1)
                dve.tensor_reduce(ms[:], sq[:], AX.X, ALU.add).then_inc(summed, 1)
                dve.wait_ge(summed, 1)
                dve.tensor_scalar(ms[:], ms[:], 1.0 / DF_V, 1e-5, ALU.mult, ALU.add).then_inc(meaned, 1)
                dve.wait_ge(rooted, 1)
                dve.reciprocal(ms[:], ms[:]).then_inc(inverted, 1)
                dve.wait_ge(inverted, 1)
                dve.wait_ge(s_ready, 1)
                for qt in range(QT):
                    rb = ms[:, qt, :].rearrange("p (g o) -> p g o", o=1).to_broadcast([P, G, DF_V])
                    dve.tensor_tensor(ctx[:, qt], ctx[:, qt], rb, ALU.mult).then_inc(scaled, 1)
                for qt in range(QT):
                    sb_ = srow[:].rearrange("p (o e) -> p o e", o=1).to_broadcast([P, G, DF_V])
                    dve.wait_ge(scaled, qt + 1)
                    dve.tensor_tensor(ctx[:, qt], ctx[:, qt], sb_, ALU.mult).then_inc(weighted, 1)
                for t in range(NT):
                    dve.wait_ge(projected, t + 1)
                    dve.tensor_tensor(x[:, t, :], x[:, t, :], banks[:, 2 + t % 2, 0:D], ALU.add).then_inc(added, 1)

            @block.tensor
            def _(pe):
                pe.wait_ge(weighted, QT)
                pe.wait_ge(loaded, 32)
                for t in range(NT):
                    b, qt = t // QT, t % QT
                    if t >= 2:
                        pe.wait_ge(kept, t - 1)
                    src = ctx[:, qt, b * HEADS:(b + 1) * HEADS, :].rearrange("p g e -> p (g e)")
                    for c in range(2):
                        mm = pe.transpose(banks[:, t % 2, c * P:(c + 1) * P], src[:, c * P:(c + 1) * P], ident[:])
                    mm.then_inc(turned, 1)
                    pe.wait_ge(kept, t + 1)
                    if t >= 2:
                        pe.wait_ge(added, t - 1)
                    for c in range(2):
                        mm = pe.matmul(banks[:, 2 + t % 2, 0:D], oT[:, t % 2, c, :], wo[:, c, :], start=c == 0, stop=c == 1)
                    mm.then_inc(projected, 1)


SW_HID = 384
SW_CUT = SW_HID // P
DEQUANT = 1.0 / 127.0


def swiglu(nc, x, d, cst, tag):
    ident = cst["ident"]
    with stage(nc, tag) as st:
        xn = st.sb("xn", [P, NT, D])
        xT = st.sb("xT", [D, TOK])
        wi = st.sb("wi", [P, 3, SW_HID], I32)
        w = st.sb("w", [P, 3, SW_HID])
        act_g = st.sb("act_g", [P, 2, SW_CUT, 512])
        hid = st.sb("hid", [P, 2, SW_CUT, 512])
        banks = st.ps("banks", [P, 8, 512])
        layer_norm(nc, st, x, xn, 1e-5)
        transpose_all(nc, st, xn, xT, ident, banks[:, 0:2, :])
        loaded, w_ready = st.sem("loaded"), st.sem("w_ready")
        u_done, g_done, silu_done, hid_done = (st.sem(n) for n in ("u_done", "g_done", "silu_done", "hid_done"))
        down_done, added = st.sem("down_done"), st.sem("added")
        with nc.Block() as block:

            @block.sync
            def _(sp):
                sp.dma_start(wi[:, 0, :], d["w_gateT"]).then_inc(loaded, 16)
                sp.dma_start(wi[:, 1, :], d["w_upT"]).then_inc(loaded, 16)
                sp.dma_start(wi[:, 2, :].rearrange("p (c n) -> p c n", n=D),
                             d["w_downT"].rearrange("(c p) n -> p c n", p=P)).then_inc(loaded, 16)

            @block.tensor
            def _(pe):
                def down(c):
                    pe.wait_ge(hid_done, SW_CUT * (c + 1))
                    for i in range(4):
                        for j in range(SW_CUT):
                            mm = pe.matmul(banks[:, 6 + c % 2, i * P:(i + 1) * P], hid[:, c % 2, j, i * P:(i + 1) * P],
                                           w[:, 2, j * D:(j + 1) * D], start=j == 0, stop=j == SW_CUT - 1)
                    mm.then_inc(down_done, 1)

                pe.wait_ge(w_ready, 1)
                for c in range(NCH):
                    for j in range(SW_CUT):
                        rhs = xT[:, c * 512:(c + 1) * 512]
                        if c >= 1:
                            pe.wait_ge(silu_done, SW_CUT * (c - 1) + j + 1)
                        pe.matmul(banks[:, j, :], w[:, 0, j * P:(j + 1) * P], rhs, start=True, stop=True).then_inc(g_done, 1)
                        if c >= 1:
                            pe.wait_ge(hid_done, SW_CUT * (c - 1) + j + 1)
                        pe.matmul(banks[:, 3 + j, :], w[:, 1, j * P:(j + 1) * P], rhs, start=True, stop=True).then_inc(u_done, 1)
                    if c >= 1:
                        if c >= 3:
                            pe.wait_ge(added, c - 2)
                        down(c - 1)
                pe.wait_ge(added, NCH - 2)
                down(NCH - 1)

            @block.scalar
            def _(act):
                for k in range(NCH * SW_CUT):
                    c, j = k // SW_CUT, k % SW_CUT
                    act.wait_ge(g_done, k + 1)
                    if c >= 2:
                        act.wait_ge(hid_done, k - 2 * SW_CUT + 1)
                    act.activation(act_g[:, c % 2, j, :], banks[:, j, :], ACT.Silu).then_inc(silu_done, 1)

            @block.vector
            def _(dve):
                dve.wait_ge(loaded, 48)
                dve.tensor_scalar(w[:], wi[:], DEQUANT, None, ALU.mult).then_inc(w_ready, 1)

                def add(c):
                    dve.wait_ge(down_done, c + 1)
                    y = banks[:, 6 + c % 2, :].rearrange("p (t n) -> p t n", t=4)
                    dve.tensor_tensor(x[:, 4 * c:4 * c + 4, :], x[:, 4 * c:4 * c + 4, :], y, ALU.add).then_inc(added, 1)

                for k in range(NCH * SW_CUT):
                    c, j = k // SW_CUT, k % SW_CUT
                    dve.wait_ge(u_done, k + 1)
                    dve.wait_ge(silu_done, k + 1)
                    if c >= 2:
                        dve.wait_ge(down_done, c - 1)
                    dve.tensor_tensor(hid[:, c % 2, j, :], banks[:, 3 + j, :], act_g[:, c % 2, j, :], ALU.mult).then_inc(hid_done, 1)
                    if j == SW_CUT - 1 and c >= 1:
                        add(c - 1)
                add(NCH - 1)


LN_DEPTH = 6


def linear(nc, x, d, cst):
    with stage(nc, "li") as st:
        y = st.sb("y", [P, NT, D])
        layer_norm(nc, st, x, y, 1e-5)
        with nc.Fori(0, LN_DEPTH) as layer:
            linear_layer(nc, y, d, cst, layer)
        added = st.sem("added")
        with nc.Block() as block:

            @block.vector
            def _(dve):
                dve.tensor_tensor(x[:], x[:], y[:], ALU.add).then_inc(added, 1)


def linear_layer(nc, y, d, cst, layer):
    ident = cst["ident"]
    with stage(nc, "ll") as st:
        h = st.sb("h", [P, NT, D])
        hT = st.sb("hT", [D, TOK])
        w = st.sb("w", [D, 3 * D])
        wo = st.sb("wo", [D, D])
        bo = st.sb("bo", [P, D])
        affine = st.sb("affine", [D, 2])
        qe = st.sb("qe", [D, 2, SEQ])
        q = st.sb("q", [P, 2, QT, D])
        k = st.sb("k", [P, 2, QT, D])
        vT = st.sb("vT", [D, 2, SEQ])
        qmax, qsum, qinv = st.sb("qmax", [D, 2]), st.sb("qsum", [D, 2]), st.sb("qinv", [D, 2])
        kmax, ksum = st.sb("kmax", [P, 2, QT]), st.sb("ksum", [P, 2, QT])
        mT, mw = st.sb("mT", [D, 2, D]), st.sb("mw", [D, 2, D])
        banks = st.ps("banks", [P, 8, 512])
        layer_norm(nc, st, y, h, 1e-5)
        loaded, biased = st.sem("loaded"), st.sem("biased")
        turned, hT_ready = st.sem("turned"), st.sem("hT_ready")
        q_done, q_max, q_exp, q_turned, q_kept, q_inv = (st.sem(n) for n in ("q_done", "q_max", "q_exp", "q_turned", "q_kept", "q_inv"))
        k_done, k_max, k_less, k_exp, k_sum, k_inv, k_ready = (st.sem(n) for n in (
            "k_done", "k_max", "k_less", "k_exp", "k_sum", "k_inv", "k_ready"))
        v_done, v_kept = st.sem("v_done"), st.sem("v_kept")
        m_done, m_kept, mw_done, mw_kept, out_done, added = (st.sem(n) for n in (
            "m_done", "m_kept", "mw_done", "mw_kept", "out_done", "added"))
        two = lambda ap: ap.rearrange("p b c -> p (b c)")
        with nc.Block() as block:

            @block.sync
            def _(sp):
                sp.dma_start(w[:], d["L1_attn_b_w_qkv"][layer]).then_inc(loaded, 16)
                sp.dma_start(wo[:], d["L1_attn_b_w_out"][layer]).then_inc(loaded, 16)
                sp.dma_start(bo[:], d["L1_attn_b_b_out"][bass.ts(layer, 1), :].to_broadcast([P, D])).then_inc(loaded, 16)
                sp.dma_start(affine[:, 0:1], d["L1_attn_b_gamma"][layer].rearrange("(p o) -> p o", o=1)).then_inc(loaded, 16)
                sp.dma_start(affine[:, 1:2], d["L1_attn_b_beta"][layer].rearrange("(p o) -> p o", o=1)).then_inc(loaded, 16)

            @block.tensor
            def _(pe):
                for c in range(NCH):
                    if c >= 2:
                        pe.wait_ge(hT_ready, c - 1)
                    for j in range(4):
                        mm = pe.transpose(banks[:, 6 + c % 2, j * P:(j + 1) * P], h[:, 4 * c + j, :], ident[:])
                    mm.then_inc(turned, 1)
                pe.wait_ge(loaded, 80)

                def project(b):
                    for c in range(2):
                        cs = slice(b * SEQ + c * 512, b * SEQ + (c + 1) * 512)
                        mm = pe.matmul(banks[:, c, :], w[:, 0:D], hT[:, cs], start=True, stop=True)
                    mm.then_inc(q_done, 1)
                    if b >= 1:
                        pe.wait_ge(k_less, 1)
                    for t in range(QT):
                        tok = b * SEQ + t * P
                        mm = pe.matmul(banks[:, 2 + t // 4, t % 4 * P:(t % 4 + 1) * P], hT[:, tok:tok + P], w[:, D:2 * D],
                                       start=True, stop=True)
                    mm.then_inc(k_done, 1)
                    if b >= 1:
                        pe.wait_ge(v_kept, 1)
                    for c in range(2):
                        cs = slice(b * SEQ + c * 512, b * SEQ + (c + 1) * 512)
                        mm = pe.matmul(banks[:, 4 + c, :], w[:, 2 * D:], hT[:, cs], start=True, stop=True)
                    mm.then_inc(v_done, 1)

                def turn_q(b):
                    pe.wait_ge(q_exp, b + 1)
                    if b >= 1:
                        pe.wait_ge(q_kept, 1)
                    for t in range(QT):
                        mm = pe.transpose(banks[:, 6 + t // 4, t % 4 * P:(t % 4 + 1) * P], qe[:, b, t * P:(t + 1) * P], ident[:])
                    mm.then_inc(q_turned, 1)

                def mix(b):
                    pe.wait_ge(q_kept, b + 1)
                    pe.wait_ge(k_ready, b + 1)
                    for t in range(QT):
                        mm = pe.matmul(banks[:, 4, 0:D], q[:, b, t, :], k[:, b, t, :], start=t == 0, stop=t == QT - 1)
                    mm.then_inc(m_done, 1)
                    pe.wait_ge(m_kept, b + 1)
                    pe.matmul(banks[:, 5, 0:D], mT[:, b, :], wo[:], start=True, stop=True).then_inc(mw_done, 1)
                    pe.wait_ge(mw_kept, b + 1)
                    for t in range(QT):
                        mm = pe.matmul(banks[:, 2 * b + t // 4, t % 4 * P:(t % 4 + 1) * P], vT[:, b, t * P:(t + 1) * P],
                                       mw[:, b, :], start=True, stop=True)
                    mm.then_inc(out_done, 1)

                pe.wait_ge(hT_ready, 4)
                project(0)
                turn_q(0)
                project(1)
                turn_q(1)
                pe.wait_ge(v_kept, 2)
                pe.wait_ge(k_less, 2)
                mix(0)
                mix(1)

            @block.scalar
            def _(act):
                for b in range(BATCH):
                    act.wait_ge(q_max, b + 1)
                    act.activation(qe[:, b, :], two(banks[:, 0:2, :]), ACT.Exp, bias=qmax[:, b:b + 1],
                                   accum_out=qsum[:, b:b + 1]).then_inc(q_exp, 1)
                    act.wait_ge(k_less, b + 1)
                    act.activation(k[:, b], k[:, b], ACT.Exp).then_inc(k_exp, 1)
                    act.wait_ge(v_done, b + 1)
                    act.activation(vT[:, b, :], two(banks[:, 4:6, :]), ACT.Copy).then_inc(v_kept, 1)
                    act.wait_ge(q_turned, b + 1)
                    act.activation(q[:, b].rearrange("p t n -> p (t n)"), two(banks[:, 6:8, :]), ACT.Copy).then_inc(q_kept, 1)
                for b in range(BATCH):
                    act.wait_ge(mw_done, b + 1)
                    act.activation(mw[:, b, :], banks[:, 5, 0:D], ACT.Copy).then_inc(mw_kept, 1)

            @block.vector
            def _(dve):
                dve.wait_ge(loaded, 80)
                for c in range(NCH):
                    dve.wait_ge(turned, c + 1)
                    dve.tensor_scalar(hT[:, c * 512:(c + 1) * 512], banks[:, 6 + c % 2, :], affine[:, 0:1], affine[:, 1:2],
                                      ALU.mult, ALU.add).then_inc(hT_ready, 1)
                bv = bo[:].rearrange("p (o n) -> p o n", o=1).to_broadcast([P, NT, D])
                dve.tensor_tensor(y[:], y[:], bv, ALU.add).then_inc(biased, 1)
                for b in range(BATCH):
                    dve.wait_ge(q_done, b + 1)
                    dve.tensor_reduce(qmax[:, b:b + 1], two(banks[:, 0:2, :]), AX.X, ALU.max, negate=True).then_inc(q_max, 1)
                    dve.wait_ge(k_done, b + 1)
                    kp = two(banks[:, 2:4, :]).rearrange("p (t n) -> p t n", n=D)
                    dve.tensor_reduce(kmax[:, b, :], kp, AX.X, ALU.max).then_inc(k_max, 1)
                    dve.wait_ge(k_max, b + 1)
                    kb = kmax[:, b, :].rearrange("p (t o) -> p t o", o=1).to_broadcast([P, QT, D])
                    dve.tensor_tensor(k[:, b], kp, kb, ALU.subtract).then_inc(k_less, 1)
                    dve.wait_ge(q_exp, b + 1)
                    dve.reciprocal(qinv[:, b:b + 1], qsum[:, b:b + 1]).then_inc(q_inv, 1)
                for b in range(BATCH):
                    dve.wait_ge(k_exp, b + 1)
                    dve.tensor_reduce(ksum[:, b, :], k[:, b], AX.X, ALU.add).then_inc(k_sum, 1)
                    dve.wait_ge(k_sum, b + 1)
                    dve.reciprocal(ksum[:, b, :], ksum[:, b, :]).then_inc(k_inv, 1)
                    dve.wait_ge(k_inv, b + 1)
                    kb = ksum[:, b, :].rearrange("p (t o) -> p t o", o=1).to_broadcast([P, QT, D])
                    dve.tensor_tensor(k[:, b], k[:, b], kb, ALU.mult).then_inc(k_ready, 1)
                for b in range(BATCH):
                    dve.wait_ge(m_done, b + 1)
                    dve.wait_ge(q_inv, b + 1)
                    dve.tensor_scalar(mT[:, b, :], banks[:, 4, 0:D], qinv[:, b:b + 1], None, ALU.mult).then_inc(m_kept, 1)
                    dve.wait_ge(out_done, b + 1)
                    dve.wait_ge(biased, 1)
                    out = two(banks[:, 2 * b:2 * b + 2, :]).rearrange("p (t n) -> p t n", n=D)
                    ys = y[:, b * QT:(b + 1) * QT, :]
                    dve.tensor_tensor(ys, ys, out, ALU.add).then_inc(added, 1)


STAGES = ("attn_a", "ffn0", "attn_b", "ffn1", "diff", "swiglu0", "linear", "swiglu1")


def build_program(nc, d, stages=STAGES):
    with ExitStack() as stack:
        x = stack.enter_context(nc.sbuf_tensor("residual", [P, NT, D], F32))
        ident = stack.enter_context(nc.sbuf_tensor("ident_s", [P, P], F32))
        shift = stack.enter_context(nc.sbuf_tensor("shift_s", [P, 2, P], F32))
        loaded = stack.enter_context(nc.semaphore("stream_loaded"))
        out_stored = stack.enter_context(nc.semaphore("out_stored"))
        cst = {"ident": ident, "shift": shift, "mask_c": d["mask_c"], "mask_p": d["mask_p"]}
        with nc.Block() as block:

            @block.sync
            def _(sp):
                for b in range(BATCH):
                    src = d["x_in"][b * SEQ:(b + 1) * SEQ, :].rearrange("(t p) c -> p t c", p=P)
                    sp.dma_start(x[:, b * QT:(b + 1) * QT, :], src).then_inc(loaded, 16)
                sp.dma_start(ident[:], d["ident"]).then_inc(loaded, 16)
                sp.dma_start(shift[:], d["shift"]).then_inc(loaded, 16)
                sp.wait_ge(loaded, 64)
        for s in stages:
            if s == "attn_a":
                attn_a(nc, x, d, cst)
            if s in ("ffn0", "ffn1"):
                ffn(nc, x, d, cst, s)
            if s == "attn_b":
                attn_b(nc, x, d, cst)
            if s == "diff":
                diff(nc, x, d, cst)
            if s in ("swiglu0", "swiglu1"):
                swiglu(nc, x, d, cst, s)
            if s == "linear":
                linear(nc, x, d, cst)
        with nc.Block() as block:

            @block.sync
            def _(sp):
                sp.dma_start(d["out"].rearrange("(t p) c -> p t c", p=P), x[:]).then_inc(out_stored, 16)
                sp.wait_ge(out_stored, 16)


def layout(inputs):
    a = {k: np.ascontiguousarray(v) for k, v in inputs.items()}
    a["x_in"] = a.pop("L0_attn_a_hidden_states").reshape(TOK, D)
    a["relT"] = np.ascontiguousarray(a.pop("L0_attn_a_rel_embeddings").T)
    a["ident"] = np.eye(P, dtype=np.float32)
    a.update(attn_a_constants())
    a.update(ffn_constants())
    a["causal"] = np.where(np.arange(P)[None, :] <= np.arange(P)[:, None], 0.0, NEG).astype(np.float32)
    for name in ("gate", "up", "down"):
        a[f"w_{name}T"] = np.ascontiguousarray(a.pop(f"L1_ffn_w_{name}").T)
    return a


def kernel(**inputs):
    import concourse.bacc as _bacc
    from concourse.bass_utils import run_bass_kernel_spmd as _run

    nc = _bacc.Bacc("TRN2", target_bir_lowering=False, num_devices=1)
    arrays, d = {}, {}
    for name, a in layout({k: np.asarray(v) for k, v in inputs.items()}).items():
        if name == "L0_attn_a_attention_mask":
            continue
        arrays[f"in_{name}"] = a
        d[name] = nc.dram_tensor(f"in_{name}", a.shape, mybir.dt.from_np(a.dtype), kind="ExternalInput").ap()
    d["out"] = nc.dram_tensor("out_0", (TOK, D), F32, kind="ExternalOutput").ap()
    build_program(nc, d)
    r = _run(nc, [arrays], core_ids=[0])
    return r.results[0]["out_0"].reshape(BATCH, SEQ, D)
```

```python
import math
from contextlib import ExitStack, contextmanager

import numpy as np

import concourse.bass as bass
from concourse import mybir

F32 = mybir.dt.float32
BF16 = mybir.dt.bfloat16
I32 = mybir.dt.int32
ALU = mybir.AluOpType
ACT = mybir.ActivationFunctionType
AX = mybir.AxisListType

P = 128
D = 128
TOK = 2048
NT = TOK // P
NCH = TOK // 512


class Stage:

    def __init__(self, nc, tag):
        self.nc, self.tag, self.stack, self.sems = nc, tag, ExitStack(), []

    def sb(self, name, shape, dt=F32):
        return self.stack.enter_context(self.nc.sbuf_tensor(f"{self.tag}_{name}", shape, dt))

    def ps(self, name, shape, dt=F32):
        return self.stack.enter_context(self.nc.psum_tensor(f"{self.tag}_{name}", shape, dt))

    def sem(self, name):
        s = self.nc.alloc_semaphore(name=f"{self.tag}_{name}")
        self.sems.append(s)
        return s

    def dram(self, name, shape, dt=F32):
        return self.nc.dram_tensor(f"{self.tag}_{name}", shape, dt).ap()


@contextmanager
def stage(nc, tag):
    st = Stage(nc, tag)
    yield st
    nc.clear_and_free_semaphores(st.sems)
    nc.all_engine_barrier()
    st.stack.close()


def layer_norm(nc, st, x, out, eps, tag=""):
    stats = st.sb("stats" + tag, [P, NT, 6])
    mean = st.sb("mean" + tag, [P, NT])
    diff = st.sb("diff" + tag, [P, NT])
    ssq = st.sb("ssq" + tag, [P, NT])
    rstd = st.sb("rstd" + tag, [P, NT])
    stats_done = st.sem("stats_done" + tag)
    moments = st.sem("moments" + tag)
    std_ready = st.sem("std_ready" + tag)
    rstd_ready = st.sem("rstd_ready" + tag)
    normed = st.sem("normed" + tag)
    with nc.Block() as block:

        @block.vector
        def _(dve):
            for t in range(NT):
                dve.bn_stats(stats[:, t, :], x[:, t, :]).then_inc(stats_done, 1)
            dve.wait_ge(stats_done, NT)
            dve.tensor_tensor(mean[:], stats[:, :, 1], stats[:, :, 4], ALU.add).then_inc(moments, 1)
            dve.tensor_tensor(diff[:], stats[:, :, 1], stats[:, :, 4], ALU.subtract).then_inc(moments, 1)
            dve.tensor_tensor(ssq[:], stats[:, :, 2], stats[:, :, 5], ALU.add).then_inc(moments, 1)
            dve.wait_ge(moments, 3)
            dve.tensor_scalar(mean[:], mean[:], 0.5, None, ALU.mult).then_inc(moments, 1)
            dve.tensor_tensor(diff[:], diff[:], diff[:], ALU.mult).then_inc(moments, 1)
            dve.tensor_scalar(ssq[:], ssq[:], 1.0 / D, eps, ALU.mult, ALU.add).then_inc(moments, 1)
            dve.wait_ge(moments, 6)
            dve.scalar_tensor_tensor(ssq[:], diff[:], 0.25, ssq[:], ALU.mult, ALU.add).then_inc(moments, 1)
            dve.wait_ge(std_ready, 1)
            dve.reciprocal(rstd[:], ssq[:]).then_inc(rstd_ready, 1)
            dve.wait_ge(rstd_ready, 1)
            for t in range(NT):
                dve.tensor_scalar(out[:, t, :], x[:, t, :], mean[:, t:t + 1], rstd[:, t:t + 1],
                                  ALU.subtract, ALU.mult).then_inc(normed, 1)

        @block.scalar
        def _(act):
            act.wait_ge(moments, 7)
            act.activation(ssq[:], ssq[:], ACT.Sqrt).then_inc(std_ready, 1)


def transpose_all(nc, st, x, xT, ident, pt, tag=""):
    turned = st.sem("turned" + tag)
    kept = st.sem("kept" + tag)
    with nc.Block() as block:

        @block.tensor
        def _(pe):
            for c in range(NCH):
                if c >= 2:
                    pe.wait_ge(kept, c - 1)
                for j in range(4):
                    mm = pe.transpose(pt[:, c % 2, j * P:(j + 1) * P], x[:, 4 * c + j, :], ident[:])
                mm.then_inc(turned, 1)

        @block.vector
        def _(dve):
            for c in range(NCH):
                dve.wait_ge(turned, c + 1)
                dve.tensor_copy(xT[:, c * 512:(c + 1) * 512], pt[:, c % 2, :]).then_inc(kept, 1)


HEADS = 16
HD = D // HEADS
SEQ = 1024
BATCH = TOK // SEQ
QT = SEQ // P
BUCKETS = 32
NPOS = 2 * BUCKETS
Q_PARTS = (0, 0, 0, 1, 1, 2)
K_PARTS = (0, 1, 2, 0, 1, 0)
STACK = len(Q_PARTS) * HD
FARROWS = 9
KROWS = STACK + FARROWS


def log_bucket(r, bucket=BUCKETS, longest=64):
    mid = bucket // 2
    a = mid - 1 if abs(r) < mid else abs(r)
    if a <= mid:
        return a
    return int((math.ceil(math.log(a / mid) / math.log((longest - 1) / mid) * (mid - 1)) + mid) * (1 if r > 0 else -1))


def attn_a_constants():
    sel_c = np.zeros((NPOS, P + 3), np.float32)
    sel_p = np.zeros((NPOS, P + 3), np.float32)
    for j in range(P):
        f = log_bucket(64 - j)
        sel_c[min(max(f + BUCKETS, 0), NPOS - 1), j] += 1
        sel_p[min(max(BUCKETS - f, 0), NPOS - 1), j] += 1
    for s in (sel_c, sel_p):
        s[0, 0:P] -= 1
        s[NPOS - 1, P] -= 1
        s[0, P] += 1
        s[NPOS - 1, P + 1] = 1
        s[0, P + 2] = 1
    row, j = np.arange(P)[:, None] % 64, np.arange(P)[None, :]
    mask_c = (64 - j > row).astype(np.float32)
    mask_p = (row + j - 64 >= 64).astype(np.float32)
    heads = (np.arange(D)[:, None] // HD == np.arange(HEADS)[None, :]).astype(np.float32)
    return {"sel_c": sel_c, "sel_p": sel_p, "mask_c": mask_c, "mask_p": mask_p, "head_of": heads,
            "gather8": np.tile(np.eye(32, HD, dtype=np.float32), (4, 1)),
            "gather16": np.tile(np.eye(32, 2 * HD, dtype=np.float32), (4, 1))}


def attn_a(nc, x, d, cst):
    G = BATCH * HEADS
    inv_scale = 1.0 / math.sqrt(3 * HD)
    with stage(nc, "aa") as st:
        xn = st.sb("xn", [P, NT, D])
        ctx = st.sb("ctx", [P, QT, G, HD])
        vh = st.sb("vh", [P, QT, G, HD])
        ident = cst["ident"]
        qh = st.dram("qh", (G, KROWS, SEQ), BF16)
        kh = st.dram("kh", (2, G, KROWS, SEQ), BF16)
        tab = st.dram("tab", (G, STACK, 2 * (P + 1)), BF16)
        SKEW = P * (2 * P + 1)
        win = st.dram("win", (2, 2, QT, SKEW))
        attn_a_prepare(nc, x, d, cst, xn, vh, qh, kh, tab, win, inv_scale)
        attn_a_heads(nc, cst, ctx, vh, qh, kh, tab, win)
        attn_a_finish(nc, x, d, cst, xn, ctx)


def attn_a_prepare(nc, x, d, cst, xn, vh, qh, kh, tab, win, inv_scale):
    ident = cst["ident"]
    with stage(nc, "ap") as st:
        layer_norm(nc, st, x, xn, 1e-5)
        xT = st.sb("xT", [D, TOK])
        banks = st.ps("banks", [P, 8, 512])
        transpose_all(nc, st, xn, xT, ident, banks[:, 0:2, :])
        w = {n: st.sb(n, [D, D]) for n in ("Wq", "Wk", "Wv")}
        bq, bk = st.sb("bq", [D, 1]), st.sb("bk", [D, 1])
        bkrow, bvrow = st.sb("bkrow", [P, D]), st.sb("bvrow", [P, D])
        relT = st.sb("relT", [D, NPOS])
        sel = st.sb("sel", [NPOS, 2, P + 3])
        head_of = st.sb("head_of", [D, HEADS])
        posk = st.sb("posk", [NPOS, D])
        table = st.sb("table", [D, 2, P + 3])
        far_w = st.sb("far_w", [D, 2, 2, HEADS])
        tparts = st.sb("tparts", [D, 2, 3, P + 1], BF16)
        trest = st.sb("trest", [D, 2, P + 1])
        val = st.sb("val", [D, 2, TOK])
        rest = st.sb("rest", [D, 2, TOK])
        parts = st.sb("parts", [D, 2, 3, TOK], BF16)
        far = st.sb("far", [2 * HEADS, 2, TOK])
        far_rest = st.sb("far_rest", [2 * HEADS, 2, TOK])
        far_parts = st.sb("far_parts", [2 * HEADS, 2, 3, TOK], BF16)
        ones = st.sb("ones", [HEADS, 3, SEQ], BF16)
        zeros = st.sb("zeros", [HEADS, 3, SEQ], BF16)
        zwin = st.sb("zwin", [P, 2056])
        loaded = st.sem("loaded")
        filled = st.sem("filled")
        step = st.sem("step")
        mm_done = st.sem("mm_done")
        evac = st.sem("evac")
        copied = st.sem("copied")
        posk_ready = st.sem("posk_ready")
        table_mm, table_ready = st.sem("table_mm"), st.sem("table_ready")
        farw_ready = st.sem("farw_ready")
        far_mm, far_ready = st.sem("far_mm"), st.sem("far_ready")
        v_mm, v_ready = st.sem("v_mm"), st.sem("v_ready")
        t_done = st.sem("t_done")
        split_done, high_done, mid_done = st.sem("split_done"), st.sem("high_done"), st.sem("mid_done")
        fsplit, fhigh, fmid = st.sem("fsplit"), st.sem("fhigh"), st.sem("fmid")
        stored = st.sem("stored")
        with nc.Block() as block:

            @block.sync
            def _(sp):
                n = 0
                for name in ("Wq", "Wk", "Wv"):
                    sp.dma_start(w[name][:], d["L0_attn_a_" + name]).then_inc(loaded, 16)
                sp.dma_start(bq[:], d["L0_attn_a_bq"].rearrange("(p o) -> p o", o=1)).then_inc(loaded, 16)
                sp.dma_start(bk[:], d["L0_attn_a_bk"].rearrange("(p o) -> p o", o=1)).then_inc(loaded, 16)
                sp.dma_start(bkrow[:], d["L0_attn_a_bk"].rearrange("(o n) -> o n", o=1).to_broadcast([P, D])).then_inc(loaded, 16)
                sp.dma_start(bvrow[:], d["L0_attn_a_bv"].rearrange("(o n) -> o n", o=1).to_broadcast([P, D])).then_inc(loaded, 16)
                sp.dma_start(relT[:], d["relT"]).then_inc(loaded, 16)
                sp.dma_start(sel[:, 0, :], d["sel_c"]).then_inc(loaded, 16)
                sp.dma_start(sel[:, 1, :], d["sel_p"]).then_inc(loaded, 16)
                sp.dma_start(head_of[:], d["head_of"]).then_inc(loaded, 16)
                sp.wait_ge(filled, 3)
                for slot in range(2):
                    for side in range(2):
                        flat = win[slot, side].rearrange("t (p c) -> p t c", p=P)
                        sp.dma_start(flat, zwin[:, 0:QT * 257].rearrange("p (t c) -> p t c", t=QT)).then_inc(stored, 16)
                        n += 1
                for b in range(BATCH):
                    gs, ts = slice(b * HEADS, (b + 1) * HEADS), slice(b * SEQ, (b + 1) * SEQ)
                    sp.dma_start(qh[gs, STACK + 6:STACK + 9, :], ones[:]).then_inc(stored, 16)
                    sp.dma_start(kh[0, gs, STACK:STACK + 3, :], ones[:]).then_inc(stored, 16)
                    sp.dma_start(kh[0, gs, STACK + 3:STACK + 6, :], zeros[:]).then_inc(stored, 16)
                    sp.dma_start(kh[1, gs, STACK:STACK + 3, :], zeros[:]).then_inc(stored, 16)
                    sp.dma_start(kh[1, gs, STACK + 3:STACK + 6, :], ones[:]).then_inc(stored, 16)
                    n += 5
                sp.wait_ge(t_done, 4)
                for side, order in ((0, K_PARTS), (1, Q_PARTS)):
                    for r, part in enumerate(order):
                        for b in range(BATCH):
                            dst = tab[b * HEADS:(b + 1) * HEADS, r * HD:(r + 1) * HD, side * (P + 1):(side + 1) * (P + 1)]
                            sp.dma_start(dst, tparts[:, side, part, :]).then_inc(stored, 16)
                            n += 1
                sp.wait_ge(split_done, 2)
                for b in range(BATCH):
                    gs, ts = slice(b * HEADS, (b + 1) * HEADS), slice(b * SEQ, (b + 1) * SEQ)
                    for r in range(len(Q_PARTS)):
                        rows = slice(r * HD, (r + 1) * HD)
                        sp.dma_start(qh[gs, rows, :], parts[:, 0, Q_PARTS[r], ts]).then_inc(stored, 16)
                        sp.dma_start(kh[0, gs, rows, :], parts[:, 1, K_PARTS[r], ts]).then_inc(stored, 16)
                        sp.dma_start(kh[1, gs, rows, :], parts[:, 1, K_PARTS[r], ts]).then_inc(stored, 16)
                        n += 3
                sp.wait_ge(fsplit, 1)
                for b in range(BATCH):
                    gs, ts = slice(b * HEADS, (b + 1) * HEADS), slice(b * SEQ, (b + 1) * SEQ)
                    for sign in range(2):
                        sp.dma_start(qh[gs, STACK + 3 * sign:STACK + 3 * sign + 3, :], far_parts[sign * HEADS:(sign + 1) * HEADS, 0, :, ts]).then_inc(stored, 16)
                        sp.dma_start(kh[sign, gs, STACK + 6:STACK + 9, :], far_parts[sign * HEADS:(sign + 1) * HEADS, 1, :, ts]).then_inc(stored, 16)
                        n += 2
                sp.wait_ge(stored, 16 * n)

            @block.gpsimd
            def _(pool):
                pool.memset(zwin[:], 0.0).then_inc(filled, 1)
                pool.memset(ones[:], 1.0).then_inc(filled, 1)
                pool.memset(zeros[:], 0.0).then_inc(filled, 1)

            @block.tensor
            def _(pe):
                pe.wait_ge(loaded, 16 * 11)
                pe.matmul(banks[0:NPOS, 0, 0:D], relT[:], w["Wk"][:], start=True, stop=True).then_inc(mm_done, 1)
                pe.wait_ge(posk_ready, 1)
                for side in range(2):
                    mm = pe.matmul(banks[:, 1 + side, 0:P + 3], posk[:], sel[:, side, :], start=True, stop=True)
                mm.then_inc(table_mm, 1)
                for c in range(NCH):
                    for i, name in enumerate(("Wq", "Wk")):
                        if c >= 1:
                            pe.wait_ge(evac, 2 * (c - 1) + i + 1)
                        pe.matmul(banks[:, 3 + i, :], w[name][:], xT[:, c * 512:(c + 1) * 512], start=True,
                                  stop=True).then_inc(copied, 1)
                for c in range(NCH):
                    if c >= 1:
                        pe.wait_ge(v_ready, c)
                    for j in range(4):
                        t = 4 * c + j
                        mm = pe.matmul(banks[:, 5, j * P:(j + 1) * P], xT[:, t * P:(t + 1) * P], w["Wv"][:],
                                       start=True, stop=True)
                    mm.then_inc(v_mm, 1)
                pe.wait_ge(farw_ready, 4)
                for c in range(NCH):
                    pe.wait_ge(evac, 2 * c + 2)
                    for i in range(2):
                        if c >= 1:
                            pe.wait_ge(far_ready, 2 * (c - 1) + i + 1)
                        pe.matmul(banks[0:2 * HEADS, 6 + i, :], far_w[:, i, :, :].rearrange("p s h -> p (s h)"),
                                  val[:, i, c * 512:(c + 1) * 512], start=True, stop=True).then_inc(far_mm, 1)

            @block.vector
            def _(dve):
                dve.wait_ge(mm_done, 1)
                dve.tensor_tensor(posk[:], banks[0:NPOS, 0, 0:D], bkrow[0:NPOS, :], ALU.add).then_inc(posk_ready, 1)
                dve.wait_ge(table_mm, 1)
                dve.tensor_copy(table[:, 0, :], banks[:, 1, 0:P + 3]).then_inc(table_ready, 1)
                dve.tensor_scalar(table[:, 1, :], banks[:, 2, 0:P + 3], inv_scale, None, ALU.mult).then_inc(table_ready, 1)
                dve.wait_ge(table_ready, 2)
                for i in range(4):
                    dve.tensor_scalar(far_w[:, i // 2, i % 2, :], head_of[:], table[:, i // 2, P + 1 + i % 2:P + 2 + i % 2], None,
                                      ALU.mult).then_inc(farw_ready, 1)
                dve.tensor_copy(tparts[:, :, 0, :], table[:, :, 0:P + 1]).then_inc(t_done, 1)
                dve.wait_ge(t_done, 1)
                dve.tensor_tensor(trest[:], table[:, :, 0:P + 1], tparts[:, :, 0, :], ALU.subtract).then_inc(t_done, 1)
                dve.wait_ge(t_done, 2)
                dve.tensor_copy(tparts[:, :, 1, :], trest[:]).then_inc(t_done, 1)
                dve.wait_ge(t_done, 3)
                dve.tensor_tensor(tparts[:, :, 2, :], trest[:], tparts[:, :, 1, :], ALU.subtract).then_inc(t_done, 1)
                for c in range(NCH):
                    cs = slice(c * 512, (c + 1) * 512)
                    dve.wait_ge(copied, 2 * c + 1)
                    dve.tensor_scalar(val[:, 0, cs], banks[:, 3, :], bq[:, 0:1], inv_scale, ALU.add, ALU.mult).then_inc(evac, 1)
                    dve.wait_ge(copied, 2 * c + 2)
                    dve.tensor_scalar(val[:, 1, cs], banks[:, 4, :], bk[:, 0:1], None, ALU.add).then_inc(evac, 1)
                for i in range(2):
                    dve.wait_ge(high_done, i + 1)
                    dve.tensor_tensor(rest[:, i, :], val[:, i, :], parts[:, i, 0, :], ALU.subtract).then_inc(step, 1)
                for c in range(NCH):
                    dve.wait_ge(v_mm, c + 1)
                    b, k0 = 4 * c // QT, 4 * c % QT
                    dst = vh[:, k0:k0 + 4, b * HEADS:(b + 1) * HEADS, :].rearrange("p t g e -> p t (g e)")
                    src = banks[:, 5, :].rearrange("p (t n) -> p t n", t=4)
                    bv = bvrow[:].rearrange("p (o n) -> p o n", o=1).to_broadcast([P, 4, D])
                    dve.tensor_tensor(dst, src, bv, ALU.add).then_inc(v_ready, 1)
                for i in range(2):
                    dve.wait_ge(mid_done, i + 1)
                    dve.tensor_tensor(parts[:, i, 2, :], rest[:, i, :], parts[:, i, 1, :], ALU.subtract).then_inc(split_done, 1)
                for c in range(NCH):
                    for i in range(2):
                        dve.wait_ge(far_mm, 2 * c + i + 1)
                        dve.tensor_copy(far[:, i, c * 512:(c + 1) * 512], banks[0:2 * HEADS, 6 + i, :]).then_inc(far_ready, 1)
                dve.wait_ge(fhigh, 1)
                dve.tensor_tensor(far_rest[:], far[:], far_parts[:, :, 0, :], ALU.subtract).then_inc(step, 1)
                dve.wait_ge(fmid, 1)
                dve.tensor_tensor(far_parts[:, :, 2, :], far_rest[:], far_parts[:, :, 1, :], ALU.subtract).then_inc(fsplit, 1)

            @block.scalar
            def _(act):
                act.wait_ge(evac, 8)
                for i in range(2):
                    act.activation(parts[:, i, 0, :], val[:, i, :], ACT.Copy).then_inc(high_done, 1)
                for i in range(2):
                    act.wait_ge(step, i + 1)
                    act.activation(parts[:, i, 1, :], rest[:, i, :], ACT.Copy).then_inc(mid_done, 1)
                act.wait_ge(far_ready, 2 * NCH)
                act.activation(far_parts[:, :, 0, :], far[:], ACT.Copy).then_inc(fhigh, 1)
                act.wait_ge(step, 3)
                act.activation(far_parts[:, :, 1, :], far_rest[:], ACT.Copy).then_inc(fmid, 1)


def back(i, s, k, nstep):
    j, r = (i, s - k) if s >= k else (i - 1, s - k + nstep)
    return nstep * i + s - k, r, 2 * j + r // QT


VCOLS = 32


def place_v(pool, v_s, vh, width, v_placed, pv_done, g, par, first):
    if not first:
        pool.wait_ge(pv_done, QT * (g - 1))
    pool.tensor_copy(v_s[:, par, :, 0:width], vh[:, :, g, :]).then_inc(v_placed, 1)


def since(eng, sem, value):
    if not isinstance(value, int) or value > 0:
        eng.wait_ge(sem, value)


def attn_a_heads(nc, cst, ctx, vh, qh, kh, tab, win):
    ident = cst["ident"]
    G = BATCH * HEADS
    NSTEP = 2 * QT
    PAIRS = QT // 2
    with stage(nc, "ah") as st:
        q_s = st.sb("q", [KROWS, 2, SEQ], BF16)
        kp_s = st.sb("kp", [KROWS, 2, SEQ], BF16)
        km_s = st.sb("km", [KROWS, 2, SEQ], BF16)
        tb_s = st.sb("tb", [STACK, 2, 2 * (P + 1)], BF16)
        band = st.sb("band", [P, 2, QT, P])
        cwin = st.sb("cwin", [P, 2, QT, 2 * P])
        pwin = st.sb("pwin", [P, 2, QT, 2 * P])
        prob = st.sb("prob", [P, 2, SEQ])
        probT = st.sb("probT", [P, 2, QT, P])
        v_s = st.sb("v", [P, 2, QT, VCOLS])
        outT = st.sb("outT", [P, 2, P])
        gather = st.sb("gather", [P, HD])
        negmax = st.sb("negmax", [P, 2])
        rowsum = st.sb("rowsum", [P, 2, QT])
        rinv = st.sb("rinv", [P, 2, QT])
        masks = st.sb("masks", [P, 2, P])
        scores = st.ps("scores", [P, 2, 2, 512])
        turned = st.ps("turned", [P, QT, P])
        BW = 2 * (P + 1)
        shared = st.ps("shared", [P, 2, 512])
        outp = shared[:, 0, BW:BW + P]
        ctxp = shared[:, 1, BW:BW + QT * HD].rearrange("p (t e) -> p t e", t=QT)
        mask_loaded = st.sem("mask_loaded")
        ops_loaded = [st.sem(f"ops_loaded{i}") for i in range(2)]
        win_stored = st.sem("win_stored")
        win_loaded = [[st.sem(f"win_loaded{i}_{half}") for half in range(2)] for i in range(2)]
        band_mm, band_kept = st.sem("band_mm"), st.sem("band_kept")
        base_done, window_added = st.sem("base_done"), st.sem("window_added")
        max_ready, probs_ready = st.sem("max_ready"), st.sem("probs_ready")
        probs_turned, kept_a, kept_v = st.sem("probs_turned"), st.sem("kept_a"), st.sem("kept_v")
        v_clear, v_placed = st.sem("v_clear"), st.sem("v_placed")
        pv_done, out_kept, gathered = st.sem("pv_done"), st.sem("out_kept"), st.sem("gathered")
        rinv_ready, ctx_kept = st.sem("rinv_ready"), st.sem("ctx_kept")


        def passes(eng, run):
            run(0, True, False)
            with eng.Fori(1, G // 2 - 1) as i:
                run(i, False, False)
            run(G // 2 - 1, False, True)

        with nc.Block() as block:

            @block.sync
            def _(sp):
                def load_head(g, par):
                    sp.dma_start(q_s[:, par, :], qh[g]).then_inc(ops_loaded[par], 16)
                    sp.dma_start(kp_s[:, par, :], kh[0, g]).then_inc(ops_loaded[par], 16)
                    sp.dma_start(km_s[:, par, :], kh[1, g]).then_inc(ops_loaded[par], 16)
                    sp.dma_start(tb_s[:, par, :], tab[g]).then_inc(ops_loaded[par], 16)

                def window_trip(g, par):
                    for half in range(2):
                        tiles = slice(half * PAIRS, (half + 1) * PAIRS)
                        sp.wait_ge(band_kept, 2 * QT * g + QT * (half + 1))
                        for side in range(2):
                            dst = win[par, side].rearrange("t (p c) -> p t c", p=P)[:, tiles, 0:P]
                            sp.dma_start(dst, band[:, side, tiles, :]).then_inc(win_stored, 16)
                        sp.wait_ge(win_stored, 64 * g + 32 * (half + 1))
                        for side, buf in ((1, pwin), (0, cwin)):
                            src = win[par, side][:, 0:2 * P * P].rearrange("t (p c) -> p t c", p=P)
                            sp.dma_start(buf[:, par, tiles, :], src[:, tiles, :]).then_inc(win_loaded[par][half], 16)

                def run(i, first, last):
                    for par in range(1 if last else 2):
                        g1 = 2 * i + par + 1
                        since(sp, window_added, QT * (g1 - 1))
                        load_head(g1, 1 - par)
                        window_trip(g1, 1 - par)

                sp.dma_start(masks[:, 0, :], cst["mask_c"]).then_inc(mask_loaded, 16)
                sp.dma_start(masks[:, 1, :], cst["mask_p"]).then_inc(mask_loaded, 16)
                sp.dma_start(gather[:], cst["gather8"]).then_inc(mask_loaded, 16)
                load_head(0, 0)
                window_trip(0, 0)
                passes(sp, run)

            @block.tensor
            def _(pe):
                def band_tiles(pair, par):
                    for k in range(2):
                        ts = slice((2 * pair + k) * P, (2 * pair + k + 1) * P)
                        pe.matmul(shared[:, k, 0:P + 1], q_s[0:STACK, par, ts], tb_s[:, par, 0:P + 1], start=True,
                                  stop=True)
                        mm = pe.matmul(shared[:, k, P + 1:BW], kp_s[0:STACK, par, ts], tb_s[:, par, P + 1:BW],
                                       start=True, stop=True)
                    mm.then_inc(band_mm, 1)

                def base(s):
                    par, t = s // QT, s % QT
                    lo = t * P
                    for bank in range(2):
                        b0, b1 = bank * 512, (bank + 1) * 512
                        todo = []
                        if max(lo + 64, b0) < b1:
                            a = max(lo + 64, b0)
                            todo.append((slice(0, P), a, b1, q_s[:, par, lo:lo + P], km_s[:, par, a:b1]))
                        if b0 < min(lo, b1):
                            a = min(lo, b1)
                            todo.append((slice(0, P), b0, a, q_s[:, par, lo:lo + P], kp_s[:, par, b0:a]))
                        if b0 <= lo < b1:
                            todo.append((slice(0, 64), lo, lo + 64, q_s[:, par, lo:lo + 64], km_s[:, par, lo:lo + 64]))
                            todo.append((slice(64, P), lo, lo + 64, q_s[:, par, lo + 64:lo + P],
                                         kp_s[:, par, lo:lo + 64]))
                        for kt, rows, cols in ((t - 1, slice(0, 64), slice(192, 256)), (t, slice(0, P), slice(64, 192)),
                                               (t + 1, slice(64, P), slice(0, 64))):
                            if 0 <= kt < QT and b0 <= kt * P < b1:
                                todo.append((rows, kt * P, kt * P + P, pwin[:, par, kt, cols], ident[:]))
                        for j, (rows, c0, c1, lhs, rhs) in enumerate(todo):
                            mm = pe.matmul(scores[rows, s % 2, bank, c0 - b0:c1 - b0], lhs, rhs, start=j == 0,
                                           stop=j == len(todo) - 1, skip_group_check=True)
                    mm.then_inc(base_done, 1)

                def turn(n, s):
                    pe.wait_ge(probs_ready, n + 1)
                    since(pe, kept_a, n)
                    since(pe, kept_v, n)
                    for kt in range(QT):
                        mm = pe.transpose(turned[:, kt, :], prob[:, s % 2, kt * P:(kt + 1) * P], ident[:])
                    mm.then_inc(probs_turned, 1)

                def times_v(n, s, g):
                    if s % QT == 0:
                        pe.wait_ge(v_placed, g + 1)
                    pe.wait_ge(kept_a, n + 1)
                    pe.wait_ge(kept_v, n + 1)
                    since(pe, out_kept, n)
                    for kt in range(QT):
                        r = kt % 4 * 32
                        mm = pe.matmul(outp[r:r + VCOLS, :], v_s[:, s // QT, kt, :], probT[:, s % 2, kt, :],
                                       start=kt < 4, stop=kt >= 4, tile_position=(0, r), skip_group_check=True)
                    mm.then_inc(pv_done, 1)

                def add_parts(n, s, g):
                    pe.wait_ge(out_kept, n + 1)
                    if s % QT == 0:
                        since(pe, ctx_kept, g)
                    pe.matmul(ctxp[:, s % QT, :], outT[:, s % 2, :], gather[:], start=True,
                              stop=True).then_inc(gathered, 1)

                def run(i, first, last):
                    for s in range(NSTEP):
                        n, par, t = NSTEP * i + s, s // QT, s % QT
                        more = not (last and par == 1)
                        if t in (0, PAIRS - 1):
                            pe.wait_ge(win_loaded[par][t // (PAIRS - 1)], 32 * (i + 1))
                        if not (first and s < 2):
                            pe.wait_ge(probs_ready, n - 1)
                        base(s)
                        if more and 1 <= t <= PAIRS:
                            pe.wait_ge(band_kept, 4 * (PAIRS * (2 * i + par + 1) + t))
                        if not (first and s < 2):
                            times_v(*back(i, s, 2, NSTEP))
                        if not (first and s < 3):
                            add_parts(*back(i, s, 3, NSTEP))
                        if not (first and s < 1):
                            turn(n - 1, s - 1)
                        if more and t < PAIRS:
                            if t == 0:
                                pe.wait_ge(ops_loaded[1 - par], 64 * (i + 1 + par))
                            if not (first and s < 2):
                                pe.wait_ge(out_kept, n - 1)
                            if t == 2:
                                since(pe, ctx_kept, 2 * i + par)
                            band_tiles(t, 1 - par)

                pe.wait_ge(mask_loaded, 48)
                pe.wait_ge(ops_loaded[0], 64)
                for pair in range(PAIRS):
                    since(pe, band_kept, 4 * pair)
                    band_tiles(pair, 0)
                pe.wait_ge(band_kept, 4 * PAIRS)
                passes(pe, run)
                times_v(*back(G // 2, 0, 2, NSTEP))
                add_parts(*back(G // 2, 0, 3, NSTEP))
                turn(QT * G - 1, NSTEP - 1)
                add_parts(*back(G // 2, 0, 2, NSTEP))
                times_v(*back(G // 2, 0, 1, NSTEP))
                add_parts(*back(G // 2, 0, 1, NSTEP))

            @block.vector
            def _(dve):
                def keep_band(pair, pairs):
                    dve.wait_ge(band_mm, pairs)
                    for k in range(2):
                        for side in range(2):
                            o = side * (P + 1)
                            dve.scalar_tensor_tensor(band[:, side, 2 * pair + k, :], masks[:, side, :],
                                                     shared[:, k, o + P:o + P + 1], shared[:, k, o:o + P],
                                                     ALU.mult, ALU.add).then_inc(band_kept, 1)

                def keep_out(n, s):
                    dve.wait_ge(pv_done, n + 1)
                    since(dve, gathered, n - 1)
                    dve.tensor_copy(outT[:, s % 2, :], outp).then_inc(out_kept, 1)

                def keep_ctx(g, par):
                    dve.wait_ge(probs_ready, QT * (g + 1))
                    dve.reciprocal(rinv[:, par, :], rowsum[:, par, :]).then_inc(rinv_ready, 1)
                    dve.wait_ge(rinv_ready, g + 1)
                    dve.wait_ge(gathered, QT * (g + 1))
                    over = rinv[:, par, :].rearrange("p (t e) -> p t e", e=1).to_broadcast([P, QT, HD])
                    dve.tensor_tensor(ctx[:, :, g, :], ctxp[:], over, ALU.mult).then_inc(ctx_kept, 1)

                def keep_turned(n, s):
                    dve.wait_ge(probs_turned, n + 1)
                    since(dve, pv_done, n - 1)
                    dve.tensor_copy(probT[:, s % 2, QT // 2:QT, :], turned[:, QT // 2:QT, :]).then_inc(kept_v, 1)

                def run(i, first, last):
                    for s in range(NSTEP):
                        n, par, t = NSTEP * i + s, s // QT, s % QT
                        if t % PAIRS == 0:
                            dve.wait_ge(win_loaded[par][t // PAIRS], 32 * (i + 1))
                        lo, hi = max(t * P - 64, 0), min(t * P + 192, SEQ)
                        off = lo - (t * P - 64)
                        dve.wait_ge(base_done, n + 1)
                        row = scores[:, s % 2, :, :].rearrange("p b c -> p (b c)")
                        dve.tensor_tensor(row[:, lo:hi], row[:, lo:hi], cwin[:, par, t, off:off + hi - lo],
                                          ALU.add).then_inc(window_added, 1)
                        dve.wait_ge(window_added, n + 1)
                        dve.tensor_reduce(negmax[:, s % 2:s % 2 + 1], row, AX.X, ALU.max, negate=True).then_inc(max_ready, 1)
                        if not (first and s < 2):
                            keep_out(n - 2, s)
                        if t == 2 and not (first and par == 0):
                            keep_ctx(2 * i + par - 1, 1 - par)
                        if not (first and s < 1):
                            keep_turned(n - 1, s - 1)
                        if t < PAIRS and not (last and par == 1):
                            if t == 0:
                                dve.wait_ge(win_stored, 64 * (2 * i + par + 1))
                            keep_band(t, PAIRS * (2 * i + par + 1) + t + 1)

                dve.wait_ge(mask_loaded, 48)
                for pair in range(PAIRS):
                    keep_band(pair, pair + 1)
                passes(dve, run)
                n = QT * G
                keep_out(n - 2, NSTEP - 2)
                keep_turned(n - 1, NSTEP - 1)
                keep_out(n - 1, NSTEP - 1)
                keep_ctx(G - 1, 1)

            @block.scalar
            def _(act):
                def keep_turned(n, s):
                    act.wait_ge(probs_turned, n + 1)
                    since(act, pv_done, n - 1)
                    act.activation(probT[:, s % 2, 0:QT // 2, :], turned[:, 0:QT // 2, :], ACT.Copy).then_inc(kept_a, 1)

                def run(i, first, last):
                    for s in range(NSTEP):
                        n = NSTEP * i + s
                        if not (first and s < 1):
                            keep_turned(n - 1, s - 1)
                        act.wait_ge(max_ready, n + 1)
                        if not (first and s < 2):
                            act.wait_ge(probs_turned, n - 1)
                        if s % QT == 0 and not first:
                            act.wait_ge(rinv_ready, 2 * i + s // QT - 1)
                        act.activation(prob[:, s % 2, :], scores[:, s % 2, :, :].rearrange("p b c -> p (b c)"), ACT.Exp,
                                       bias=negmax[:, s % 2:s % 2 + 1],
                                       accum_out=rowsum[:, s // QT, s % QT:s % QT + 1]).then_inc(probs_ready, 1)

                passes(act, run)
                keep_turned(QT * G - 1, NSTEP - 1)

            @block.gpsimd
            def _(pool):
                def run(i, first, last):
                    for par in range(2):
                        place_v(pool, v_s, vh, HD, v_placed, pv_done, 2 * i + par, par, first)

                pool.memset(v_s[:], 0.0).then_inc(v_clear, 1)
                pool.wait_ge(v_clear, 1)
                passes(pool, run)


def attn_a_finish(nc, x, d, cst, xn, ctx):
    ident = cst["ident"]
    with stage(nc, "af") as st:
        wo = st.sb("wo", [D, D])
        rows = st.sb("rows", [P, 3, D])
        ctxT = st.sb("ctxT", [D, 2, P])
        y = st.sb("y", [P, NT, D])
        z = st.sb("z", [P, NT, D])
        banks = st.ps("banks", [P, 4, 512])
        loaded = st.sem("loaded")
        turned, kept, projected = st.sem("turned"), st.sem("kept"), st.sem("projected")
        summed, biased = st.sem("summed"), st.sem("biased")
        scaled, shifted, added = st.sem("scaled"), st.sem("shifted"), st.sem("added")
        with nc.Block() as block:

            @block.sync
            def _(sp):
                sp.dma_start(wo[:], d["L0_attn_a_Wo"]).then_inc(loaded, 16)
                for i, name in enumerate(("bo", "ln_scale", "ln_bias")):
                    src = d["L0_attn_a_" + name].rearrange("(o n) -> o n", o=1).to_broadcast([P, D])
                    sp.dma_start(rows[:, i, :], src).then_inc(loaded, 16)

            @block.tensor
            def _(pe):
                for t in range(NT):
                    b, qt = t // QT, t % QT
                    if t >= 2:
                        pe.wait_ge(kept, t - 1)
                    src = ctx[:, qt, b * HEADS:(b + 1) * HEADS, :].rearrange("p g e -> p (g e)")
                    pe.transpose(banks[:, t % 2, 0:P], src, ident[:]).then_inc(turned, 1)
                    if t == 0:
                        pe.wait_ge(loaded, 64)
                    pe.wait_ge(kept, t + 1)
                    if t >= 2:
                        pe.wait_ge(summed, t - 1)
                    pe.matmul(banks[:, 2 + t % 2, 0:D], ctxT[:, t % 2, :], wo[:], start=True, stop=True).then_inc(projected, 1)

            @block.scalar
            def _(act):
                for t in range(NT):
                    act.wait_ge(turned, t + 1)
                    if t >= 2:
                        act.wait_ge(projected, t - 1)
                    act.activation(ctxT[:, t % 2, :], banks[:, t % 2, 0:P], ACT.Copy).then_inc(kept, 1)

            @block.vector
            def _(dve):
                dve.wait_ge(loaded, 64)
                for t in range(NT):
                    dve.tensor_tensor(xn[:, t, :], xn[:, t, :], rows[:, 0, :], ALU.add).then_inc(biased, 1)
                for t in range(NT):
                    dve.wait_ge(projected, t + 1)
                    dve.wait_ge(biased, t + 1)
                    dve.tensor_tensor(y[:, t, :], banks[:, 2 + t % 2, 0:D], xn[:, t, :], ALU.add).then_inc(summed, 1)
        layer_norm(nc, st, y, z, 1e-7)
        with nc.Block() as block:

            @block.vector
            def _(dve):
                for t in range(NT):
                    dve.tensor_tensor(z[:, t, :], z[:, t, :], rows[:, 1, :], ALU.mult).then_inc(scaled, 1)
                for t in range(NT):
                    dve.wait_ge(scaled, t + 1)
                    dve.tensor_tensor(z[:, t, :], z[:, t, :], rows[:, 2, :], ALU.add).then_inc(shifted, 1)
                for t in range(NT):
                    dve.wait_ge(shifted, t + 1)
                    dve.tensor_tensor(x[:, t, :], x[:, t, :], z[:, t, :], ALU.add).then_inc(added, 1)


FF_DEPTH = 2
FF_HEADS = 8
FF_HD = 64
FF_WIN = 64
FF_INNER = FF_HEADS * FF_HD
FF_PAIRS = FF_INNER // P
HID = int(D * 4 * 2 / 3)
HID_CUT = [(0, 128), (128, 256), (256, HID)]
NEG = -1e30


def ffn_constants():
    f4 = np.float32
    half = np.arange(0, FF_HD, 2, dtype=f4)
    inv_freq = (f4(1.0) / np.power(f4(10000.0), half / f4(FF_HD))).astype(f4)
    t = np.arange(SEQ, dtype=f4)
    freqs = t[:, None] * inv_freq[None, :]
    base = ((half + f4(0.4 * FF_HD)) / f4(1.4 * FF_HD)).astype(f4)
    power = ((t - SEQ // 2) / f4(FF_WIN // 2)).astype(f4)
    scale = np.power(base[None, :], power[:, None]).astype(f4)
    cos, sin = np.cos(freqs), np.sin(freqs)
    two = lambda a: np.concatenate([a, a], axis=-1)
    signed = np.concatenate([-sin, sin], axis=-1)
    tabs = np.stack([two(cos * scale), signed * two(scale), two(cos / scale), signed / two(scale)]).astype(f4)
    rot = tabs.reshape(4, QT, P, FF_HD).transpose(2, 0, 1, 3)
    m, i = np.arange(P)[None, :], (np.arange(P) % FF_WIN)[:, None]
    allowed = (m <= i + FF_WIN) & (m >= i)
    first = allowed & ((m >= FF_WIN) | (np.arange(P)[:, None] >= FF_WIN))
    mask = np.where(np.stack([allowed, first], axis=1), 0.0, NEG).astype(f4)
    shift = np.zeros((P, 2, P), f4)
    shift[np.arange(P - 1), 0, np.arange(1, P)] = 1
    shift[P - 1, 1, 0] = 1
    return {"rot": np.ascontiguousarray(rot), "local_mask": mask, "shift": shift}


def ffn(nc, x, d, cst, tag):
    with stage(nc, tag) as st:
        u = st.sb("u", [P, NT, D])
        layer_norm(nc, st, x, u, 1e-5)
        with nc.Fori(0, FF_DEPTH) as layer:
            ffn_attention(nc, u, d, cst, layer, tag + "a")
            ffn_glu(nc, u, d, cst, layer, tag + "g")
        added = st.sem("added")
        with nc.Block() as block:

            @block.vector
            def _(dve):
                dve.tensor_tensor(x[:], x[:], u[:], ALU.add).then_inc(added, 1)


def row_of(ap, n):
    return ap.rearrange("(o n) -> o n", o=1).to_broadcast([n, ap.shape[0]])


def ffn_attention(nc, u, d, cst, layer, tag):
    ident, shift = cst["ident"], cst["shift"]
    PAD = FF_WIN
    with stage(nc, tag) as st:
        qT = st.sb("qT", [P, FF_PAIRS, TOK])
        kT = st.sb("kT", [P, FF_PAIRS, PAD + TOK])
        v_own = st.sb("v_own", [P, NT, FF_HEADS, FF_HD + 1])
        v_prev = st.sb("v_prev", [P, NT, FF_HEADS, FF_HD + 1])
        ffn_qkv(nc, u, d, cst, layer, tag + "q", qT, kT, v_own, v_prev)
        ffn_windows(nc, u, d, cst, layer, tag + "w", qT, kT, v_own, v_prev)


def ffn_qkv(nc, u, d, cst, layer, tag, qT, kT, v_own, v_prev):
    ident = cst["ident"]
    QK = (2, FF_HEADS, FF_HD)
    with stage(nc, tag) as st:
        w = st.sb("w", [D, 3 * FF_INNER])
        srow = st.sb("srow", [P, 2, FF_HD])
        rot = st.sb("rot", [P, 2, 2, QT, FF_HD])
        hT = st.sb("hT", [D, TOK])
        sq = st.sb("sq", [P, 2, *QK])
        norm = st.sb("norm", [P, 2, 2, FF_HEADS])
        rn = st.sb("rn", [P, 2, 2, FF_HEADS])
        tc = st.sb("tc", [P, 3, *QK])
        ts_ = st.sb("ts", [P, 2, *QK])
        qk = st.ps("qk", [P, 2, 2, 512])
        vp = st.ps("vp", [P, 512])
        hp = st.ps("hp", [P, 512])
        tp = st.ps("tp", [P, 2, 512])
        loaded, table_ready = st.sem("loaded"), st.sem("table_ready")
        h_turned, h_kept, filled = st.sem("h_turned"), st.sem("h_kept"), st.sem("filled")
        qk_done, v_done, v_kept, v_moved = (st.sem(n) for n in ("qk_done", "v_done", "v_kept", "v_moved"))
        squared, summed, rooted, clipped, inverted = (st.sem(n) for n in ("squared", "summed", "rooted", "clipped", "inverted"))
        products, rotated, q_scaled, k_scaled = (st.sem(n) for n in ("products", "rotated", "q_scaled", "k_scaled"))
        turned, kept = st.sem("turned"), st.sem("kept")
        with nc.Block() as block:

            @block.sync
            def _(sp):
                sp.dma_start(w[:], d["L0_ffn_wqkv"][layer]).then_inc(loaded, 16)
                sp.dma_start(srow[:, 0, :], d["L0_ffn_q_scale"][bass.ts(layer, 1), :].to_broadcast([P, FF_HD])).then_inc(loaded, 16)
                sp.dma_start(srow[:, 1, :], d["L0_ffn_k_scale"][bass.ts(layer, 1), :].to_broadcast([P, FF_HD])).then_inc(loaded, 16)
                sp.dma_start(rot[:], d["rot"].rearrange("p (i c) t e -> p i c t e", c=2)).then_inc(loaded, 16)
                sp.wait_ge(filled, 4)
                for c in range(NCH):
                    sp.wait_ge(v_kept, 4 * c + 4)
                    lo, hi = 4 * c, 4 * c + 4
                    end = min(hi, NT - 1)
                    sp.dma_start(v_prev[FF_WIN:P, lo:hi], v_own[0:FF_WIN, lo:hi]).then_inc(v_moved, 16)
                    sp.dma_start(v_prev[0:FF_WIN, lo + 1:end + 1], v_own[FF_WIN:P, lo:end]).then_inc(v_moved, 16)
                sp.wait_ge(v_moved, 32 * NCH)

            @block.tensor
            def _(pe):
                def turn_h(c):
                    since(pe, h_kept, 2 * c)
                    for j in range(4):
                        mm = pe.transpose(hp[:, j * P:(j + 1) * P], u[:, 4 * c + j, :], ident[:])
                    mm.then_inc(h_turned, 1)

                def turn(t):
                    pe.wait_ge(k_scaled, t + 1)
                    pe.wait_ge(q_scaled, t + 1)
                    since(pe, kept, 2 * t)
                    for i in range(2):
                        flat = tc[:, t % 3, i].rearrange("p h e -> p (h e)")
                        for c in range(FF_PAIRS):
                            mm = pe.transpose(tp[:, i, c * P:(c + 1) * P], flat[:, c * P:(c + 1) * P], ident[:])
                    mm.then_inc(turned, 1)

                turn_h(0)
                pe.wait_ge(loaded, 64)
                pe.wait_ge(filled, 4)
                for t in range(NT):
                    own = hT[:, t * P:(t + 1) * P]
                    if t % 4 == 0:
                        pe.wait_ge(h_kept, 2 * (t // 4) + 2)
                    since(pe, products, 3 * (t - 1))
                    since(pe, squared, t - 1)
                    for i in range(2):
                        mm = pe.matmul(qk[:, t % 2, i, :], own, w[:, i * FF_INNER:(i + 1) * FF_INNER], start=True, stop=True)
                    mm.then_inc(qk_done, 1)
                    since(pe, v_kept, t)
                    pe.matmul(vp[:], own, w[:, 2 * FF_INNER:], start=True, stop=True).then_inc(v_done, 1)
                    if t % 4 == 1 and t // 4 + 1 < NCH:
                        turn_h(t // 4 + 1)
                    if t >= 2:
                        turn(t - 2)
                turn(NT - 2)
                turn(NT - 1)

            @block.scalar
            def _(act):
                def keep(t):
                    act.wait_ge(turned, t + 1)
                    for i, (buf, pad) in enumerate(((qT, 0), (kT, FF_WIN))):
                        src = tp[:, i, :].rearrange("p (c n) -> p c n", c=FF_PAIRS)
                        act.activation(buf[:, :, pad + t * P:pad + (t + 1) * P], src, ACT.Copy).then_inc(kept, 1)

                def keep_h(c):
                    act.wait_ge(h_turned, c + 1)
                    act.activation(hT[0:64, c * 512:(c + 1) * 512], hp[0:64, :], ACT.Copy).then_inc(h_kept, 1)
                    n = 512 if (c + 1) * 512 % SEQ else 511
                    act.activation(hT[64:P, c * 512 + 1:c * 512 + 1 + n], hp[64:P, 0:n], ACT.Copy).then_inc(h_kept, 1)

                act.wait_ge(filled, 4)
                keep_h(0)
                for t in range(NT + 2):
                    if t < NT:
                        act.wait_ge(qk_done, t + 1)
                        since(act, summed, t - 1)
                        act.activation(sq[:, t % 2].rearrange("p i h e -> p i (h e)"), qk[:, t % 2], ACT.Square).then_inc(squared, 1)
                    if 1 <= t <= NT:
                        act.wait_ge(summed, t)
                        act.activation(norm[:, (t - 1) % 2], norm[:, (t - 1) % 2], ACT.Sqrt).then_inc(rooted, 1)
                    if t < NT:
                        act.wait_ge(v_done, t + 1)
                        act.activation(v_own[:, t, :, 0:FF_HD], vp[:].rearrange("p (h e) -> p h e", h=FF_HEADS),
                                       ACT.Copy).then_inc(v_kept, 1)
                        if t % 4 == 1 and t // 4 + 1 < NCH:
                            keep_h(t // 4 + 1)
                    if t >= 2:
                        keep(t - 2)

            @block.vector
            def _(dve):
                dve.wait_ge(loaded, 64)
                half = FF_HD // 2
                for i in range(2):
                    cosrow = srow[:, i, :].rearrange("p (o e) -> p o e", o=1).to_broadcast([P, QT, FF_HD])
                    dve.tensor_tensor(rot[:, i, 0], rot[:, i, 0], cosrow, ALU.mult).then_inc(table_ready, 1)
                    for a, b in ((0, half), (half, 0)):
                        sinrow = srow[:, i, b:b + half].rearrange("p (o e) -> p o e", o=1).to_broadcast([P, QT, half])
                        dve.tensor_tensor(rot[:, i, 1, :, a:a + half], rot[:, i, 1, :, a:a + half], sinrow,
                                          ALU.mult).then_inc(table_ready, 1)
                dve.wait_ge(table_ready, 6)

                def times_cos(t):
                    dve.wait_ge(squared, t + 1)
                    since(dve, turned, t - 2)
                    src = qk[:, t % 2].rearrange("p i (h e) -> p i h e", e=FF_HD)
                    cosb = rot[:, :, 0, t % QT, :].rearrange("p i (o e) -> p i o e", o=1).to_broadcast([P, *QK])
                    dve.tensor_tensor(tc[:, t % 3], src, cosb, ALU.mult).then_inc(products, 1)

                def times_sin(t):
                    since(dve, rotated, 2 * (t - 1))
                    src = qk[:, t % 2].rearrange("p i (h e) -> p i h e", e=FF_HD)
                    for a, b in ((0, half), (half, 0)):
                        sinb = rot[:, :, 1, t % QT, a:a + half].rearrange("p i (o e) -> p i o e", o=1)
                        dve.tensor_tensor(ts_[:, t % 2, :, :, a:a + half], src[:, :, :, b:b + half],
                                          sinb.to_broadcast([P, 2, FF_HEADS, half]), ALU.mult).then_inc(products, 1)

                def clip(t):
                    dve.wait_ge(rooted, t + 1)
                    since(dve, q_scaled, t - 1)
                    since(dve, k_scaled, t - 1)
                    dve.tensor_scalar(rn[:, t % 2], norm[:, t % 2], 1e-12, None, ALU.max).then_inc(clipped, 1)

                for t in range(NT + 1):
                    if t < NT:
                        times_cos(t)
                    if t >= 1:
                        clip(t - 1)
                    if t < NT:
                        times_sin(t)
                    if t >= 1:
                        dve.wait_ge(clipped, t)
                        dve.reciprocal(rn[:, (t - 1) % 2], rn[:, (t - 1) % 2]).then_inc(inverted, 1)
                    if t < NT:
                        since(dve, clipped, t - 1)
                        dve.tensor_reduce(norm[:, t % 2], sq[:, t % 2], AX.X, ALU.add).then_inc(summed, 1)
                    if t >= 1:
                        r = t - 1
                        dve.wait_ge(inverted, r + 1)
                        dve.wait_ge(rotated, 2 * r + 1)
                        rnb = rn[:, r % 2, 1, :].rearrange("p (h o) -> p h o", o=1).to_broadcast([P, FF_HEADS, FF_HD])
                        dve.tensor_tensor(tc[:, r % 3, 1], tc[:, r % 3, 1], rnb, ALU.mult).then_inc(k_scaled, 1)

            @block.gpsimd
            def _(pool):
                pool.memset(kT[:, :, 0:FF_WIN], 0.0).then_inc(filled, 1)
                pool.memset(v_own[:, :, :, FF_HD:FF_HD + 1], 1.0).then_inc(filled, 1)
                pool.wait_ge(filled, 2)
                pool.memset(v_prev[0:FF_WIN, 0], 0.0).then_inc(filled, 1)
                pool.wait_ge(filled, 3)
                pool.memset(hT[64:P, :].rearrange("p (b n) -> p b n", n=SEQ)[:, :, 0:1], 0.0).then_inc(filled, 1)
                for t in range(NT + 1):
                    if t < NT:
                        pool.wait_ge(products, 3 * t + 3)
                        for i in (1, 0):
                            pool.tensor_tensor(tc[:, t % 3, i], tc[:, t % 3, i], ts_[:, t % 2, i], ALU.add).then_inc(rotated, 1)
                    if t >= 1:
                        r = t - 1
                        pool.wait_ge(rotated, 2 * r + 2)
                        pool.wait_ge(inverted, r + 1)
                        rnb = rn[:, r % 2, 0, :].rearrange("p (h o) -> p h o", o=1).to_broadcast([P, FF_HEADS, FF_HD])
                        pool.tensor_tensor(tc[:, r % 3, 0], tc[:, r % 3, 0], rnb, ALU.mult).then_inc(q_scaled, 1)


def ffn_windows(nc, u, d, cst, layer, tag, qT, kT, v_own, v_prev):
    ident = cst["ident"]
    HB = FF_HEADS // 2
    with stage(nc, tag) as st:
        wo = st.sb("wo", [P, FF_PAIRS, D])
        mask = st.sb("mask", [P, 2, P])
        maskb = st.sb("maskb", [P, 2, HB, P], BF16)
        identb = st.sb("identb", [P, P], BF16)
        mx = st.sb("mx", [P, 2, FF_HEADS])
        less = st.sb("less", [P, 2, FF_HEADS, P])
        prob = st.sb("prob", [P, 2, FF_HEADS, P])
        probT = st.sb("probT", [P, 2, FF_HEADS, P])
        rinv = st.sb("rinv", [P, 2, FF_HEADS])
        o = st.sb("o", [P, 2, FF_HEADS, FF_HD])
        oT = st.sb("oT", [P, 2, FF_PAIRS, P])
        scores = st.ps("scores", [P, 2, 512])
        turned = st.ps("turned", [P, 2, 512])
        outp = st.ps("outp", [P, 2, 512])
        oTp = st.ps("oTp", [P, 512])
        projp = st.ps("projp", [P, 512])
        loaded, cast = st.sem("loaded"), st.sem("cast")
        scored, max_ready, lessened, probs_ready = (st.sem(n) for n in ("scored", "max_ready", "lessened", "probs_ready"))
        probs_turned, t_kept, pv_done, inverted, o_ready = (st.sem(n) for n in ("probs_turned", "t_kept", "pv_done", "inverted", "o_ready"))
        o_turned, oT_kept, projected, added = (st.sem(n) for n in ("o_turned", "oT_kept", "projected", "added"))
        with nc.Block() as block:

            @block.sync
            def _(sp):
                sp.dma_start(wo[:], d["L0_ffn_wo"][layer].rearrange("(c p) n -> p c n", p=P)).then_inc(loaded, 16)
                sp.dma_start(mask[:], d["local_mask"]).then_inc(loaded, 16)

            @block.tensor
            def _(pe):
                def score(t):
                    if t >= 1:
                        pe.wait_ge(lessened, 2 * t)
                    which = 1 if t % QT == 0 else 0
                    for b in range(2):
                        pe.matmul(scores[:, b, :], identb[:], maskb[:, which].rearrange("p h n -> p (h n)"),
                                  start=True, stop=False, skip_group_check=True)
                        for h4 in range(HB):
                            rows, pair = slice(b * 64, b * 64 + 64), h4
                            for w in range(2):
                                k0 = t * P + w * FF_WIN
                                mm = pe.matmul(scores[w * 64:w * 64 + 64, b, h4 * P:(h4 + 1) * P],
                                               qT[rows, pair, t * P + w * 64:t * P + w * 64 + 64],
                                               kT[rows, pair, k0:k0 + P], start=False,
                                               stop=h4 == HB - 1, skip_group_check=True)
                    mm.then_inc(scored, 1)

                def turn(t):
                    pe.wait_ge(probs_ready, t + 1)
                    if t >= 1:
                        pe.wait_ge(t_kept, t)
                    for h in range(FF_HEADS):
                        mm = pe.transpose(turned[:, h // HB, h % HB * P:(h % HB + 1) * P], prob[:, t % 2, h, :], ident[:])
                    mm.then_inc(probs_turned, 1)

                def times_v(t):
                    pe.wait_ge(t_kept, t + 1)
                    since(pe, o_ready, 2 * t)
                    for h in range(FF_HEADS):
                        slot = h % 2 * HB + h // 2
                        for w, v in ((0, v_prev), (1, v_own)):
                            mm = pe.matmul(outp[w * 64:w * 64 + 64, h // HB, h % HB * 65:h % HB * 65 + 65],
                                           probT[:, t % 2, slot, w * 64:w * 64 + 64], v[:, t, h, :], start=True, stop=True)
                    mm.then_inc(pv_done, 1)

                def turn_o(t):
                    pe.wait_ge(o_ready, 2 * t + 2)
                    since(pe, oT_kept, t)
                    of = o[:, t % 2].rearrange("p h e -> p (h e)")
                    for c in range(FF_PAIRS):
                        mm = pe.transpose(oTp[:, c * P:(c + 1) * P], of[:, c * P:(c + 1) * P], ident[:])
                    mm.then_inc(o_turned, 1)

                def project(t):
                    pe.wait_ge(oT_kept, t + 1)
                    since(pe, added, t)
                    for c in range(FF_PAIRS):
                        mm = pe.matmul(projp[:, 0:D], oT[:, t % 2, c, :], wo[:, c, :], start=c == 0, stop=c == FF_PAIRS - 1)
                    mm.then_inc(projected, 1)

                pe.wait_ge(cast, 2)
                pe.wait_ge(loaded, 32)
                for t in range(NT + 4):
                    if t < NT:
                        score(t)
                    if 2 <= t < NT + 2:
                        times_v(t - 2)
                    if 1 <= t <= NT:
                        turn(t - 1)
                    if 3 <= t < NT + 3:
                        turn_o(t - 3)
                    if 4 <= t:
                        project(t - 4)

            @block.scalar
            def _(act):
                def keep(t):
                    act.wait_ge(probs_turned, t + 1)
                    since(act, pv_done, t - 1)
                    act.activation(probT[:, t % 2], turned[:].rearrange("p b (h n) -> p (b h) n", h=HB), ACT.Copy).then_inc(t_kept, 1)

                def keep_o(t):
                    act.wait_ge(o_turned, t + 1)
                    since(act, projected, t - 1)
                    act.activation(oT[:, t % 2].rearrange("p c n -> p (c n)"), oTp[:], ACT.Copy).then_inc(oT_kept, 1)

                for t in range(NT + 3):
                    if t < NT:
                        act.wait_ge(lessened, 2 * t + 2)
                        if t >= 2:
                            act.wait_ge(probs_turned, t - 1)
                        act.activation(prob[:, t % 2, :, :], less[:, t % 2, :, :], ACT.Exp, scale=8.0).then_inc(probs_ready, 1)
                    if 1 <= t <= NT:
                        keep(t - 1)
                    if 3 <= t:
                        keep_o(t - 3)

            @block.vector
            def _(dve):
                dve.wait_ge(loaded, 32)
                dve.tensor_copy(maskb[:], mask[:].rearrange("p k (o n) -> p k o n", o=1).to_broadcast([P, 2, HB, P])).then_inc(cast, 1)
                dve.tensor_copy(identb[:], ident[:]).then_inc(cast, 1)

                def normalise(t):
                    dve.wait_ge(pv_done, t + 1)
                    sums = outp[:, :, 0:HB * 65].rearrange("p b (h e) -> p b h e", e=65)
                    since(dve, o_ready, 2 * (t - 1))
                    since(dve, o_turned, t - 1)
                    dve.reciprocal(rinv[:, t % 2].rearrange("p (b h o) -> p b h o", b=2, o=1), sums[:, :, :, 64:65]).then_inc(inverted, 1)
                    dve.wait_ge(inverted, t + 1)
                    for b in range(2):
                        rb = rinv[:, t % 2, b * HB:(b + 1) * HB].rearrange("p (h o) -> p h o", o=1).to_broadcast([P, HB, FF_HD])
                        dve.tensor_tensor(o[:, t % 2, b * HB:(b + 1) * HB, :], sums[:, b, :, 0:FF_HD], rb, ALU.mult).then_inc(o_ready, 1)

                def add(t):
                    dve.wait_ge(projected, t + 1)
                    dve.tensor_tensor(u[:, t, :], u[:, t, :], projp[:, 0:D], ALU.add).then_inc(added, 1)

                for t in range(NT + 4):
                    if t < NT:
                        dve.wait_ge(scored, t + 1)
                        sv = scores[:].rearrange("p b (h n) -> p b h n", h=HB)
                        mxv = mx[:, t % 2, :].rearrange("p (b h) -> p b h", b=2)
                        dve.tensor_reduce(mxv, sv, AX.X, ALU.max).then_inc(max_ready, 1)
                        dve.wait_ge(max_ready, t + 1)
                        if t >= 2:
                            dve.wait_ge(probs_ready, t - 1)
                        for b in range(2):
                            mb = mx[:, t % 2, b * HB:(b + 1) * HB].rearrange("p (h o) -> p h o", o=1).to_broadcast([P, HB, P])
                            dve.tensor_tensor(less[:, t % 2, b * HB:(b + 1) * HB, :], sv[:, b], mb, ALU.subtract).then_inc(lessened, 1)
                    if 2 <= t < NT + 2:
                        normalise(t - 2)
                    if 4 <= t:
                        add(t - 4)


def ffn_glu(nc, u, d, cst, layer, tag):
    ident, shift = cst["ident"], cst["shift"]
    with stage(nc, tag) as st:
        h = st.sb("h", [P, NT, D])
        hT = st.sb("hT", [D, TOK])
        w1 = st.sb("w1", [D, 2 * HID])
        w2 = st.sb("w2", [P, 3, D])
        b1 = st.sb("b1", [P, 6])
        b2 = st.sb("b2", [P, D])
        affine = st.sb("affine", [D, 2])
        act_g = st.sb("act_g", [P, 2, 3, 512])
        hid = st.sb("hid", [P, 2, 3, 512])
        banks = st.ps("banks", [P, 8, 512])
        loaded = st.sem("loaded")
        shifted, kept, biased = st.sem("shifted"), st.sem("kept"), st.sem("biased")
        turned, hT_ready = st.sem("turned"), st.sem("hT_ready")
        a_done, g_done, gelu_done, hid_done = (st.sem(n) for n in ("a_done", "g_done", "gelu_done", "hid_done"))
        down_done, added = st.sem("down_done"), st.sem("added")
        with nc.Block() as block:

            @block.sync
            def _(sp):
                sp.dma_start(w1[:], d["L0_ffn_w1"][layer]).then_inc(loaded, 16)
                for j, (a, b) in enumerate(HID_CUT):
                    sp.dma_start(w2[0:b - a, j, :], d["L0_ffn_w2"][layer][a:b, :]).then_inc(loaded, 16)
                    for i in range(2):
                        src = d["L0_ffn_b1"][layer][i * HID + a:i * HID + b].rearrange("(p o) -> p o", o=1)
                        sp.dma_start(b1[0:b - a, 3 * i + j:3 * i + j + 1], src).then_inc(loaded, 16)
                sp.dma_start(b2[:], d["L0_ffn_b2"][bass.ts(layer, 1), :].to_broadcast([P, D])).then_inc(loaded, 16)
                sp.dma_start(affine[:, 0:1], d["L0_ffn_ln_g"][layer].rearrange("(p o) -> p o", o=1)).then_inc(loaded, 16)
                sp.dma_start(affine[:, 1:2], d["L0_ffn_ln_b"][layer].rearrange("(p o) -> p o", o=1)).then_inc(loaded, 16)
                sp.wait_ge(loaded, 16 * 13)

            @block.tensor
            def _(pe):
                for t in range(NT):
                    if t >= 2:
                        pe.wait_ge(kept, t - 1)
                    first = t % QT == 0
                    mm = pe.matmul(banks[:, t % 2, 0:64], shift[:, 0, :], u[:, t, 64:D], start=True, stop=first)
                    if not first:
                        mm = pe.matmul(banks[:, t % 2, 0:64], shift[:, 1, :], u[:, t - 1, 64:D], start=False, stop=True)
                    mm.then_inc(shifted, 1)

            @block.scalar
            def _(act):
                act.activation(h[:, :, 0:64], u[:, :, 0:64], ACT.Copy)

            @block.vector
            def _(dve):
                for t in range(NT):
                    dve.wait_ge(shifted, t + 1)
                    dve.tensor_copy(h[:, t, 64:D], banks[:, t % 2, 0:64]).then_inc(kept, 1)
        layer_norm(nc, st, h, h, 1e-5)
        with nc.Block() as block:

            @block.tensor
            def _(pe):
                def turn(c):
                    for j in range(4):
                        mm = pe.transpose(banks[:, 6, j * P:(j + 1) * P], h[:, 4 * c + j, :], ident[:])
                    mm.then_inc(turned, 1)

                def down(c):
                    pe.wait_ge(hid_done, 3 * c + 3)
                    for i in range(4):
                        for j, (a, b) in enumerate(HID_CUT):
                            mm = pe.matmul(banks[:, 7, i * P:(i + 1) * P], hid[0:b - a, c % 2, j, i * P:(i + 1) * P],
                                           w2[0:b - a, j, :], start=j == 0, stop=j == 2)
                    mm.then_inc(down_done, 1)

                turn(0)
                for c in range(NCH):
                    pe.wait_ge(hT_ready, c + 1)
                    if c + 1 < NCH:
                        turn(c + 1)
                    for j, (a, b) in enumerate(HID_CUT):
                        if c >= 1:
                            pe.wait_ge(gelu_done, 3 * (c - 1) + j + 1)
                        pe.matmul(banks[0:b - a, 3 + j, :], w1[:, HID + a:HID + b], hT[:, c * 512:(c + 1) * 512],
                                  start=True, stop=True).then_inc(g_done, 1)
                        if c >= 1:
                            pe.wait_ge(hid_done, 3 * (c - 1) + j + 1)
                        pe.matmul(banks[0:b - a, j, :], w1[:, a:b], hT[:, c * 512:(c + 1) * 512],
                                  start=True, stop=True).then_inc(a_done, 1)
                    if c >= 1:
                        if c >= 2:
                            pe.wait_ge(added, c - 1)
                        down(c - 1)
                pe.wait_ge(added, NCH - 1)
                down(NCH - 1)

            @block.scalar
            def _(act):
                for c in range(NCH):
                    for j, (a, b) in enumerate(HID_CUT):
                        act.wait_ge(g_done, 3 * c + j + 1)
                        if c >= 2:
                            act.wait_ge(hid_done, 3 * (c - 2) + j + 1)
                        act.activation(act_g[0:b - a, c % 2, j, :], banks[0:b - a, 3 + j, :], ACT.Gelu,
                                       bias=b1[0:b - a, 3 + j:4 + j]).then_inc(gelu_done, 1)

            @block.vector
            def _(dve):
                b2v = b2[:].rearrange("p (o n) -> p o n", o=1).to_broadcast([P, NT, D])
                dve.tensor_tensor(u[:], u[:], b2v, ALU.add).then_inc(biased, 1)

                def keep_h(c):
                    dve.wait_ge(turned, c + 1)
                    dve.tensor_scalar(hT[:, c * 512:(c + 1) * 512], banks[:, 6, :], affine[:, 0:1], affine[:, 1:2],
                                      ALU.mult, ALU.add).then_inc(hT_ready, 1)

                def add(c):
                    dve.wait_ge(down_done, c + 1)
                    dve.wait_ge(biased, 1)
                    y = banks[:, 7, :].rearrange("p (t n) -> p t n", t=4)
                    dve.tensor_tensor(u[:, 4 * c:4 * c + 4, :], u[:, 4 * c:4 * c + 4, :], y, ALU.add).then_inc(added, 1)

                keep_h(0)
                for c in range(NCH):
                    if c + 1 < NCH:
                        keep_h(c + 1)
                    for j, (a, b) in enumerate(HID_CUT):
                        dve.wait_ge(a_done, 3 * c + j + 1)
                        dve.wait_ge(gelu_done, 3 * c + j + 1)
                        if c >= 2:
                            dve.wait_ge(down_done, c - 1)
                        dve.scalar_tensor_tensor(hid[0:b - a, c % 2, j, :], banks[0:b - a, j, :], b1[0:b - a, j:j + 1],
                                                 act_g[0:b - a, c % 2, j, :], ALU.add, ALU.mult).then_inc(hid_done, 1)
                    if c >= 1:
                        add(c - 1)
                add(NCH - 1)


NSTATE = 16


def attn_b(nc, x, d, cst):
    ident = cst["ident"]
    with stage(nc, "ab") as st:
        xn = st.sb("xn", [P, NT, D])
        layer_norm(nc, st, x, xn, 1e-5)
        xT = st.sb("xT", [D, TOK])
        banks = st.ps("banks", [P, 8, 512])
        transpose_all(nc, st, xn, xT, ident, banks[:, 0:2, :])
        z = st.sb("z", [D, TOK])
        dt = st.sb("dt", [D, TOK])
        dtx = st.sb("dtx", [D, TOK])
        y = st.sb("y", [D, TOK])
        attn_b_prepare(nc, d, xT, banks, z, dt, dtx)
        attn_b_scan(nc, d, xT, banks, dt, dtx, y)
        attn_b_finish(nc, x, d, banks, z, y)


def attn_b_prepare(nc, d, xT, banks, z, dt, dtx):
    with stage(nc, "bp") as st:
        w = st.sb("w", [D, 3, D])
        b = st.sb("b", [D, 3])
        pos = st.sb("pos", [D, TOK])
        loaded, projected = st.sem("loaded"), st.sem("projected")
        gate, dt_in, magnitude, decayed, plus_one, logged = (st.sem(n) for n in (
            "gate", "dt_in", "magnitude", "decayed", "plus_one", "logged"))
        positive, dt_ready, xs_ready, dtx_ready = (st.sem(n) for n in ("positive", "dt_ready", "xs_ready", "dtx_ready"))
        with nc.Block() as block:

            @block.sync
            def _(sp):
                for i, name in enumerate(("z", "dt", "x")):
                    sp.dma_start(w[:, i, :], d["L0_attn_b_W" + name]).then_inc(loaded, 16)
                    sp.dma_start(b[:, i:i + 1], d["L0_attn_b_b" + name].rearrange("(p o) -> p o", o=1)).then_inc(loaded, 16)

            @block.tensor
            def _(pe):
                pe.wait_ge(loaded, 96)
                for c in range(NCH):
                    for i, used in enumerate((gate, dt_in, xs_ready)):
                        if c >= 2:
                            pe.wait_ge(used, c - 1)
                        pe.matmul(banks[:, 2 * i + c % 2, :], w[:, i, :], xT[:, c * 512:(c + 1) * 512], start=True,
                                  stop=True).then_inc(projected, 1)

            @block.scalar
            def _(act):
                for c in range(NCH):
                    act.wait_ge(projected, 3 * c + 1)
                    act.activation(z[:, c * 512:(c + 1) * 512], banks[:, c % 2, :], ACT.Sigmoid, bias=b[:, 0:1]).then_inc(gate, 1)
                act.wait_ge(positive, 1)
                act.activation(dt[:], dt[:], ACT.Abs).then_inc(magnitude, 1)
                act.wait_ge(magnitude, 1)
                act.activation(dt[:], dt[:], ACT.Exp, scale=-1.0).then_inc(decayed, 1)
                act.wait_ge(plus_one, 1)
                act.activation(dt[:], dt[:], ACT.Ln).then_inc(logged, 1)

            @block.vector
            def _(dve):
                for c in range(NCH):
                    cs = slice(c * 512, (c + 1) * 512)
                    dve.wait_ge(projected, 3 * c + 2)
                    dve.tensor_scalar(dt[:, cs], banks[:, 2 + c % 2, :], b[:, 1:2], None, ALU.add).then_inc(dt_in, 1)
                    dve.wait_ge(projected, 3 * c + 3)
                    dve.tensor_scalar(dtx[:, cs], banks[:, 4 + c % 2, :], b[:, 2:3], None, ALU.add).then_inc(xs_ready, 1)
                dve.wait_ge(dt_in, NCH)
                dve.tensor_scalar(pos[:], dt[:], 0.0, None, ALU.max).then_inc(positive, 1)
                dve.wait_ge(decayed, 1)
                dve.tensor_scalar(dt[:], dt[:], 1.0, None, ALU.add).then_inc(plus_one, 1)
                dve.wait_ge(logged, 1)
                dve.tensor_tensor(dt[:], dt[:], pos[:], ALU.add).then_inc(dt_ready, 1)
                dve.wait_ge(dt_ready, 1)
                dve.wait_ge(xs_ready, NCH)
                dve.tensor_tensor(dtx[:], dtx[:], dt[:], ALU.mult).then_inc(dtx_ready, 1)


def attn_b_scan(nc, d, xT, banks, dt, dtx, y):
    with stage(nc, "bs") as st:
        wrow = st.sb("wrow", [D, 2, NSTATE])
        wrep = st.sb("wrep", [D, 2, NSTATE, D])
        brow = st.sb("brow", [D, 2, NSTATE])
        a = st.sb("a", [D, NSTATE])
        decay = st.sb("decay", [D, 2, SEQ])
        inp = st.sb("inp", [D, 2, SEQ])
        h = st.sb("h", [D, 2, SEQ])
        hc = st.sb("hc", [D, 2, SEQ])
        loaded, repeated, a_exp, a_ready = (st.sem(n) for n in ("loaded", "repeated", "a_exp", "a_ready"))
        b_done, c_done, decay_ready, inp_ready, scanned, hc_ready, y_added, y_zero = (st.sem(n) for n in (
            "b_done", "c_done", "decay_ready", "inp_ready", "scanned", "hc_ready", "y_added", "y_zero"))
        N = BATCH * NSTATE
        with nc.Block() as block:

            @block.sync
            def _(sp):
                for i, name in enumerate("BC"):
                    sp.dma_start(wrow[:, i, :], d["L0_attn_b_W" + name]).then_inc(loaded, 16)
                    sp.dma_start(brow[:, i, :], row_of(d["L0_attn_b_b" + name], D)).then_inc(loaded, 16)
                sp.dma_start(a[:], d["L0_attn_b_A_log"]).then_inc(loaded, 16)

            @block.tensor
            def _(pe):
                pe.wait_ge(repeated, 2)

                def project(i, k, bank, sem):
                    for c in range(2):
                        tok = (k // NSTATE) * SEQ + c * 512
                        mm = pe.matmul(banks[:, bank + c, :], wrep[:, i, k % NSTATE, :], xT[:, tok:tok + 512],
                                       start=True, stop=True)
                    mm.then_inc(sem, 1)

                for k in range(N):
                    if k >= 2:
                        pe.wait_ge(inp_ready, k - 1)
                    project(0, k, 2 * (k % 2), b_done)
                    if k >= 2:
                        pe.wait_ge(hc_ready, k - 1)
                    project(1, k, 4 + 2 * (k % 2), c_done)

            @block.scalar
            def _(act):
                act.wait_ge(loaded, 80)
                act.activation(a[:], a[:], ACT.Exp).then_inc(a_exp, 1)
                act.wait_ge(a_ready, 1)
                for k in range(N):
                    if k >= 2:
                        act.wait_ge(scanned, k - 1)
                    tok = (k // NSTATE) * SEQ
                    act.activation(decay[:, k % 2, :], dt[:, tok:tok + SEQ], ACT.Exp,
                                   scale=a[:, k % NSTATE:k % NSTATE + 1]).then_inc(decay_ready, 1)

            @block.vector
            def _(dve):
                dve.wait_ge(loaded, 80)
                for i in range(2):
                    src = wrow[:, i, :].rearrange("p (n o) -> p n o", o=1).to_broadcast([D, NSTATE, D])
                    dve.tensor_copy(wrep[:, i, :, :], src).then_inc(repeated, 1)
                dve.wait_ge(a_exp, 1)
                dve.tensor_scalar(a[:], a[:], -1.0, None, ALU.mult).then_inc(a_ready, 1)

                def feed(k):
                    tok, n = (k // NSTATE) * SEQ, k % NSTATE
                    dve.wait_ge(b_done, k + 1)
                    bank = 2 * (k % 2)
                    if k >= 2:
                        dve.wait_ge(scanned, k - 1)
                    dve.scalar_tensor_tensor(inp[:, k % 2, :], banks[:, bank:bank + 2, :].rearrange("p b c -> p (b c)"),
                                             brow[:, 0, n:n + 1], dtx[:, tok:tok + SEQ], ALU.add, ALU.mult).then_inc(inp_ready, 1)

                def scan(k):
                    dve.wait_ge(decay_ready, k + 1)
                    dve.wait_ge(inp_ready, k + 1)
                    if k >= 2:
                        dve.wait_ge(hc_ready, k - 1)
                    dve.tensor_tensor_scan(h[:, k % 2, :], decay[:, k % 2, :], inp[:, k % 2, :], 0.0, ALU.mult,
                                           ALU.add).then_inc(scanned, 1)

                def weigh(k):
                    n = k % NSTATE
                    dve.wait_ge(c_done, k + 1)
                    dve.wait_ge(scanned, k + 1)
                    if k >= 2:
                        dve.wait_ge(y_added, k - 1)
                    bank = 4 + 2 * (k % 2)
                    dve.scalar_tensor_tensor(hc[:, k % 2, :], banks[:, bank:bank + 2, :].rearrange("p b c -> p (b c)"),
                                             brow[:, 1, n:n + 1], h[:, k % 2, :], ALU.add, ALU.mult).then_inc(hc_ready, 1)

                feed(0)
                for k in range(N):
                    scan(k)
                    if k + 1 < N:
                        feed(k + 1)
                    weigh(k)

            @block.gpsimd
            def _(pool):
                pool.memset(y[:], 0.0).then_inc(y_zero, 1)
                pool.wait_ge(y_zero, 1)
                for k in range(N):
                    tok = (k // NSTATE) * SEQ
                    pool.wait_ge(hc_ready, k + 1)
                    if k >= 1:
                        pool.wait_ge(y_added, k)
                    pool.tensor_tensor(y[:, tok:tok + SEQ], y[:, tok:tok + SEQ], hc[:, k % 2, :], ALU.add).then_inc(y_added, 1)


def attn_b_finish(nc, x, d, banks, z, y):
    with stage(nc, "bf") as st:
        w = st.sb("w", [D, D])
        b = st.sb("b", [P, D])
        loaded, gated, biased, projected, added = (st.sem(n) for n in ("loaded", "gated", "biased", "projected", "added"))
        with nc.Block() as block:

            @block.sync
            def _(sp):
                sp.dma_start(w[:], d["L0_attn_b_Wout"]).then_inc(loaded, 16)
                sp.dma_start(b[:], row_of(d["L0_attn_b_bout"], P)).then_inc(loaded, 16)

            @block.tensor
            def _(pe):
                pe.wait_ge(loaded, 32)
                for c in range(NCH):
                    pe.wait_ge(gated, c + 1)
                    for j in range(4):
                        t = 4 * c + j
                        mm = pe.matmul(banks[:, c, j * P:(j + 1) * P], y[:, t * P:(t + 1) * P], w[:], start=True, stop=True)
                    mm.then_inc(projected, 1)

            @block.vector
            def _(dve):
                for c in range(NCH):
                    cs = slice(c * 512, (c + 1) * 512)
                    dve.tensor_tensor(y[:, cs], y[:, cs], z[:, cs], ALU.mult).then_inc(gated, 1)
                dve.wait_ge(loaded, 32)
                bv = b[:].rearrange("p (o n) -> p o n", o=1).to_broadcast([P, NT, D])
                dve.tensor_tensor(x[:], x[:], bv, ALU.add).then_inc(biased, 1)
                dve.wait_ge(biased, 1)
                for c in range(NCH):
                    dve.wait_ge(projected, c + 1)
                    src = banks[:, c, :].rearrange("p (t n) -> p t n", t=4)
                    dve.tensor_tensor(x[:, 4 * c:4 * c + 4, :], x[:, 4 * c:4 * c + 4, :], src, ALU.add).then_inc(added, 1)


DF_HD = 8
DF_V = 2 * DF_HD
LAMBDA_INIT = 0.8
DF_STACK = len(Q_PARTS) * DF_HD


def diff(nc, x, d, cst):
    G = BATCH * HEADS
    with stage(nc, "df") as st:
        qh = st.dram("qh", (2 * G, DF_STACK, SEQ), BF16)
        kh = st.dram("kh", (2 * G, DF_STACK, SEQ), BF16)
        ctx = st.sb("ctx", [P, QT, G, DF_V])
        vh = st.sb("vh", [P, QT, G, DF_V])
        neglam = st.sb("neglam", [P, G])
        diff_prepare(nc, x, d, cst, qh, kh, vh, neglam)
        diff_heads(nc, cst, d, ctx, vh, qh, kh, neglam)
        diff_finish(nc, x, d, cst, ctx)


def diff_prepare(nc, x, d, cst, qh, kh, vh, neglam):
    ident = cst["ident"]
    WD = HEADS * DF_V
    with stage(nc, "dp") as st:
        banks = st.ps("banks", [P, 8, 512])
        w = st.sb("w", [D, 3, WD])
        lamrow = st.sb("lamrow", [P, 4, HEADS * DF_HD])
        lamprod = st.sb("lamprod", [P, 2, HEADS * DF_HD])
        lam = st.sb("lam", [P, 2, HEADS])
        xT = st.sb("xT", [D, TOK])
        xn = st.sb("xn", [P, NT, D])
        layer_norm(nc, st, x, xn, 1e-5)
        transpose_all(nc, st, xn, xT, ident, banks[:, 0:2, :])
        val = st.sb("val", [P, 2, TOK])
        rest = st.sb("rest", [P, 2, TOK])
        parts = st.sb("parts", [P, 2, 3, TOK], BF16)
        loaded, projected, evac = st.sem("loaded"), st.sem("projected"), st.sem("evac")
        high, less, mid, split = (st.sem(n) for n in ("high", "less", "mid", "split"))
        v_mm, v_ready, stored = st.sem("v_mm"), st.sem("v_ready"), [st.sem(f"stored{i}") for i in range(2)]
        lam_step, lam_exp = st.sem("lam_step"), st.sem("lam_exp")
        UNITS, NW = 4, BATCH * 6
        with nc.Block() as block:

            @block.sync
            def _(sp):
                for i, name in enumerate("qkv"):
                    sp.dma_start(w[:, i, :], d["L1_attn_a_W" + name]).then_inc(loaded, 16)
                for i, name in enumerate(("q1", "k1", "q2", "k2")):
                    src = d["L1_attn_a_lambda_" + name].rearrange("(o h) e -> o (h e)", o=1).to_broadcast([P, HEADS * DF_HD])
                    sp.dma_start(lamrow[:, i, :], src).then_inc(loaded, 16)
                for r in range(UNITS):
                    sp.wait_ge(split, r + 1)
                    dst_all, order = ((qh, Q_PARTS), (kh, K_PARTS))[r // 2]
                    for b in range(BATCH):
                        g0 = b * HEADS + r % 2 * 8
                        for j, part in enumerate(order):
                            dst = dst_all[2 * g0:2 * g0 + 16, j * DF_HD:(j + 1) * DF_HD, :]
                            sp.dma_start(dst, parts[:, r % 2, part, b * SEQ:(b + 1) * SEQ]).then_inc(stored[r % 2], 16)
                for i in range(2):
                    sp.wait_ge(stored[i], 16 * NW * 2)

            @block.tensor
            def _(pe):
                pe.wait_ge(loaded, 7 * 16)
                for r in range(UNITS):
                    for c in range(NCH):
                        if r >= 1 or c >= 2:
                            pe.wait_ge(evac, NCH * r + c - 1)
                        lhs = w[:, r // 2, r % 2 * P:(r % 2 + 1) * P]
                        pe.matmul(banks[:, c % 2, :], lhs, xT[:, c * 512:(c + 1) * 512], start=True,
                                  stop=True).then_inc(projected, 1)
                for t in range(NT // 2):
                    if t >= 2:
                        pe.wait_ge(v_ready, t - 1)
                    for j in range(2):
                        mm = pe.matmul(banks[:, 2 + t % 2, j * WD:(j + 1) * WD], xT[:, (2 * t + j) * P:(2 * t + j + 1) * P],
                                       w[:, 2, :], start=True, stop=True)
                    mm.then_inc(v_mm, 1)

            @block.scalar
            def _(act):
                act.wait_ge(lam_step, 3)
                act.activation(lam[:], lam[:], ACT.Exp).then_inc(lam_exp, 1)
                for r in range(UNITS):
                    act.wait_ge(evac, NCH * (r + 1))
                    if r >= 2:
                        act.wait_ge(stored[r % 2], 16 * NW)
                    act.activation(parts[:, r % 2, 0, :], val[:, r % 2, :], ACT.Copy).then_inc(high, 1)
                    act.wait_ge(less, r + 1)
                    act.activation(parts[:, r % 2, 1, :], rest[:, r % 2, :], ACT.Copy).then_inc(mid, 1)

            @block.vector
            def _(dve):
                dve.wait_ge(loaded, 7 * 16)
                for i in range(2):
                    dve.tensor_tensor(lamprod[:, i, :], lamrow[:, 2 * i, :], lamrow[:, 2 * i + 1, :], ALU.mult).then_inc(lam_step, 1)
                dve.wait_ge(lam_step, 2)
                dve.tensor_reduce(lam[:], lamprod[:].rearrange("p i (h e) -> p i h e", e=DF_HD), AX.X, ALU.add).then_inc(lam_step, 1)
                for r in range(UNITS):
                    for c in range(NCH):
                        dve.wait_ge(projected, NCH * r + c + 1)
                        if r >= 2 and c == 0:
                            dve.wait_ge(split, r - 1)
                        factor = 1.0 / math.sqrt(DF_HD) if r < 2 else 1.0
                        dve.tensor_scalar(val[:, r % 2, c * 512:(c + 1) * 512], banks[:, c % 2, :], factor, None,
                                          ALU.mult).then_inc(evac, 1)
                    dve.wait_ge(high, r + 1)
                    dve.tensor_tensor(rest[:, r % 2, :], val[:, r % 2, :], parts[:, r % 2, 0, :], ALU.subtract).then_inc(less, 1)
                    dve.wait_ge(mid, r + 1)
                    dve.tensor_tensor(parts[:, r % 2, 2, :], rest[:, r % 2, :], parts[:, r % 2, 1, :], ALU.subtract).then_inc(split, 1)
                for t in range(NT // 2):
                    dve.wait_ge(v_mm, t + 1)
                    b, k0 = 2 * t // QT, 2 * t % QT
                    dst = vh[:, k0:k0 + 2, b * HEADS:(b + 1) * HEADS, :].rearrange("p t g e -> p t (g e)")
                    dve.tensor_copy(dst, banks[:, 2 + t % 2, :].rearrange("p (t n) -> p t n", t=2)).then_inc(v_ready, 1)
                dve.wait_ge(lam_exp, 1)
                for b in range(BATCH):
                    dve.tensor_tensor(neglam[:, b * HEADS:(b + 1) * HEADS], lam[:, 1, :], lam[:, 0, :], ALU.subtract).then_inc(lam_step, 1)
                dve.wait_ge(lam_step, 5)
                dve.tensor_scalar(neglam[:], neglam[:], LAMBDA_INIT, None, ALU.subtract).then_inc(lam_step, 1)


def diff_heads(nc, cst, d, ctx, vh, qh, kh, neglam):
    ident = cst["ident"]
    G = BATCH * HEADS
    NSTEP = 2 * QT
    M2 = 64
    with stage(nc, "dh") as st:
        q_s = st.sb("q", [P, 2, SEQ], BF16)
        k_s = st.sb("k", [P, 2, SEQ], BF16)
        mask = st.sb("mask", [P, P])
        maskb = st.sb("maskb", [P, P], BF16)
        identb = st.sb("identb", [P, P], BF16)
        prob = st.sb("prob", [P, 2, 2, SEQ])
        both = st.sb("both", [P, 2, SEQ])
        probT = st.sb("probT", [P, 2, QT, P])
        v_s = st.sb("v", [P, 2, QT, VCOLS])
        outT = st.sb("outT", [P, 2, P])
        gather = st.sb("gather", [P, DF_V])
        negmax = st.sb("negmax", [P, 2, 2])
        rowsum = st.sb("rowsum", [P, 2, QT, 2])
        rinv = st.sb("rinv", [P, 2, QT, 2])
        coef = st.sb("coef", [P, 2])
        scores = st.ps("scores", [P, 2, 2, 512])
        turned = st.ps("turned", [P, QT, P])
        outp = st.ps("outp", [P, 512])
        ctxp = st.ps("ctxp", [P, QT, DF_V])
        mask_loaded, cast = st.sem("mask_loaded"), st.sem("cast")
        ops_loaded = [st.sem(f"ops_loaded{i}") for i in range(2)]
        scored = [st.sem(f"scored{m}") for m in range(2)]
        max_ready = [st.sem(f"max_ready{m}") for m in range(2)]
        probs_ready = [st.sem(f"probs_ready{m}") for m in range(2)]
        inverted, coef_ready, combined = st.sem("inverted"), st.sem("coef_ready"), st.sem("combined")
        probs_turned, turned_kept = st.sem("probs_turned"), st.sem("turned_kept")
        v_clear, v_placed = st.sem("v_clear"), st.sem("v_placed")
        pv_done, out_kept, gathered, ctx_kept = (st.sem(n) for n in ("pv_done", "out_kept", "gathered", "ctx_kept"))

        def passes(eng, run):
            run(0, True, False)
            with eng.Fori(1, G // 2 - 1) as i:
                run(i, False, False)
            run(G // 2 - 1, False, True)

        with nc.Block() as block:

            @block.sync
            def _(sp):
                def load_head(g, par):
                    for m in range(2):
                        rows = slice(m * M2, m * M2 + DF_STACK)
                        sp.dma_start(q_s[rows, par, :], qh[2 * g + m]).then_inc(ops_loaded[par], 16)
                        sp.dma_start(k_s[rows, par, :], kh[2 * g + m]).then_inc(ops_loaded[par], 16)

                def run(i, first, last):
                    for par in range(1 if last else 2):
                        g1 = 2 * i + par + 1
                        since(sp, scored[1], QT * (g1 - 1))
                        load_head(g1, 1 - par)

                sp.dma_start(mask[:], d["causal"]).then_inc(mask_loaded, 16)
                sp.dma_start(gather[:], cst["gather16"]).then_inc(mask_loaded, 16)
                load_head(0, 0)
                passes(sp, run)

            @block.tensor
            def _(pe):
                def score(n, s, first):
                    par, t = s // QT, s % QT
                    width = (t + 1) * P
                    for m in range(2):
                        if not (first and s < 1):
                            pe.wait_ge(probs_ready[m], n)
                        rows = slice(m * M2, m * M2 + DF_STACK)
                        for bank in range((width + 511) // 512):
                            b0, b1 = bank * 512, min(width, bank * 512 + 512)
                            diag = b1 == width
                            mm = pe.matmul(scores[:, m, bank, 0:b1 - b0], q_s[rows, par, t * P:(t + 1) * P],
                                           k_s[rows, par, b0:b1], start=True, stop=not diag, skip_group_check=True)
                            if diag:
                                mm = pe.matmul(scores[:, m, bank, b1 - P - b0:b1 - b0], identb[:], maskb[:],
                                               start=False, stop=True, skip_group_check=True)
                        mm.then_inc(scored[m], 1)

                def turn(n, s, g):
                    t = s % QT
                    pe.wait_ge(combined, n + 1)
                    since(pe, turned_kept, n)
                    for kt in range(t + 1):
                        mm = pe.transpose(turned[:, kt, :], both[:, s % 2, kt * P:(kt + 1) * P], ident[:])
                    mm.then_inc(probs_turned, 1)

                def times_v(n, s, g):
                    t = s % QT
                    if t == 0:
                        pe.wait_ge(v_placed, g + 1)
                    pe.wait_ge(turned_kept, n + 1)
                    since(pe, out_kept, n)
                    for kt in range(t + 1):
                        r = kt % 4 * 32
                        mm = pe.matmul(outp[r:r + VCOLS, 0:P], v_s[:, s // QT, kt, :], probT[:, s % 2, kt, :],
                                       start=kt < 4, stop=kt + 4 > t, tile_position=(0, r), skip_group_check=True)
                    mm.then_inc(pv_done, 1)

                def add_parts(n, s, g):
                    t = s % QT
                    rows = slice(0, 32 * min(t + 1, 4))
                    pe.wait_ge(out_kept, n + 1)
                    if t == 0:
                        since(pe, ctx_kept, g)
                    pe.matmul(ctxp[:, t, :], outT[rows, s % 2, :], gather[rows, :], start=True,
                              stop=True).then_inc(gathered, 1)

                def run(i, first, last):
                    for s in range(NSTEP):
                        n, par, t = NSTEP * i + s, s // QT, s % QT
                        if t == 0:
                            pe.wait_ge(ops_loaded[par], 64 * (i + 1))
                        score(n, s, first)
                        if not (first and s < 2):
                            turn(*back(i, s, 2, NSTEP))
                        if not (first and s < 3):
                            times_v(*back(i, s, 3, NSTEP))
                        if not (first and s < 4):
                            add_parts(*back(i, s, 4, NSTEP))

                pe.wait_ge(cast, 2)
                passes(pe, run)
                for k in range(4):
                    if k < 2:
                        turn(*back(G // 2, k, 2, NSTEP))
                    if k < 3:
                        times_v(*back(G // 2, k, 3, NSTEP))
                    add_parts(*back(G // 2, k, 4, NSTEP))

            @block.vector
            def _(dve):
                dve.wait_ge(mask_loaded, 32)
                dve.tensor_copy(maskb[:], mask[:]).then_inc(cast, 1)
                dve.tensor_copy(identb[:], ident[:]).then_inc(cast, 1)

                def invert(n, s, g):
                    dve.wait_ge(probs_ready[1], n + 1)
                    if s % QT == 0:
                        since(dve, ctx_kept, g - 1)
                    dve.reciprocal(rinv[:, s // QT, s % QT, :], rowsum[:, s // QT, s % QT, :]).then_inc(inverted, 1)

                def take_coef(n, s, g):
                    dve.wait_ge(inverted, n + 1)
                    since(dve, combined, n - 1)
                    dve.scalar_tensor_tensor(coef[:, s % 2:s % 2 + 1], rinv[:, s // QT, s % QT, 1:2],
                                             rowsum[:, s // QT, s % QT, 0:1], neglam[:, bass.ts(g, 1)],
                                             ALU.mult, ALU.mult).then_inc(coef_ready, 1)

                def combine(n, s, g):
                    width = (s % QT + 1) * P
                    dve.wait_ge(coef_ready, n + 1)
                    since(dve, probs_turned, n - 1)
                    dve.scalar_tensor_tensor(both[:, s % 2, 0:width], prob[:, s % 2, 1, 0:width], coef[:, s % 2:s % 2 + 1],
                                             prob[:, s % 2, 0, 0:width], ALU.mult, ALU.add).then_inc(combined, 1)

                def keep_out(n, s, g):
                    rows = slice(0, 32 * min(s % QT + 1, 4))
                    dve.wait_ge(pv_done, n + 1)
                    since(dve, gathered, n - 1)
                    dve.tensor_copy(outT[rows, s % 2, :], outp[rows, 0:P]).then_inc(out_kept, 1)

                def keep_ctx(g, par):
                    dve.wait_ge(gathered, QT * (g + 1))
                    over = rinv[:, par, :, 0:1].to_broadcast([P, QT, DF_V])
                    dve.tensor_tensor(ctx[:, :, g, :], ctxp[:], over, ALU.mult).then_inc(ctx_kept, 1)

                def run(i, first, last):
                    for s in range(NSTEP):
                        n, width = NSTEP * i + s, (s % QT + 1) * P

                        def take_max(m):
                            dve.wait_ge(scored[m], n + 1)
                            row = scores[:, m, :, :].rearrange("p b c -> p (b c)")[:, 0:width]
                            dve.tensor_reduce(negmax[:, s % 2, m:m + 1], row, AX.X, ALU.max, negate=True).then_inc(max_ready[m], 1)

                        if not (first and s < 4):
                            keep_out(*back(i, s, 4, NSTEP))
                        if s % QT == 4 and not (first and s < QT):
                            keep_ctx(2 * i + s // QT - 1, 1 - s // QT)
                        take_max(0)
                        if not (first and s < 1):
                            invert(*back(i, s, 1, NSTEP))
                        take_max(1)
                        if not (first and s < 1):
                            take_coef(*back(i, s, 1, NSTEP))
                            combine(*back(i, s, 1, NSTEP))

                passes(dve, run)
                for k in range(4):
                    keep_out(*back(G // 2, k, 4, NSTEP))
                    if k == 0:
                        invert(*back(G // 2, 0, 1, NSTEP))
                        take_coef(*back(G // 2, 0, 1, NSTEP))
                        combine(*back(G // 2, 0, 1, NSTEP))
                keep_ctx(G - 1, 1)

            @block.scalar
            def _(act):
                def keep_turned(n, s, g):
                    t = s % QT
                    act.wait_ge(probs_turned, n + 1)
                    since(act, pv_done, n - 1)
                    act.activation(probT[:, s % 2, 0:t + 1, :], turned[:, 0:t + 1, :], ACT.Copy).then_inc(turned_kept, 1)

                def run(i, first, last):
                    for s in range(NSTEP):
                        n, width = NSTEP * i + s, (s % QT + 1) * P
                        if not (first and s < 3):
                            keep_turned(*back(i, s, 3, NSTEP))
                        for m in range(2):
                            act.wait_ge(max_ready[m], n + 1)
                            if m == 0 and not (first and s < 2):
                                act.wait_ge(combined, n - 1)
                            if m == 0 and not (first and s < 4):
                                act.wait_ge(coef_ready, n - 3)
                            row = scores[:, m, :, :].rearrange("p b c -> p (b c)")[:, 0:width]
                            act.activation(prob[:, s % 2, m, 0:width], row, ACT.Exp, bias=negmax[:, s % 2, m:m + 1],
                                           accum_out=rowsum[:, s // QT, s % QT, m:m + 1]).then_inc(probs_ready[m], 1)

                passes(act, run)
                for k in range(3):
                    keep_turned(*back(G // 2, k, 3, NSTEP))

            @block.gpsimd
            def _(pool):
                def run(i, first, last):
                    for par in range(2):
                        place_v(pool, v_s, vh, DF_V, v_placed, pv_done, 2 * i + par, par, first)

                pool.memset(v_s[:], 0.0).then_inc(v_clear, 1)
                pool.wait_ge(v_clear, 1)
                passes(pool, run)


def diff_finish(nc, x, d, cst, ctx):
    ident = cst["ident"]
    G = BATCH * HEADS
    with stage(nc, "dz") as st:
        sq = st.sb("sq", [P, QT, G, DF_V])
        ms = st.sb("ms", [P, QT, G])
        srow = st.sb("srow", [P, DF_V])
        wo = st.sb("wo", [P, 2, D])
        oT = st.sb("oT", [P, 2, 2, P])
        banks = st.ps("banks", [P, 4, 512])
        loaded, squared, summed, meaned, rooted, inverted, s_ready, scaled, weighted = (st.sem(n) for n in (
            "loaded", "squared", "summed", "meaned", "rooted", "inverted", "s_ready", "scaled", "weighted"))
        turned, kept, projected, added = (st.sem(n) for n in ("turned", "kept", "projected", "added"))
        with nc.Block() as block:

            @block.sync
            def _(sp):
                sp.dma_start(wo[:], d["L1_attn_a_Wo"].rearrange("(c p) n -> p c n", p=P)).then_inc(loaded, 16)
                sp.dma_start(srow[:], row_of(d["L1_attn_a_rms_scale"], P)).then_inc(loaded, 16)

            @block.scalar
            def _(act):
                act.activation(sq[:], ctx[:], ACT.Square).then_inc(squared, 1)
                act.wait_ge(meaned, 1)
                act.activation(ms[:], ms[:], ACT.Sqrt).then_inc(rooted, 1)
                for t in range(NT):
                    act.wait_ge(turned, t + 1)
                    if t >= 2:
                        act.wait_ge(projected, t - 1)
                    act.activation(oT[:, t % 2, :, :], banks[:, t % 2, 0:2 * P].rearrange("p (c n) -> p c n", c=2),
                                   ACT.Copy).then_inc(kept, 1)

            @block.vector
            def _(dve):
                dve.wait_ge(loaded, 32)
                dve.tensor_scalar(srow[:], srow[:], 1.0 - LAMBDA_INIT, None, ALU.mult).then_inc(s_ready, 1)
                dve.wait_ge(squared, 1)
                dve.tensor_reduce(ms[:], sq[:], AX.X, ALU.add).then_inc(summed, 1)
                dve.wait_ge(summed, 1)
                dve.tensor_scalar(ms[:], ms[:], 1.0 / DF_V, 1e-5, ALU.mult, ALU.add).then_inc(meaned, 1)
                dve.wait_ge(rooted, 1)
                dve.reciprocal(ms[:], ms[:]).then_inc(inverted, 1)
                dve.wait_ge(inverted, 1)
                dve.wait_ge(s_ready, 1)
                for qt in range(QT):
                    rb = ms[:, qt, :].rearrange("p (g o) -> p g o", o=1).to_broadcast([P, G, DF_V])
                    dve.tensor_tensor(ctx[:, qt], ctx[:, qt], rb, ALU.mult).then_inc(scaled, 1)
                for qt in range(QT):
                    sb_ = srow[:].rearrange("p (o e) -> p o e", o=1).to_broadcast([P, G, DF_V])
                    dve.wait_ge(scaled, qt + 1)
                    dve.tensor_tensor(ctx[:, qt], ctx[:, qt], sb_, ALU.mult).then_inc(weighted, 1)
                for t in range(NT):
                    dve.wait_ge(projected, t + 1)
                    dve.tensor_tensor(x[:, t, :], x[:, t, :], banks[:, 2 + t % 2, 0:D], ALU.add).then_inc(added, 1)

            @block.tensor
            def _(pe):
                pe.wait_ge(weighted, QT)
                pe.wait_ge(loaded, 32)
                for t in range(NT):
                    b, qt = t // QT, t % QT
                    if t >= 2:
                        pe.wait_ge(kept, t - 1)
                    src = ctx[:, qt, b * HEADS:(b + 1) * HEADS, :].rearrange("p g e -> p (g e)")
                    for c in range(2):
                        mm = pe.transpose(banks[:, t % 2, c * P:(c + 1) * P], src[:, c * P:(c + 1) * P], ident[:])
                    mm.then_inc(turned, 1)
                    pe.wait_ge(kept, t + 1)
                    if t >= 2:
                        pe.wait_ge(added, t - 1)
                    for c in range(2):
                        mm = pe.matmul(banks[:, 2 + t % 2, 0:D], oT[:, t % 2, c, :], wo[:, c, :], start=c == 0, stop=c == 1)
                    mm.then_inc(projected, 1)


SW_HID = 384
SW_CUT = SW_HID // P
DEQUANT = 1.0 / 127.0


def swiglu(nc, x, d, cst, tag):
    ident = cst["ident"]
    with stage(nc, tag) as st:
        xn = st.sb("xn", [P, NT, D])
        xT = st.sb("xT", [D, TOK])
        wi = st.sb("wi", [P, 3, SW_HID], I32)
        w = st.sb("w", [P, 3, SW_HID])
        act_g = st.sb("act_g", [P, 2, SW_CUT, 512])
        hid = st.sb("hid", [P, 2, SW_CUT, 512])
        banks = st.ps("banks", [P, 8, 512])
        layer_norm(nc, st, x, xn, 1e-5)
        transpose_all(nc, st, xn, xT, ident, banks[:, 0:2, :])
        loaded, w_ready = st.sem("loaded"), st.sem("w_ready")
        u_done, g_done, silu_done, hid_done = (st.sem(n) for n in ("u_done", "g_done", "silu_done", "hid_done"))
        down_done, added = st.sem("down_done"), st.sem("added")
        with nc.Block() as block:

            @block.sync
            def _(sp):
                sp.dma_start(wi[:, 0, :], d["w_gateT"]).then_inc(loaded, 16)
                sp.dma_start(wi[:, 1, :], d["w_upT"]).then_inc(loaded, 16)
                sp.dma_start(wi[:, 2, :].rearrange("p (c n) -> p c n", n=D),
                             d["w_downT"].rearrange("(c p) n -> p c n", p=P)).then_inc(loaded, 16)

            @block.tensor
            def _(pe):
                def down(c):
                    pe.wait_ge(hid_done, SW_CUT * (c + 1))
                    for i in range(4):
                        for j in range(SW_CUT):
                            mm = pe.matmul(banks[:, 6 + c % 2, i * P:(i + 1) * P], hid[:, c % 2, j, i * P:(i + 1) * P],
                                           w[:, 2, j * D:(j + 1) * D], start=j == 0, stop=j == SW_CUT - 1)
                    mm.then_inc(down_done, 1)

                pe.wait_ge(w_ready, 1)
                for c in range(NCH):
                    for j in range(SW_CUT):
                        rhs = xT[:, c * 512:(c + 1) * 512]
                        if c >= 1:
                            pe.wait_ge(silu_done, SW_CUT * (c - 1) + j + 1)
                        pe.matmul(banks[:, j, :], w[:, 0, j * P:(j + 1) * P], rhs, start=True, stop=True).then_inc(g_done, 1)
                        if c >= 1:
                            pe.wait_ge(hid_done, SW_CUT * (c - 1) + j + 1)
                        pe.matmul(banks[:, 3 + j, :], w[:, 1, j * P:(j + 1) * P], rhs, start=True, stop=True).then_inc(u_done, 1)
                    if c >= 1:
                        if c >= 3:
                            pe.wait_ge(added, c - 2)
                        down(c - 1)
                pe.wait_ge(added, NCH - 2)
                down(NCH - 1)

            @block.scalar
            def _(act):
                for k in range(NCH * SW_CUT):
                    c, j = k // SW_CUT, k % SW_CUT
                    act.wait_ge(g_done, k + 1)
                    if c >= 2:
                        act.wait_ge(hid_done, k - 2 * SW_CUT + 1)
                    act.activation(act_g[:, c % 2, j, :], banks[:, j, :], ACT.Silu).then_inc(silu_done, 1)

            @block.vector
            def _(dve):
                dve.wait_ge(loaded, 48)
                dve.tensor_scalar(w[:], wi[:], DEQUANT, None, ALU.mult).then_inc(w_ready, 1)

                def add(c):
                    dve.wait_ge(down_done, c + 1)
                    y = banks[:, 6 + c % 2, :].rearrange("p (t n) -> p t n", t=4)
                    dve.tensor_tensor(x[:, 4 * c:4 * c + 4, :], x[:, 4 * c:4 * c + 4, :], y, ALU.add).then_inc(added, 1)

                for k in range(NCH * SW_CUT):
                    c, j = k // SW_CUT, k % SW_CUT
                    dve.wait_ge(u_done, k + 1)
                    dve.wait_ge(silu_done, k + 1)
                    if c >= 2:
                        dve.wait_ge(down_done, c - 1)
                    dve.tensor_tensor(hid[:, c % 2, j, :], banks[:, 3 + j, :], act_g[:, c % 2, j, :], ALU.mult).then_inc(hid_done, 1)
                    if j == SW_CUT - 1 and c >= 1:
                        add(c - 1)
                add(NCH - 1)


LN_DEPTH = 6


def linear(nc, x, d, cst):
    with stage(nc, "li") as st:
        y = st.sb("y", [P, NT, D])
        layer_norm(nc, st, x, y, 1e-5)
        with nc.Fori(0, LN_DEPTH) as layer:
            linear_layer(nc, y, d, cst, layer)
        added = st.sem("added")
        with nc.Block() as block:

            @block.vector
            def _(dve):
                dve.tensor_tensor(x[:], x[:], y[:], ALU.add).then_inc(added, 1)


def linear_layer(nc, y, d, cst, layer):
    ident = cst["ident"]
    with stage(nc, "ll") as st:
        h = st.sb("h", [P, NT, D])
        hT = st.sb("hT", [D, TOK])
        w = st.sb("w", [D, 3 * D])
        wo = st.sb("wo", [D, D])
        bo = st.sb("bo", [P, D])
        affine = st.sb("affine", [D, 2])
        qe = st.sb("qe", [D, 2, SEQ])
        q = st.sb("q", [P, 2, QT, D])
        k = st.sb("k", [P, 2, QT, D])
        vT = st.sb("vT", [D, 2, SEQ])
        qmax, qsum, qinv = st.sb("qmax", [D, 2]), st.sb("qsum", [D, 2]), st.sb("qinv", [D, 2])
        kmax, ksum = st.sb("kmax", [P, 2, QT]), st.sb("ksum", [P, 2, QT])
        mT, mw = st.sb("mT", [D, 2, D]), st.sb("mw", [D, 2, D])
        banks = st.ps("banks", [P, 8, 512])
        layer_norm(nc, st, y, h, 1e-5)
        loaded, biased = st.sem("loaded"), st.sem("biased")
        turned, hT_ready = st.sem("turned"), st.sem("hT_ready")
        q_done, q_max, q_exp, q_turned, q_kept, q_inv = (st.sem(n) for n in ("q_done", "q_max", "q_exp", "q_turned", "q_kept", "q_inv"))
        k_done, k_max, k_less, k_exp, k_sum, k_inv, k_ready = (st.sem(n) for n in (
            "k_done", "k_max", "k_less", "k_exp", "k_sum", "k_inv", "k_ready"))
        v_done, v_kept = st.sem("v_done"), st.sem("v_kept")
        m_done, m_kept, mw_done, mw_kept, out_done, added = (st.sem(n) for n in (
            "m_done", "m_kept", "mw_done", "mw_kept", "out_done", "added"))
        two = lambda ap: ap.rearrange("p b c -> p (b c)")
        with nc.Block() as block:

            @block.sync
            def _(sp):
                sp.dma_start(w[:], d["L1_attn_b_w_qkv"][layer]).then_inc(loaded, 16)
                sp.dma_start(wo[:], d["L1_attn_b_w_out"][layer]).then_inc(loaded, 16)
                sp.dma_start(bo[:], d["L1_attn_b_b_out"][bass.ts(layer, 1), :].to_broadcast([P, D])).then_inc(loaded, 16)
                sp.dma_start(affine[:, 0:1], d["L1_attn_b_gamma"][layer].rearrange("(p o) -> p o", o=1)).then_inc(loaded, 16)
                sp.dma_start(affine[:, 1:2], d["L1_attn_b_beta"][layer].rearrange("(p o) -> p o", o=1)).then_inc(loaded, 16)

            @block.tensor
            def _(pe):
                for c in range(NCH):
                    if c >= 2:
                        pe.wait_ge(hT_ready, c - 1)
                    for j in range(4):
                        mm = pe.transpose(banks[:, 6 + c % 2, j * P:(j + 1) * P], h[:, 4 * c + j, :], ident[:])
                    mm.then_inc(turned, 1)
                pe.wait_ge(loaded, 80)

                def project(b):
                    for c in range(2):
                        cs = slice(b * SEQ + c * 512, b * SEQ + (c + 1) * 512)
                        mm = pe.matmul(banks[:, c, :], w[:, 0:D], hT[:, cs], start=True, stop=True)
                    mm.then_inc(q_done, 1)
                    if b >= 1:
                        pe.wait_ge(k_less, 1)
                    for t in range(QT):
                        tok = b * SEQ + t * P
                        mm = pe.matmul(banks[:, 2 + t // 4, t % 4 * P:(t % 4 + 1) * P], hT[:, tok:tok + P], w[:, D:2 * D],
                                       start=True, stop=True)
                    mm.then_inc(k_done, 1)
                    if b >= 1:
                        pe.wait_ge(v_kept, 1)
                    for c in range(2):
                        cs = slice(b * SEQ + c * 512, b * SEQ + (c + 1) * 512)
                        mm = pe.matmul(banks[:, 4 + c, :], w[:, 2 * D:], hT[:, cs], start=True, stop=True)
                    mm.then_inc(v_done, 1)

                def turn_q(b):
                    pe.wait_ge(q_exp, b + 1)
                    if b >= 1:
                        pe.wait_ge(q_kept, 1)
                    for t in range(QT):
                        mm = pe.transpose(banks[:, 6 + t // 4, t % 4 * P:(t % 4 + 1) * P], qe[:, b, t * P:(t + 1) * P], ident[:])
                    mm.then_inc(q_turned, 1)

                def mix(b):
                    pe.wait_ge(q_kept, b + 1)
                    pe.wait_ge(k_ready, b + 1)
                    for t in range(QT):
                        mm = pe.matmul(banks[:, 4, 0:D], q[:, b, t, :], k[:, b, t, :], start=t == 0, stop=t == QT - 1)
                    mm.then_inc(m_done, 1)
                    pe.wait_ge(m_kept, b + 1)
                    pe.matmul(banks[:, 5, 0:D], mT[:, b, :], wo[:], start=True, stop=True).then_inc(mw_done, 1)
                    pe.wait_ge(mw_kept, b + 1)
                    for t in range(QT):
                        mm = pe.matmul(banks[:, 2 * b + t // 4, t % 4 * P:(t % 4 + 1) * P], vT[:, b, t * P:(t + 1) * P],
                                       mw[:, b, :], start=True, stop=True)
                    mm.then_inc(out_done, 1)

                pe.wait_ge(hT_ready, 4)
                project(0)
                turn_q(0)
                project(1)
                turn_q(1)
                pe.wait_ge(v_kept, 2)
                pe.wait_ge(k_less, 2)
                mix(0)
                mix(1)

            @block.scalar
            def _(act):
                for b in range(BATCH):
                    act.wait_ge(q_max, b + 1)
                    act.activation(qe[:, b, :], two(banks[:, 0:2, :]), ACT.Exp, bias=qmax[:, b:b + 1],
                                   accum_out=qsum[:, b:b + 1]).then_inc(q_exp, 1)
                    act.wait_ge(k_less, b + 1)
                    act.activation(k[:, b], k[:, b], ACT.Exp).then_inc(k_exp, 1)
                    act.wait_ge(v_done, b + 1)
                    act.activation(vT[:, b, :], two(banks[:, 4:6, :]), ACT.Copy).then_inc(v_kept, 1)
                    act.wait_ge(q_turned, b + 1)
                    act.activation(q[:, b].rearrange("p t n -> p (t n)"), two(banks[:, 6:8, :]), ACT.Copy).then_inc(q_kept, 1)
                for b in range(BATCH):
                    act.wait_ge(mw_done, b + 1)
                    act.activation(mw[:, b, :], banks[:, 5, 0:D], ACT.Copy).then_inc(mw_kept, 1)

            @block.vector
            def _(dve):
                dve.wait_ge(loaded, 80)
                for c in range(NCH):
                    dve.wait_ge(turned, c + 1)
                    dve.tensor_scalar(hT[:, c * 512:(c + 1) * 512], banks[:, 6 + c % 2, :], affine[:, 0:1], affine[:, 1:2],
                                      ALU.mult, ALU.add).then_inc(hT_ready, 1)
                bv = bo[:].rearrange("p (o n) -> p o n", o=1).to_broadcast([P, NT, D])
                dve.tensor_tensor(y[:], y[:], bv, ALU.add).then_inc(biased, 1)
                for b in range(BATCH):
                    dve.wait_ge(q_done, b + 1)
                    dve.tensor_reduce(qmax[:, b:b + 1], two(banks[:, 0:2, :]), AX.X, ALU.max, negate=True).then_inc(q_max, 1)
                    dve.wait_ge(k_done, b + 1)
                    kp = two(banks[:, 2:4, :]).rearrange("p (t n) -> p t n", n=D)
                    dve.tensor_reduce(kmax[:, b, :], kp, AX.X, ALU.max).then_inc(k_max, 1)
                    dve.wait_ge(k_max, b + 1)
                    kb = kmax[:, b, :].rearrange("p (t o) -> p t o", o=1).to_broadcast([P, QT, D])
                    dve.tensor_tensor(k[:, b], kp, kb, ALU.subtract).then_inc(k_less, 1)
                    dve.wait_ge(q_exp, b + 1)
                    dve.reciprocal(qinv[:, b:b + 1], qsum[:, b:b + 1]).then_inc(q_inv, 1)
                for b in range(BATCH):
                    dve.wait_ge(k_exp, b + 1)
                    dve.tensor_reduce(ksum[:, b, :], k[:, b], AX.X, ALU.add).then_inc(k_sum, 1)
                    dve.wait_ge(k_sum, b + 1)
                    dve.reciprocal(ksum[:, b, :], ksum[:, b, :]).then_inc(k_inv, 1)
                    dve.wait_ge(k_inv, b + 1)
                    kb = ksum[:, b, :].rearrange("p (t o) -> p t o", o=1).to_broadcast([P, QT, D])
                    dve.tensor_tensor(k[:, b], k[:, b], kb, ALU.mult).then_inc(k_ready, 1)
                for b in range(BATCH):
                    dve.wait_ge(m_done, b + 1)
                    dve.wait_ge(q_inv, b + 1)
                    dve.tensor_scalar(mT[:, b, :], banks[:, 4, 0:D], qinv[:, b:b + 1], None, ALU.mult).then_inc(m_kept, 1)
                    dve.wait_ge(out_done, b + 1)
                    dve.wait_ge(biased, 1)
                    out = two(banks[:, 2 * b:2 * b + 2, :]).rearrange("p (t n) -> p t n", n=D)
                    ys = y[:, b * QT:(b + 1) * QT, :]
                    dve.tensor_tensor(ys, ys, out, ALU.add).then_inc(added, 1)


STAGES = ("attn_a", "ffn0", "attn_b", "ffn1", "diff", "swiglu0", "linear", "swiglu1")


def build_program(nc, d, stages=STAGES):
    with ExitStack() as stack:
        x = stack.enter_context(nc.sbuf_tensor("residual", [P, NT, D], F32))
        ident = stack.enter_context(nc.sbuf_tensor("ident_s", [P, P], F32))
        shift = stack.enter_context(nc.sbuf_tensor("shift_s", [P, 2, P], F32))
        loaded = stack.enter_context(nc.semaphore("stream_loaded"))
        out_stored = stack.enter_context(nc.semaphore("out_stored"))
        cst = {"ident": ident, "shift": shift, "mask_c": d["mask_c"], "mask_p": d["mask_p"],
               "gather8": d["gather8"], "gather16": d["gather16"]}
        with nc.Block() as block:

            @block.sync
            def _(sp):
                for b in range(BATCH):
                    src = d["x_in"][b * SEQ:(b + 1) * SEQ, :].rearrange("(t p) c -> p t c", p=P)
                    sp.dma_start(x[:, b * QT:(b + 1) * QT, :], src).then_inc(loaded, 16)
                sp.dma_start(ident[:], d["ident"]).then_inc(loaded, 16)
                sp.dma_start(shift[:], d["shift"]).then_inc(loaded, 16)
                sp.wait_ge(loaded, 64)
        for s in stages:
            if s == "attn_a":
                attn_a(nc, x, d, cst)
            if s in ("ffn0", "ffn1"):
                ffn(nc, x, d, cst, s)
            if s == "attn_b":
                attn_b(nc, x, d, cst)
            if s == "diff":
                diff(nc, x, d, cst)
            if s in ("swiglu0", "swiglu1"):
                swiglu(nc, x, d, cst, s)
            if s == "linear":
                linear(nc, x, d, cst)
        with nc.Block() as block:

            @block.sync
            def _(sp):
                sp.dma_start(d["out"].rearrange("(t p) c -> p t c", p=P), x[:]).then_inc(out_stored, 16)
                sp.wait_ge(out_stored, 16)


def layout(inputs):
    a = {k: np.ascontiguousarray(v) for k, v in inputs.items()}
    a["x_in"] = a.pop("L0_attn_a_hidden_states").reshape(TOK, D)
    a["relT"] = np.ascontiguousarray(a.pop("L0_attn_a_rel_embeddings").T)
    a["ident"] = np.eye(P, dtype=np.float32)
    a.update(attn_a_constants())
    a.update(ffn_constants())
    a["causal"] = np.where(np.arange(P)[None, :] <= np.arange(P)[:, None], 0.0, NEG).astype(np.float32)
    for name in ("gate", "up", "down"):
        a[f"w_{name}T"] = np.ascontiguousarray(a.pop(f"L1_ffn_w_{name}").T)
    return a


def kernel(**inputs):
    import concourse.bacc as _bacc
    from concourse.bass_utils import run_bass_kernel_spmd as _run

    nc = _bacc.Bacc("TRN2", target_bir_lowering=False, num_devices=1)
    arrays, d = {}, {}
    for name, a in layout({k: np.asarray(v) for k, v in inputs.items()}).items():
        if name == "L0_attn_a_attention_mask":
            continue
        arrays[f"in_{name}"] = a
        d[name] = nc.dram_tensor(f"in_{name}", a.shape, mybir.dt.from_np(a.dtype), kind="ExternalInput").ap()
    d["out"] = nc.dram_tensor("out_0", (TOK, D), F32, kind="ExternalOutput").ap()
    build_program(nc, d)
    r = _run(nc, [arrays], core_ids=[0])
    return r.results[0]["out_0"].reshape(BATCH, SEQ, D)
```

```python
import math
from contextlib import ExitStack, contextmanager

import numpy as np

import concourse.bass as bass
from concourse import mybir

F32 = mybir.dt.float32
BF16 = mybir.dt.bfloat16
I32 = mybir.dt.int32
ALU = mybir.AluOpType
ACT = mybir.ActivationFunctionType
AX = mybir.AxisListType

P = 128
D = 128
TOK = 2048
NT = TOK // P
NCH = TOK // 512


class Stage:

    def __init__(self, nc, tag):
        self.nc, self.tag, self.stack, self.sems = nc, tag, ExitStack(), []

    def sb(self, name, shape, dt=F32):
        return self.stack.enter_context(self.nc.sbuf_tensor(f"{self.tag}_{name}", shape, dt))

    def ps(self, name, shape, dt=F32):
        return self.stack.enter_context(self.nc.psum_tensor(f"{self.tag}_{name}", shape, dt))

    def sem(self, name):
        s = self.nc.alloc_semaphore(name=f"{self.tag}_{name}")
        self.sems.append(s)
        return s

    def dram(self, name, shape, dt=F32):
        return self.nc.dram_tensor(f"{self.tag}_{name}", shape, dt).ap()


@contextmanager
def stage(nc, tag):
    st = Stage(nc, tag)
    yield st
    nc.clear_and_free_semaphores(st.sems)
    nc.all_engine_barrier()
    st.stack.close()


GP_TILES = (3, 7, 11, 15)


class Norm:

    def __init__(self, st, x, out, eps, tag=""):
        self.x, self.out, self.eps = x, out, eps
        self.stats = st.sb("stats" + tag, [P, NT, 6])
        self.mean, self.diff = st.sb("mean" + tag, [P, NT]), st.sb("diff" + tag, [P, NT])
        self.ssq, self.rstd = st.sb("ssq" + tag, [P, NT]), st.sb("rstd" + tag, [P, NT])
        self.stats_done, self.moments = st.sem("stats_done" + tag), st.sem("moments" + tag)
        self.std_ready, self.rstd_ready = st.sem("std_ready" + tag), st.sem("rstd_ready" + tag)
        self.normed_v, self.normed_p = st.sem("normed_v" + tag), st.sem("normed_p" + tag)

    def apply(self, eng, t, normed):
        eng.tensor_scalar(self.out[:, t, :], self.x[:, t, :], self.mean[:, t:t + 1], self.rstd[:, t:t + 1],
                          ALU.subtract, ALU.mult).then_inc(normed, 1)

    def vector(self, dve):
        stats, mean, diff, ssq, moments = self.stats, self.mean, self.diff, self.ssq, self.moments
        for t in range(NT):
            dve.bn_stats(stats[:, t, :], self.x[:, t, :]).then_inc(self.stats_done, 1)
        dve.wait_ge(self.stats_done, NT)
        dve.tensor_tensor(mean[:], stats[:, :, 1], stats[:, :, 4], ALU.add).then_inc(moments, 1)
        dve.tensor_tensor(diff[:], stats[:, :, 1], stats[:, :, 4], ALU.subtract).then_inc(moments, 1)
        dve.tensor_tensor(ssq[:], stats[:, :, 2], stats[:, :, 5], ALU.add).then_inc(moments, 1)
        dve.wait_ge(moments, 3)
        dve.tensor_scalar(mean[:], mean[:], 0.5, None, ALU.mult).then_inc(moments, 1)
        dve.tensor_tensor(diff[:], diff[:], diff[:], ALU.mult).then_inc(moments, 1)
        dve.tensor_scalar(ssq[:], ssq[:], 1.0 / D, self.eps, ALU.mult, ALU.add).then_inc(moments, 1)
        dve.wait_ge(moments, 6)
        dve.scalar_tensor_tensor(ssq[:], diff[:], 0.25, ssq[:], ALU.mult, ALU.add).then_inc(moments, 1)
        dve.wait_ge(self.std_ready, 1)
        dve.reciprocal(self.rstd[:], ssq[:]).then_inc(self.rstd_ready, 1)
        dve.wait_ge(self.rstd_ready, 1)
        for t in range(NT):
            if t not in GP_TILES:
                self.apply(dve, t, self.normed_v)

    def scalar(self, act):
        act.wait_ge(self.moments, 7)
        act.activation(self.ssq[:], self.ssq[:], ACT.Sqrt).then_inc(self.std_ready, 1)

    def gpsimd(self, pool):
        pool.wait_ge(self.rstd_ready, 1)
        for t in GP_TILES:
            self.apply(pool, t, self.normed_p)

    def wait_chunk(self, eng, c):
        done = 4 * c + 4
        on_gp = sum(t < done for t in GP_TILES)
        eng.wait_ge(self.normed_v, done - on_gp)
        since(eng, self.normed_p, on_gp)


def layer_norm(nc, st, x, out, eps, load=None):
    norm = Norm(st, x, out, eps)
    with nc.Block() as block:

        @block.sync
        def _(sp):
            if load is not None:
                load(sp)

        @block.vector
        def _(dve):
            norm.vector(dve)

        @block.scalar
        def _(act):
            norm.scalar(act)

        @block.gpsimd
        def _(pool):
            norm.gpsimd(pool)


class NormTurn:

    def __init__(self, nc, st, x, xn, xT, eps, ident, pt, affine=None, affine_loaded=None):
        self.norm = Norm(st, x, xn, eps)
        self.xn, self.xT, self.ident, self.pt, self.affine, self.affine_loaded = xn, xT, ident, pt, affine, affine_loaded
        self.turned, self.kept = st.sem("nt_turned"), st.sem("nt_kept")

    def turn(self, pe, c):
        if c >= 2:
            pe.wait_ge(self.kept, c - 1)
        self.norm.wait_chunk(pe, c)
        for j in range(4):
            mm = pe.transpose(self.pt[:, c % 2, j * P:(j + 1) * P], self.xn[:, 4 * c + j, :], self.ident[:])
        mm.then_inc(self.turned, 1)

    def keep(self, act, c):
        if c == 0 and self.affine is not None:
            act.wait_ge(*self.affine_loaded)
        act.wait_ge(self.turned, c + 1)
        dst = self.xT[:, c * 512:(c + 1) * 512]
        if self.affine is None:
            act.activation(dst, self.pt[:, c % 2, :], ACT.Copy).then_inc(self.kept, 1)
        else:
            act.activation(dst, self.pt[:, c % 2, :], ACT.Identity, bias=self.affine[:, 1:2],
                           scale=self.affine[:, 0:1]).then_inc(self.kept, 1)


HEADS = 16
HD = D // HEADS
SEQ = 1024
BATCH = TOK // SEQ
QT = SEQ // P
BUCKETS = 32
NPOS = 2 * BUCKETS
Q_PARTS = (0, 0, 0, 1, 1, 2)
K_PARTS = (0, 1, 2, 0, 1, 0)
STACK = len(Q_PARTS) * HD
FARROWS = 9
KROWS = STACK + FARROWS


def stacked(dst, parts, order):
    for j, (a, b) in enumerate(((0, 3), (3, 5), (5, 6))):
        run = order[a:b]
        if len(set(run)) == 1:
            src = parts[:, run[0]:run[0] + 1, :].to_broadcast([P, b - a, parts.shape[2]])
        else:
            src = parts[:, run[0]:run[-1] + 1, :]
        yield dst[:, a:b, :], src


def log_bucket(r, bucket=BUCKETS, longest=64):
    mid = bucket // 2
    a = mid - 1 if abs(r) < mid else abs(r)
    if a <= mid:
        return a
    return int((math.ceil(math.log(a / mid) / math.log((longest - 1) / mid) * (mid - 1)) + mid) * (1 if r > 0 else -1))


def attn_a_constants():
    sel_c = np.zeros((NPOS, P + 3), np.float32)
    sel_p = np.zeros((NPOS, P + 3), np.float32)
    for j in range(P):
        f = log_bucket(64 - j)
        sel_c[min(max(f + BUCKETS, 0), NPOS - 1), j] += 1
        sel_p[min(max(BUCKETS - f, 0), NPOS - 1), j] += 1
    for s in (sel_c, sel_p):
        s[0, 0:P] -= 1
        s[NPOS - 1, P] -= 1
        s[0, P] += 1
        s[NPOS - 1, P + 1] = 1
        s[0, P + 2] = 1
    row, j = np.arange(P)[:, None] % 64, np.arange(P)[None, :]
    mask_c = (64 - j > row).astype(np.float32)
    mask_p = (row + j - 64 >= 64).astype(np.float32)
    heads = (np.arange(D)[:, None] // HD == np.arange(HEADS)[None, :]).astype(np.float32)
    return {"sel_c": sel_c, "sel_p": sel_p, "mask_c": mask_c, "mask_p": mask_p, "head_of": heads,
            "gather8": np.tile(np.eye(32, HD, dtype=np.float32), (4, 1)),
            "gather16": np.tile(np.eye(32, 2 * HD, dtype=np.float32), (4, 1))}


def attn_a(nc, x, d, cst):
    G = BATCH * HEADS
    inv_scale = 1.0 / math.sqrt(3 * HD)
    with stage(nc, "aa") as st:
        xn = st.sb("xn", [P, NT, D])
        ctx = st.sb("ctx", [P, QT, G, HD])
        vh = st.sb("vh", [P, QT, G, HD])
        ident = cst["ident"]
        qh = st.dram("qh", (G, STACK, SEQ), BF16)
        qf = st.dram("qf", (G, FARROWS, SEQ), BF16)
        kh = st.dram("kh", (G, STACK, SEQ), BF16)
        kf = st.dram("kf", (2, G, FARROWS, SEQ), BF16)
        tab = st.dram("tab", (G, STACK, 2 * (P + 1)), BF16)
        SKEW = P * (2 * P + 1)
        win = st.dram("win", (2, 2, QT, SKEW))
        attn_a_prepare(nc, x, d, cst, xn, vh, qh, qf, kh, kf, tab, win, inv_scale)
        attn_a_heads(nc, cst, ctx, vh, qh, qf, kh, kf, tab, win)
        attn_a_finish(nc, x, d, cst, xn, ctx)


def attn_a_prepare(nc, x, d, cst, xn, vh, qh, qf, kh, kf, tab, win, inv_scale):
    ident = cst["ident"]
    with stage(nc, "ap") as st:
        xT = st.sb("xT", [D, TOK])
        banks = st.ps("banks", [P, 8, 512])
        w = {n: st.sb(n, [D, D]) for n in ("Wq", "Wk", "Wv")}
        bq, bk = st.sb("bq", [D, 1]), st.sb("bk", [D, 1])
        bkrow, bvrow = st.sb("bkrow", [P, D]), st.sb("bvrow", [P, D])
        relT = st.sb("relT", [D, NPOS])
        sel = st.sb("sel", [NPOS, 2, P + 3])
        head_of = st.sb("head_of", [D, HEADS])
        posk = st.sb("posk", [NPOS, D])
        table = st.sb("table", [D, 2, P + 3])
        far_w = st.sb("far_w", [D, 2, 2, HEADS])
        tparts = st.sb("tparts", [D, 2, 3, P + 1], BF16)
        trest = st.sb("trest", [D, 2, P + 1])
        val = st.sb("val", [D, 2, TOK])
        rest = st.sb("rest", [D, 2, TOK])
        parts = st.sb("parts", [D, 2, 3, TOK], BF16)
        far = st.sb("far", [4 * HEADS, TOK])
        far_rest = st.sb("far_rest", [4 * HEADS, TOK])
        far_parts = st.sb("far_parts", [4 * HEADS, 3, TOK], BF16)
        ones = st.sb("ones", [HEADS, 3, SEQ], BF16)
        zeros = st.sb("zeros", [HEADS, 3, SEQ], BF16)
        zwin = st.sb("zwin", [P, 2056])
        loaded = st.sem("loaded")
        filled = st.sem("filled")
        step = st.sem("step")
        mm_done = st.sem("mm_done")
        evac = st.sem("evac")
        copied = st.sem("copied")
        posk_ready = st.sem("posk_ready")
        table_mm, table_ready = st.sem("table_mm"), st.sem("table_ready")
        farw_ready = st.sem("farw_ready")
        far_mm, far_ready = st.sem("far_mm"), st.sem("far_ready")
        v_mm, v_ready = st.sem("v_mm"), st.sem("v_ready")
        t_done = st.sem("t_done")
        split_done, high_done, mid_done = st.sem("split_done"), st.sem("high_done"), st.sem("mid_done")
        fsplit, fhigh, fmid = st.sem("fsplit"), st.sem("fhigh"), st.sem("fmid")
        stored = st.sem("stored")

        def load(sp):
            for name in ("Wq", "Wk", "Wv"):
                sp.dma_start(w[name][:], d["L0_attn_a_" + name]).then_inc(loaded, 16)
            sp.dma_start(bq[:], d["L0_attn_a_bq"].rearrange("(p o) -> p o", o=1)).then_inc(loaded, 16)
            sp.dma_start(bk[:], d["L0_attn_a_bk"].rearrange("(p o) -> p o", o=1)).then_inc(loaded, 16)
            sp.dma_start(bkrow[:], d["L0_attn_a_bk"].rearrange("(o n) -> o n", o=1).to_broadcast([P, D])).then_inc(loaded, 16)
            sp.dma_start(bvrow[:], d["L0_attn_a_bv"].rearrange("(o n) -> o n", o=1).to_broadcast([P, D])).then_inc(loaded, 16)
            sp.dma_start(relT[:], d["relT"]).then_inc(loaded, 16)
            sp.dma_start(sel[:, 0, :], d["sel_c"]).then_inc(loaded, 16)
            sp.dma_start(sel[:, 1, :], d["sel_p"]).then_inc(loaded, 16)
            sp.dma_start(head_of[:], d["head_of"]).then_inc(loaded, 16)
            sp.wait_ge(filled, 3)
            for slot in range(2):
                for side in range(2):
                    flat = win[slot, side].rearrange("t (p c) -> p t c", p=P)
                    sp.dma_start(flat, zwin[:, 0:QT * 257].rearrange("p (t c) -> p t c", t=QT)).then_inc(stored, 16)
            for b in range(BATCH):
                gs = slice(b * HEADS, (b + 1) * HEADS)
                sp.dma_start(qf[gs, 6:9, :], ones[:]).then_inc(stored, 16)
                sp.dma_start(kf[0, gs, 0:3, :], ones[:]).then_inc(stored, 16)
                sp.dma_start(kf[0, gs, 3:6, :], zeros[:]).then_inc(stored, 16)
                sp.dma_start(kf[1, gs, 0:3, :], zeros[:]).then_inc(stored, 16)
                sp.dma_start(kf[1, gs, 3:6, :], ones[:]).then_inc(stored, 16)

        def fill(pool):
            pool.memset(zwin[:], 0.0).then_inc(filled, 1)
            pool.memset(ones[:], 1.0).then_inc(filled, 1)
            pool.memset(zeros[:], 0.0).then_inc(filled, 1)

        ln = NormTurn(nc, st, x, xn, xT, 1e-5, ident, banks[:, 6:8, :])
        with nc.Block() as block:

            @block.gpsimd
            def _(pool):
                fill(pool)
                ln.norm.gpsimd(pool)

            @block.sync
            def _(sp):
                load(sp)
                n = 4 + 5 * BATCH
                sp.wait_ge(t_done, 4)
                for side, order in ((0, K_PARTS), (1, Q_PARTS)):
                    for b in range(BATCH):
                        rows = tab[b * HEADS:(b + 1) * HEADS].rearrange("h (e r) c -> (h e) r c", e=HD)
                        for dst, src in stacked(rows[:, :, side * (P + 1):(side + 1) * (P + 1)], tparts[:, side], order):
                            sp.dma_start(dst, src).then_inc(stored, 16)
                            n += 1
                for side, (buf, order) in enumerate(((qh, Q_PARTS), (kh, K_PARTS))):
                    sp.wait_ge(split_done, side + 1)
                    for b in range(BATCH):
                        rows = buf[b * HEADS:(b + 1) * HEADS].rearrange("h (e r) c -> (h e) r c", e=HD)
                        for dst, src in stacked(rows, parts[:, side, :, b * SEQ:(b + 1) * SEQ], order):
                            sp.dma_start(dst, src).then_inc(stored, 16)
                            n += 1
                sp.wait_ge(fsplit, 1)
                for b in range(BATCH):
                    gs, ts = slice(b * HEADS, (b + 1) * HEADS), slice(b * SEQ, (b + 1) * SEQ)
                    for sign in range(2):
                        sp.dma_start(qf[gs, 3 * sign:3 * sign + 3, :], far_parts[sign * HEADS:(sign + 1) * HEADS, :, ts]).then_inc(stored, 16)
                        sp.dma_start(kf[sign, gs, 6:9, :], far_parts[(2 + sign) * HEADS:(3 + sign) * HEADS, :, ts]).then_inc(stored, 16)
                        n += 2
                sp.wait_ge(stored, 16 * n)

            @block.tensor
            def _(pe):
                for c in range(NCH):
                    ln.turn(pe, c)
                pe.wait_ge(loaded, 16 * 11)
                pe.matmul(banks[0:NPOS, 0, 0:D], relT[:], w["Wk"][:], start=True, stop=True).then_inc(mm_done, 1)
                pe.wait_ge(posk_ready, 1)
                for side in range(2):
                    mm = pe.matmul(banks[:, 1 + side, 0:P + 3], posk[:], sel[:, side, :], start=True, stop=True)
                mm.then_inc(table_mm, 1)
                for c in range(NCH):
                    pe.wait_ge(ln.kept, c + 1)
                    for i, name in enumerate(("Wq", "Wk")):
                        if c >= 1:
                            pe.wait_ge(evac, 2 * (c - 1) + i + 1)
                        pe.matmul(banks[:, 3 + i, :], w[name][:], xT[:, c * 512:(c + 1) * 512], start=True,
                                  stop=True).then_inc(copied, 1)
                pe.wait_ge(farw_ready, 4)
                for c in range(NCH):
                    pe.wait_ge(evac, 2 * c + 2)
                    if c >= 2:
                        pe.wait_ge(far_ready, c - 1)
                    for i in range(2):
                        rows = slice(i * 2 * HEADS, (i + 1) * 2 * HEADS)
                        mm = pe.matmul(banks[rows, 6 + c % 2, :], far_w[:, i, :, :].rearrange("p s h -> p (s h)"),
                                       val[:, i, c * 512:(c + 1) * 512], start=True, stop=True,
                                       tile_position=(0, i * 2 * HEADS))
                    mm.then_inc(far_mm, 1)
                for c in range(NCH):
                    if c >= 1:
                        pe.wait_ge(v_ready, c)
                    for j in range(4):
                        t = 4 * c + j
                        mm = pe.matmul(banks[:, 5, j * P:(j + 1) * P], xT[:, t * P:(t + 1) * P], w["Wv"][:],
                                       start=True, stop=True)
                    mm.then_inc(v_mm, 1)

            @block.vector
            def _(dve):
                ln.norm.vector(dve)
                dve.wait_ge(loaded, 16 * 11)
                dve.wait_ge(mm_done, 1)
                dve.tensor_tensor(posk[:], banks[0:NPOS, 0, 0:D], bkrow[0:NPOS, :], ALU.add).then_inc(posk_ready, 1)
                dve.wait_ge(table_mm, 1)
                dve.tensor_copy(table[:, 0, :], banks[:, 1, 0:P + 3]).then_inc(table_ready, 1)
                dve.tensor_scalar(table[:, 1, :], banks[:, 2, 0:P + 3], inv_scale, None, ALU.mult).then_inc(table_ready, 1)
                dve.wait_ge(table_ready, 2)
                for i in range(4):
                    dve.tensor_scalar(far_w[:, i // 2, i % 2, :], head_of[:], table[:, i // 2, P + 1 + i % 2:P + 2 + i % 2], None,
                                      ALU.mult).then_inc(farw_ready, 1)
                dve.tensor_copy(tparts[:, :, 0, :], table[:, :, 0:P + 1]).then_inc(t_done, 1)
                dve.wait_ge(t_done, 1)
                dve.tensor_tensor(trest[:], table[:, :, 0:P + 1], tparts[:, :, 0, :], ALU.subtract).then_inc(t_done, 1)
                dve.wait_ge(t_done, 2)
                dve.tensor_copy(tparts[:, :, 1, :], trest[:]).then_inc(t_done, 1)
                dve.wait_ge(t_done, 3)
                dve.tensor_tensor(tparts[:, :, 2, :], trest[:], tparts[:, :, 1, :], ALU.subtract).then_inc(t_done, 1)
                for c in range(NCH):
                    cs = slice(c * 512, (c + 1) * 512)
                    dve.wait_ge(copied, 2 * c + 1)
                    dve.tensor_scalar(val[:, 0, cs], banks[:, 3, :], bq[:, 0:1], inv_scale, ALU.add, ALU.mult).then_inc(evac, 1)
                    dve.wait_ge(copied, 2 * c + 2)
                    dve.tensor_scalar(val[:, 1, cs], banks[:, 4, :], bk[:, 0:1], None, ALU.add).then_inc(evac, 1)
                for c in range(NCH):
                    dve.wait_ge(far_mm, c + 1)
                    dve.tensor_copy(far[:, c * 512:(c + 1) * 512], banks[0:4 * HEADS, 6 + c % 2, :]).then_inc(far_ready, 1)
                for i in range(2):
                    dve.wait_ge(high_done, i + 1)
                    dve.tensor_tensor(rest[:, i, :], val[:, i, :], parts[:, i, 0, :], ALU.subtract).then_inc(step, 1)
                dve.wait_ge(fhigh, 1)
                dve.tensor_tensor(far_rest[:], far[:], far_parts[:, 0, :], ALU.subtract).then_inc(step, 1)
                for i in range(2):
                    dve.wait_ge(mid_done, i + 1)
                    dve.tensor_tensor(parts[:, i, 2, :], rest[:, i, :], parts[:, i, 1, :], ALU.subtract).then_inc(split_done, 1)
                dve.wait_ge(fmid, 1)
                dve.tensor_tensor(far_parts[:, 2, :], far_rest[:], far_parts[:, 1, :], ALU.subtract).then_inc(fsplit, 1)
                for c in range(NCH):
                    dve.wait_ge(v_mm, c + 1)
                    b, k0 = 4 * c // QT, 4 * c % QT
                    dst = vh[:, k0:k0 + 4, b * HEADS:(b + 1) * HEADS, :].rearrange("p t g e -> p t (g e)")
                    src = banks[:, 5, :].rearrange("p (t n) -> p t n", t=4)
                    bv = bvrow[:].rearrange("p (o n) -> p o n", o=1).to_broadcast([P, 4, D])
                    dve.tensor_tensor(dst, src, bv, ALU.add).then_inc(v_ready, 1)

            @block.scalar
            def _(act):
                ln.norm.scalar(act)
                for c in range(NCH):
                    ln.keep(act, c)
                act.wait_ge(evac, 8)
                for i in range(2):
                    act.activation(parts[:, i, 0, :], val[:, i, :], ACT.Copy).then_inc(high_done, 1)
                act.wait_ge(far_ready, NCH)
                act.activation(far_parts[:, 0, :], far[:], ACT.Copy).then_inc(fhigh, 1)
                for i in range(2):
                    act.wait_ge(step, i + 1)
                    act.activation(parts[:, i, 1, :], rest[:, i, :], ACT.Copy).then_inc(mid_done, 1)
                act.wait_ge(step, 3)
                act.activation(far_parts[:, 1, :], far_rest[:], ACT.Copy).then_inc(fmid, 1)


def back(i, s, k, nstep):
    j, r = (i, s - k) if s >= k else (i - 1, s - k + nstep)
    return nstep * i + s - k, r, 2 * j + r // QT


VCOLS = 32


def place_v(pool, v_s, vh, width, v_placed, pv_done, g, par, first):
    if not first:
        pool.wait_ge(pv_done, QT * (g - 1))
    pool.tensor_copy(v_s[:, par, :, 0:width], vh[:, :, g, :]).then_inc(v_placed, 1)


def since(eng, sem, value):
    if not isinstance(value, int) or value > 0:
        eng.wait_ge(sem, value)


def attn_a_heads(nc, cst, ctx, vh, qh, qf, kh, kf, tab, win):
    ident = cst["ident"]
    G = BATCH * HEADS
    NSTEP = 2 * QT
    PAIRS = QT // 2
    LIVE = ((slice(0, 64), slice(0, 192)), (slice(64, P), slice(64, 2 * P)))
    with stage(nc, "ah") as st:
        q_s = st.sb("q", [KROWS, 2, SEQ], BF16)
        kp_s = st.sb("kp", [KROWS, 2, SEQ], BF16)
        km_s = st.sb("km", [KROWS, 2, SEQ], BF16)
        tb_s = st.sb("tb", [STACK, 2, 2 * (P + 1)], BF16)
        band = st.sb("band", [P, 2, QT, P])
        raw = st.sb("raw", [P, 2, 2, 2, P + 1])
        far = st.sb("far", [P, 2, 2, P])
        cwin = st.sb("cwin", [P, 2, QT, 2 * P])
        pwin = st.sb("pwin", [P, 2, QT, 2 * P])
        prob = st.sb("prob", [P, 2, SEQ])
        probT = st.sb("probT", [P, 2, QT, P])
        v_s = st.sb("v", [P, 2, QT, VCOLS])
        outT = st.sb("outT", [P, 2, P])
        gather = st.sb("gather", [P, HD])
        negmax = st.sb("negmax", [P, 2])
        rowsum = st.sb("rowsum", [P, 2, QT])
        rinv = st.sb("rinv", [P, 2, QT])
        masks = st.sb("masks", [P, 2, P])
        scores = st.ps("scores", [P, 2, 2, 512])
        turned = st.ps("turned", [P, QT, P])
        BW = 2 * (P + 1)
        shared = st.ps("shared", [P, 2, 512])
        outp = shared[:, 0, BW:BW + P]
        ctxp = shared[:, 1, BW:BW + QT * HD].rearrange("p (t e) -> p t e", t=QT)
        mask_loaded = st.sem("mask_loaded")
        band_ops, base_ops = ([st.sem(f"{n}_ops{i}") for i in range(2)] for n in ("band", "base"))
        win_stored = st.sem("win_stored")
        win_loaded = [[st.sem(f"win_loaded{i}_{half}") for half in range(2)] for i in range(2)]
        band_mm, band_raw, far_masked, band_kept = (st.sem(n) for n in ("band_mm", "band_raw", "far_masked", "band_kept"))
        base_done, window_added = st.sem("base_done"), st.sem("window_added")
        max_ready, probs_ready = st.sem("max_ready"), st.sem("probs_ready")
        probs_turned, kept_a, kept_v = st.sem("probs_turned"), st.sem("kept_a"), st.sem("kept_v")
        corners = st.sem("corners")
        v_clear, v_placed = st.sem("v_clear"), st.sem("v_placed")
        pv_done, out_kept, gathered = st.sem("pv_done"), st.sem("out_kept"), st.sem("gathered")
        rinv_ready, ctx_kept = st.sem("rinv_ready"), st.sem("ctx_kept")


        def passes(eng, run):
            run(0, True, False)
            with eng.Fori(1, G // 2 - 1) as i:
                run(i, False, False)
            run(G // 2 - 1, False, True)

        with nc.Block() as block:

            @block.sync
            def _(sp):
                def load_head(g, par):
                    for dst, src in ((q_s[0:STACK, par, :], qh[g]), (kp_s[0:STACK, par, :], kh[g]), (tb_s[:, par, :], tab[g])):
                        sp.dma_start(dst, src).then_inc(band_ops[par], 16)
                    for dst, src in ((q_s[STACK:KROWS, par, :], qf[g]), (kp_s[STACK:KROWS, par, :], kf[0, g]), (km_s[0:STACK, par, :], kh[g]),
                                     (km_s[STACK:KROWS, par, :], kf[1, g])):
                        sp.dma_start(dst, src).then_inc(base_ops[par], 16)

                def window_trip(g, par):
                    for half in range(2):
                        tiles = slice(half * PAIRS, (half + 1) * PAIRS)
                        sp.wait_ge(band_kept, PAIRS * g + PAIRS // 2 * (half + 1))
                        for side in range(2):
                            dst = win[par, side].rearrange("t (p c) -> p t c", p=P)[:, tiles, 0:P]
                            sp.dma_start(dst, band[:, side, tiles, :]).then_inc(win_stored, 16)
                        sp.wait_ge(win_stored, 64 * g + 32 * (half + 1))
                        for side, buf in ((1, pwin), (0, cwin)):
                            src = win[par, side][:, 0:2 * P * P].rearrange("t (p c) -> p t c", p=P)
                            for rows, cols in LIVE:
                                sp.dma_start(buf[rows, par, tiles, cols],
                                             src[rows, tiles, cols]).then_inc(win_loaded[par][half], 16)

                def run(i, first, last):
                    for par in range(1 if last else 2):
                        g1 = 2 * i + par + 1
                        since(sp, window_added, QT * (g1 - 1))
                        load_head(g1, 1 - par)
                        window_trip(g1, 1 - par)

                sp.dma_start(masks[:, 0, :], cst["mask_c"]).then_inc(mask_loaded, 16)
                sp.dma_start(masks[:, 1, :], cst["mask_p"]).then_inc(mask_loaded, 16)
                sp.dma_start(gather[:], cst["gather8"]).then_inc(mask_loaded, 16)
                load_head(0, 0)
                window_trip(0, 0)
                passes(sp, run)

            @block.tensor
            def _(pe):
                def band_tiles(pair, par):
                    for k in range(2):
                        ts = slice((2 * pair + k) * P, (2 * pair + k + 1) * P)
                        pe.matmul(shared[:, k, 0:P + 1], q_s[0:STACK, par, ts], tb_s[:, par, 0:P + 1], start=True,
                                  stop=True)
                        mm = pe.matmul(shared[:, k, P + 1:BW], kp_s[0:STACK, par, ts], tb_s[:, par, P + 1:BW],
                                       start=True, stop=True)
                    mm.then_inc(band_mm, 1)

                def base(s):
                    par, t = s // QT, s % QT
                    lo = t * P
                    for bank in range(2):
                        b0, b1 = bank * 512, (bank + 1) * 512
                        todo = []
                        if max(lo + 64, b0) < b1:
                            a = max(lo + 64, b0)
                            todo.append((slice(0, P), a, b1, q_s[:, par, lo:lo + P], km_s[:, par, a:b1]))
                        if b0 < min(lo, b1):
                            a = min(lo, b1)
                            todo.append((slice(0, P), b0, a, q_s[:, par, lo:lo + P], kp_s[:, par, b0:a]))
                        if b0 <= lo < b1:
                            todo.append((slice(0, 64), lo, lo + 64, q_s[:, par, lo:lo + 64], km_s[:, par, lo:lo + 64]))
                            todo.append((slice(64, P), lo, lo + 64, q_s[:, par, lo + 64:lo + P],
                                         kp_s[:, par, lo:lo + 64]))
                        for kt, rows, cols in ((t - 1, slice(0, 64), slice(192, 256)), (t, slice(0, P), slice(64, 192)),
                                               (t + 1, slice(64, P), slice(0, 64))):
                            if 0 <= kt < QT and b0 <= kt * P < b1:
                                todo.append((rows, kt * P, kt * P + P, pwin[:, par, kt, cols], ident[:]))
                        for j, (rows, c0, c1, lhs, rhs) in enumerate(todo):
                            mm = pe.matmul(scores[rows, s % 2, bank, c0 - b0:c1 - b0], lhs, rhs, start=j == 0,
                                           stop=j == len(todo) - 1, skip_group_check=True)
                    mm.then_inc(base_done, 1)

                def turn(n, s):
                    pe.wait_ge(probs_ready, n + 1)
                    since(pe, kept_a, n)
                    since(pe, kept_v, n)
                    for kt in range(QT):
                        mm = pe.transpose(turned[:, kt, :], prob[:, s % 2, kt * P:(kt + 1) * P], ident[:])
                    mm.then_inc(probs_turned, 1)

                def times_v(n, s, g):
                    if s % QT == 0:
                        pe.wait_ge(v_placed, g + 1)
                    pe.wait_ge(kept_a, n + 1)
                    pe.wait_ge(kept_v, n + 1)
                    since(pe, out_kept, n)
                    for kt in range(QT):
                        r = kt % 4 * 32
                        mm = pe.matmul(outp[r:r + VCOLS, :], v_s[:, s // QT, kt, :], probT[:, s % 2, kt, :],
                                       start=kt < 4, stop=kt >= 4, tile_position=(0, r), skip_group_check=True)
                    mm.then_inc(pv_done, 1)

                def add_parts(n, s, g):
                    pe.wait_ge(out_kept, n + 1)
                    if s % QT == 0:
                        since(pe, ctx_kept, g)
                    pe.matmul(ctxp[:, s % QT, :], outT[:, s % 2, :], gather[:], start=True,
                              stop=True).then_inc(gathered, 1)

                def run(i, first, last):
                    for s in range(NSTEP):
                        n, par, t = NSTEP * i + s, s // QT, s % QT
                        more = not (last and par == 1)
                        if t == 0:
                            pe.wait_ge(base_ops[par], 64 * (i + 1))
                        if t in (0, PAIRS - 1):
                            pe.wait_ge(win_loaded[par][t // (PAIRS - 1)], 64 * (i + 1))
                        if not (first and s < 2):
                            pe.wait_ge(probs_ready, n - 1)
                        base(s)
                        if more and 1 <= t <= PAIRS:
                            pe.wait_ge(band_raw, PAIRS * (2 * i + par + 1) + t)
                        if not (first and s < 2):
                            times_v(*back(i, s, 2, NSTEP))
                        if not (first and s < 3):
                            add_parts(*back(i, s, 3, NSTEP))
                        if not (first and s < 1):
                            turn(n - 1, s - 1)
                        if more and t < PAIRS:
                            if t == 0:
                                pe.wait_ge(band_ops[1 - par], 48 * (i + 1 + par))
                            if not (first and s < 2):
                                pe.wait_ge(out_kept, n - 1)
                            if t == 2:
                                since(pe, ctx_kept, 2 * i + par)
                            band_tiles(t, 1 - par)

                pe.wait_ge(mask_loaded, 48)
                pe.wait_ge(corners, 4)
                pe.wait_ge(band_ops[0], 48)
                for pair in range(PAIRS):
                    since(pe, band_raw, pair)
                    band_tiles(pair, 0)
                pe.wait_ge(band_raw, PAIRS)
                passes(pe, run)
                times_v(*back(G // 2, 0, 2, NSTEP))
                add_parts(*back(G // 2, 0, 3, NSTEP))
                turn(QT * G - 1, NSTEP - 1)
                add_parts(*back(G // 2, 0, 2, NSTEP))
                times_v(*back(G // 2, 0, 1, NSTEP))
                add_parts(*back(G // 2, 0, 1, NSTEP))

            @block.vector
            def _(dve):
                def keep_out(n, s):
                    dve.wait_ge(pv_done, n + 1)
                    since(dve, gathered, n - 1)
                    dve.tensor_copy(outT[:, s % 2, :], outp).then_inc(out_kept, 1)

                def invert(g, par):
                    dve.wait_ge(probs_ready, QT * (g + 1))
                    dve.reciprocal(rinv[:, par, :], rowsum[:, par, :]).then_inc(rinv_ready, 1)

                def keep_ctx(g, par):
                    dve.wait_ge(rinv_ready, g + 1)
                    dve.wait_ge(gathered, QT * (g + 1))
                    over = rinv[:, par, :].rearrange("p (t e) -> p t e", e=1).to_broadcast([P, QT, HD])
                    dve.tensor_tensor(ctx[:, :, g, :], ctxp[:], over, ALU.mult).then_inc(ctx_kept, 1)

                def keep_turned(n, s):
                    dve.wait_ge(probs_turned, n + 1)
                    since(dve, pv_done, n - 1)
                    dve.tensor_copy(probT[:, s % 2, QT // 2:QT, :], turned[:, QT // 2:QT, :]).then_inc(kept_v, 1)

                def run(i, first, last):
                    for s in range(NSTEP):
                        n, par, t = NSTEP * i + s, s // QT, s % QT
                        if t % PAIRS == 0:
                            dve.wait_ge(win_loaded[par][t // PAIRS], 64 * (i + 1))
                        lo, hi = max(t * P - 64, 0), min(t * P + 192, SEQ)
                        off = lo - (t * P - 64)
                        dve.wait_ge(base_done, n + 1)
                        row = scores[:, s % 2, :, :].rearrange("p b c -> p (b c)")
                        dve.tensor_tensor(row[:, lo:hi], row[:, lo:hi], cwin[:, par, t, off:off + hi - lo],
                                          ALU.add).then_inc(window_added, 1)
                        dve.wait_ge(window_added, n + 1)
                        dve.tensor_reduce(negmax[:, s % 2:s % 2 + 1], row, AX.X, ALU.max, negate=True).then_inc(max_ready, 1)
                        if not (first and s < 2):
                            keep_out(n - 2, s)
                        if t == 2 and not (first and par == 0):
                            keep_ctx(2 * i + par - 1, 1 - par)
                        if not (first and s < 1):
                            keep_turned(n - 1, s - 1)
                        if t == 1 and not (first and par == 0):
                            invert(2 * i + par - 1, 1 - par)
                dve.wait_ge(corners, 4)
                passes(dve, run)
                n = QT * G
                keep_out(n - 2, NSTEP - 2)
                keep_turned(n - 1, NSTEP - 1)
                keep_out(n - 1, NSTEP - 1)
                invert(G - 1, 1)
                keep_ctx(G - 1, 1)

            @block.scalar
            def _(act):
                def keep_turned(n, s):
                    act.wait_ge(probs_turned, n + 1)
                    since(act, pv_done, n - 1)
                    act.activation(probT[:, s % 2, 0:QT // 2, :], turned[:, 0:QT // 2, :], ACT.Copy).then_inc(kept_a, 1)

                def keep_band(pair, pairs):
                    act.wait_ge(band_mm, pairs)
                    since(act, band_kept, pairs - 2)
                    act.activation(raw[:, pair % 2].rearrange("p k s c -> p k (s c)"), shared[:, :, 0:BW],
                                   ACT.Copy).then_inc(band_raw, 1)

                def run(i, first, last):
                    for s in range(NSTEP):
                        n, par, t = NSTEP * i + s, s // QT, s % QT
                        if not (first and s < 1):
                            keep_turned(n - 1, s - 1)
                        if t < PAIRS and not (last and par == 1):
                            keep_band(t, PAIRS * (2 * i + par + 1) + t + 1)
                        act.wait_ge(max_ready, n + 1)
                        if not (first and s < 2):
                            act.wait_ge(probs_turned, n - 1)
                        if s % QT == 0 and not first:
                            act.wait_ge(rinv_ready, 2 * i + s // QT - 1)
                        act.activation(prob[:, s % 2, :], scores[:, s % 2, :, :].rearrange("p b c -> p (b c)"), ACT.Exp,
                                       bias=negmax[:, s % 2:s % 2 + 1],
                                       accum_out=rowsum[:, s // QT, s % QT:s % QT + 1]).then_inc(probs_ready, 1)

                for pair in range(PAIRS):
                    keep_band(pair, pair + 1)
                passes(act, run)
                keep_turned(QT * G - 1, NSTEP - 1)

            @block.gpsimd
            def _(pool):
                def run(i, first, last):
                    for par in range(2):
                        place_v(pool, v_s, vh, HD, v_placed, pv_done, 2 * i + par, par, first)
                        if not (last and par == 1):
                            pool.wait_ge(win_stored, 64 * (2 * i + par + 1))
                            for pair in range(PAIRS):
                                finish_band(pair, PAIRS * (2 * i + par + 1) + pair + 1)

                def finish_band(pair, pairs):
                    pool.wait_ge(band_raw, pairs)
                    since(pool, band_kept, pairs - 1)
                    pair_of = raw[:, pair % 2]
                    mask = masks[:].rearrange("p (k s) c -> p k s c", k=1).to_broadcast([P, 2, 2, P])
                    pool.tensor_tensor(far[:], mask, pair_of[:, :, :, P:P + 1].to_broadcast([P, 2, 2, P]),
                                       ALU.mult).then_inc(far_masked, 1)
                    pool.wait_ge(far_masked, pairs)
                    dst = band[:, :, 2 * pair:2 * pair + 2, :].rearrange("p s k c -> p k s c")
                    pool.tensor_tensor(dst, pair_of[:, :, :, 0:P], far[:], ALU.add).then_inc(band_kept, 1)

                pool.memset(v_s[:], 0.0).then_inc(v_clear, 1)
                pool.wait_ge(v_clear, 1)
                for k, buf in enumerate((cwin, pwin)):
                    since(pool, corners, 2 * k)
                    pool.memset(buf[0:64, :, :, 192:2 * P], 0.0).then_inc(corners, 1)
                    pool.wait_ge(corners, 2 * k + 1)
                    pool.memset(buf[64:P, :, :, 0:64], 0.0).then_inc(corners, 1)
                pool.wait_ge(mask_loaded, 48)
                for pair in range(PAIRS):
                    finish_band(pair, pair + 1)
                passes(pool, run)


def attn_a_finish(nc, x, d, cst, xn, ctx):
    ident = cst["ident"]
    with stage(nc, "af") as st:
        wo = st.sb("wo", [D, D])
        rows = st.sb("rows", [P, 3, D])
        ctxT = st.sb("ctxT", [D, 2, P])
        y = st.sb("y", [P, NT, D])
        z = st.sb("z", [P, NT, D])
        banks = st.ps("banks", [P, 4, 512])
        loaded = st.sem("loaded")
        turned, kept, projected = st.sem("turned"), st.sem("kept"), st.sem("projected")
        summed, biased = st.sem("summed"), st.sem("biased")
        scaled, shifted, added = st.sem("scaled"), st.sem("shifted"), st.sem("added")

        def of_all(i):
            return rows[:, i:i + 1, :].to_broadcast([P, NT, D])

        with nc.Block() as block:

            @block.gpsimd
            def _(pool):
                pool.wait_ge(loaded, 64)
                pool.tensor_tensor(x[:], x[:], of_all(2), ALU.add).then_inc(shifted, 1)

            @block.sync
            def _(sp):
                sp.dma_start(wo[:], d["L0_attn_a_Wo"]).then_inc(loaded, 16)
                for i, name in enumerate(("bo", "ln_scale", "ln_bias")):
                    src = d["L0_attn_a_" + name].rearrange("(o n) -> o n", o=1).to_broadcast([P, D])
                    sp.dma_start(rows[:, i, :], src).then_inc(loaded, 16)

            @block.tensor
            def _(pe):
                def turn(t):
                    b, qt = t // QT, t % QT
                    since(pe, kept, t - 1)
                    src = ctx[:, qt, b * HEADS:(b + 1) * HEADS, :].rearrange("p g e -> p (g e)")
                    pe.transpose(banks[:, t % 2, 0:P], src, ident[:]).then_inc(turned, 1)

                turn(0)
                pe.wait_ge(loaded, 64)
                for t in range(NT):
                    if t + 1 < NT:
                        turn(t + 1)
                    pe.wait_ge(kept, t + 1)
                    since(pe, summed, t - 1)
                    pe.matmul(banks[:, 2 + t % 2, 0:D], ctxT[:, t % 2, :], wo[:], start=True, stop=True).then_inc(projected, 1)

            @block.scalar
            def _(act):
                for t in range(NT):
                    act.wait_ge(turned, t + 1)
                    if t >= 2:
                        act.wait_ge(projected, t - 1)
                    act.activation(ctxT[:, t % 2, :], banks[:, t % 2, 0:P], ACT.Copy).then_inc(kept, 1)

            @block.vector
            def _(dve):
                dve.wait_ge(loaded, 64)
                dve.tensor_tensor(xn[:], xn[:], of_all(0), ALU.add).then_inc(biased, 1)
                dve.wait_ge(biased, 1)
                for t in range(NT):
                    dve.wait_ge(projected, t + 1)
                    dve.tensor_tensor(y[:, t, :], banks[:, 2 + t % 2, 0:D], xn[:, t, :], ALU.add).then_inc(summed, 1)
        layer_norm(nc, st, y, z, 1e-7)
        with nc.Block() as block:

            @block.vector
            def _(dve):
                dve.tensor_tensor(z[:], z[:], of_all(1), ALU.mult).then_inc(scaled, 1)
                dve.wait_ge(scaled, 1)
                dve.wait_ge(shifted, 1)
                dve.tensor_tensor(x[:], x[:], z[:], ALU.add).then_inc(added, 1)


FF_DEPTH = 2
FF_HEADS = 8
FF_HD = 64
FF_WIN = 64
FF_INNER = FF_HEADS * FF_HD
FF_PAIRS = FF_INNER // P
HID = int(D * 4 * 2 / 3)
HID_CUT = [(0, 128), (128, 256), (256, HID)]
NEG = -1e30


def ffn_constants():
    f4 = np.float32
    half = np.arange(0, FF_HD, 2, dtype=f4)
    inv_freq = (f4(1.0) / np.power(f4(10000.0), half / f4(FF_HD))).astype(f4)
    t = np.arange(SEQ, dtype=f4)
    freqs = t[:, None] * inv_freq[None, :]
    base = ((half + f4(0.4 * FF_HD)) / f4(1.4 * FF_HD)).astype(f4)
    power = ((t - SEQ // 2) / f4(FF_WIN // 2)).astype(f4)
    scale = np.power(base[None, :], power[:, None]).astype(f4)
    cos, sin = np.cos(freqs), np.sin(freqs)
    two = lambda a: np.concatenate([a, a], axis=-1)
    signed = np.concatenate([-sin, sin], axis=-1)
    tabs = np.stack([two(cos * scale), signed * two(scale), two(cos / scale), signed / two(scale)]).astype(f4)
    rot = tabs.reshape(4, QT, P, FF_HD).transpose(2, 0, 1, 3)
    m, i = np.arange(P)[None, :], (np.arange(P) % FF_WIN)[:, None]
    allowed = (m <= i + FF_WIN) & (m >= i)
    first = allowed & ((m >= FF_WIN) | (np.arange(P)[:, None] >= FF_WIN))
    mask = np.where(np.stack([allowed, first], axis=1), 0.0, NEG).astype(f4)
    return {"rot": np.ascontiguousarray(rot), "local_mask": mask}


def ffn(nc, x, d, cst, tag):
    with stage(nc, tag) as st:
        u = st.sb("u", [P, NT, D])
        h = st.sb("h", [P, NT, D])
        rot0 = st.sb("rot0", [P, 2, 2, QT, FF_HD])
        mask = st.sb("mask", [P, 2, P])
        tables = st.sem("tables")

        def load(sp):
            sp.dma_start(mask[:], d["local_mask"]).then_inc(tables, 16)
            sp.dma_start(rot0[:], d["rot"].rearrange("p (i c) t e -> p i c t e", c=2)).then_inc(tables, 16)
            sp.wait_ge(tables, 32)

        layer_norm(nc, st, x, u, 1e-5, load)
        with nc.Fori(0, FF_DEPTH) as layer:
            ffn_attention(nc, u, d, cst, layer, tag + "a", rot0, mask, h)
            ffn_glu(nc, u, d, cst, layer, tag + "g", h)
        added = st.sem("added")
        with nc.Block() as block:

            @block.vector
            def _(dve):
                dve.tensor_tensor(x[:], x[:], u[:], ALU.add).then_inc(added, 1)


def row_of(ap, n):
    return ap.rearrange("(o n) -> o n", o=1).to_broadcast([n, ap.shape[0]])


def ffn_attention(nc, u, d, cst, layer, tag, rot0, mask, h):
    ident = cst["ident"]
    PAD = FF_WIN
    with stage(nc, tag) as st:
        qT = st.sb("qT", [P, FF_PAIRS, TOK])
        kT = st.sb("kT", [P, FF_PAIRS, PAD + TOK])
        v_own = st.sb("v_own", [P, NT, FF_HEADS, FF_HD + 1])
        v_prev = st.sb("v_prev", [P, NT, FF_HEADS, FF_HD + 1])
        wo = st.sb("wo", [P, FF_PAIRS, D])
        ffn_qkv(nc, u, d, cst, layer, tag + "q", rot0, h, qT, kT, v_own, v_prev, wo)
        ffn_windows(nc, u, d, cst, layer, tag + "w", mask, h, qT, kT, v_own, v_prev, wo)


def ffn_qkv(nc, u, d, cst, layer, tag, rot0, h, qT, kT, v_own, v_prev, wo):
    ident = cst["ident"]
    QK = (2, FF_HEADS, FF_HD)
    with stage(nc, tag) as st:
        w = st.sb("w", [D, 3 * FF_INNER])
        srow = st.sb("srow", [P, 2, FF_HD])
        rot = st.sb("rot", [P, 2, 2, QT, FF_HD])
        hT = h[:].rearrange("p t c -> p (t c)")
        sq = st.sb("sq", [P, *QK])
        norm = st.sb("norm", [P, 2, 2, FF_HEADS])
        rn = st.sb("rn", [P, 2, 2, FF_HEADS])
        tc = st.sb("tc", [P, 4, *QK])
        ts_ = st.sb("ts", [P, *QK])
        qk = st.ps("qk", [P, 2, 2, 512])
        vp = st.ps("vp", [P, 512])
        hp = st.ps("hp", [P, 512])
        tp = st.ps("tp", [P, 2, 512])
        loaded, w_loaded, table_ready = st.sem("loaded"), st.sem("w_loaded"), st.sem("table_ready")
        h_turned, h_kept, filled = st.sem("h_turned"), st.sem("h_kept"), st.sem("filled")
        qk_done, v_done, v_kept, v_moved = (st.sem(n) for n in ("qk_done", "v_done", "v_kept", "v_moved"))
        squared, summed, rooted, clipped, inverted = (st.sem(n) for n in ("squared", "summed", "rooted", "clipped", "inverted"))
        products, rotated, q_scaled, k_scaled = (st.sem(n) for n in ("products", "rotated", "q_scaled", "k_scaled"))
        turned, kept = st.sem("turned"), st.sem("kept")
        with nc.Block() as block:

            @block.sync
            def _(sp):
                sp.dma_start(srow[:, 0, :], d["L0_ffn_q_scale"][bass.ts(layer, 1), :].to_broadcast([P, FF_HD])).then_inc(loaded, 16)
                sp.dma_start(srow[:, 1, :], d["L0_ffn_k_scale"][bass.ts(layer, 1), :].to_broadcast([P, FF_HD])).then_inc(loaded, 16)
                sp.dma_start(w[:], d["L0_ffn_wqkv"][layer]).then_inc(w_loaded, 16)
                sp.dma_start(wo[:], d["L0_ffn_wo"][layer].rearrange("(c p) n -> p c n", p=P)).then_inc(w_loaded, 16)
                sp.wait_ge(filled, 4)
                for c in range(NCH):
                    sp.wait_ge(v_kept, 4 * c + 4)
                    lo, hi = 4 * c, 4 * c + 4
                    end = min(hi, NT - 1)
                    sp.dma_start(v_prev[FF_WIN:P, lo:hi], v_own[0:FF_WIN, lo:hi]).then_inc(v_moved, 16)
                    sp.dma_start(v_prev[0:FF_WIN, lo + 1:end + 1], v_own[FF_WIN:P, lo:end]).then_inc(v_moved, 16)
                sp.wait_ge(v_moved, 32 * NCH)

            @block.tensor
            def _(pe):
                def turn_h(c):
                    since(pe, h_kept, 2 * c)
                    for j in range(4):
                        mm = pe.transpose(hp[:, j * P:(j + 1) * P], u[:, 4 * c + j, :], ident[:])
                    mm.then_inc(h_turned, 1)

                def turn(t):
                    pe.wait_ge(k_scaled, t + 1)
                    pe.wait_ge(q_scaled, t + 1)
                    since(pe, kept, 2 * t)
                    for i in range(2):
                        flat = tc[:, t % 4, i].rearrange("p h e -> p (h e)")
                        for c in range(FF_PAIRS):
                            mm = pe.transpose(tp[:, i, c * P:(c + 1) * P], flat[:, c * P:(c + 1) * P], ident[:])
                    mm.then_inc(turned, 1)

                turn_h(0)
                pe.wait_ge(w_loaded, 32)
                pe.wait_ge(filled, 4)
                for t in range(NT):
                    own = hT[:, t * P:(t + 1) * P]
                    if t % 4 == 0:
                        pe.wait_ge(h_kept, 2 * (t // 4) + 2)
                    since(pe, products, 3 * (t - 1))
                    since(pe, squared, t - 1)
                    for i in range(2):
                        mm = pe.matmul(qk[:, t % 2, i, :], own, w[:, i * FF_INNER:(i + 1) * FF_INNER], start=True, stop=True)
                    mm.then_inc(qk_done, 1)
                    since(pe, v_kept, t)
                    pe.matmul(vp[:], own, w[:, 2 * FF_INNER:], start=True, stop=True).then_inc(v_done, 1)
                    if t % 4 == 1 and t // 4 + 1 < NCH:
                        turn_h(t // 4 + 1)
                    if t >= 3:
                        turn(t - 3)
                for t in range(NT - 3, NT):
                    turn(t)

            @block.scalar
            def _(act):
                def keep(t):
                    act.wait_ge(turned, t + 1)
                    for i, (buf, pad) in enumerate(((qT, 0), (kT, FF_WIN))):
                        src = tp[:, i, :].rearrange("p (c n) -> p c n", c=FF_PAIRS)
                        act.activation(buf[:, :, pad + t * P:pad + (t + 1) * P], src, ACT.Copy).then_inc(kept, 1)

                def keep_h(c):
                    act.wait_ge(h_turned, c + 1)
                    act.activation(hT[0:64, c * 512:(c + 1) * 512], hp[0:64, :], ACT.Copy).then_inc(h_kept, 1)
                    n = 512 if (c + 1) * 512 % SEQ else 511
                    act.activation(hT[64:P, c * 512 + 1:c * 512 + 1 + n], hp[64:P, 0:n], ACT.Copy).then_inc(h_kept, 1)

                act.wait_ge(filled, 4)
                keep_h(0)
                for t in range(NT + 3):
                    if t < NT:
                        act.wait_ge(qk_done, t + 1)
                        since(act, summed, t)
                        act.activation(sq[:].rearrange("p i h e -> p i (h e)"), qk[:, t % 2], ACT.Square).then_inc(squared, 1)
                    if 1 <= t <= NT:
                        act.wait_ge(summed, t)
                        act.activation(norm[:, (t - 1) % 2], norm[:, (t - 1) % 2], ACT.Sqrt).then_inc(rooted, 1)
                    if t < NT:
                        act.wait_ge(v_done, t + 1)
                        act.activation(v_own[:, t, :, 0:FF_HD], vp[:].rearrange("p (h e) -> p h e", h=FF_HEADS),
                                       ACT.Copy).then_inc(v_kept, 1)
                        if t % 4 == 1 and t // 4 + 1 < NCH:
                            keep_h(t // 4 + 1)
                    if t >= 3:
                        keep(t - 3)

            @block.vector
            def _(dve):
                dve.wait_ge(loaded, 32)
                half = FF_HD // 2
                for i in range(2):
                    cosrow = srow[:, i, :].rearrange("p (o e) -> p o e", o=1).to_broadcast([P, QT, FF_HD])
                    dve.tensor_tensor(rot[:, i, 0], rot0[:, i, 0], cosrow, ALU.mult).then_inc(table_ready, 1)
                    for a, b in ((0, half), (half, 0)):
                        sinrow = srow[:, i, b:b + half].rearrange("p (o e) -> p o e", o=1).to_broadcast([P, QT, half])
                        dve.tensor_tensor(rot[:, i, 1, :, a:a + half], rot0[:, i, 1, :, a:a + half], sinrow,
                                          ALU.mult).then_inc(table_ready, 1)
                dve.wait_ge(table_ready, 6)

                def times_cos(t):
                    dve.wait_ge(squared, t + 1)
                    since(dve, turned, t - 3)
                    src = qk[:, t % 2].rearrange("p i (h e) -> p i h e", e=FF_HD)
                    cosb = rot[:, :, 0, t % QT, :].rearrange("p i (o e) -> p i o e", o=1).to_broadcast([P, *QK])
                    dve.tensor_tensor(tc[:, t % 4], src, cosb, ALU.mult).then_inc(products, 1)

                def times_sin(t):
                    since(dve, rotated, 2 * t)
                    src = qk[:, t % 2].rearrange("p i (h e) -> p i h e", e=FF_HD)
                    for a, b in ((0, half), (half, 0)):
                        sinb = rot[:, :, 1, t % QT, a:a + half].rearrange("p i (o e) -> p i o e", o=1)
                        dve.tensor_tensor(ts_[:, :, :, a:a + half], src[:, :, :, b:b + half],
                                          sinb.to_broadcast([P, 2, FF_HEADS, half]), ALU.mult).then_inc(products, 1)

                def clip(t):
                    dve.wait_ge(rooted, t + 1)
                    since(dve, q_scaled, t - 1)
                    since(dve, k_scaled, t - 1)
                    dve.tensor_scalar(rn[:, t % 2], norm[:, t % 2], 1e-12, None, ALU.max).then_inc(clipped, 1)

                for t in range(NT + 1):
                    if t < NT:
                        times_cos(t)
                    if t >= 1:
                        clip(t - 1)
                    if t < NT:
                        since(dve, clipped, t - 1)
                        dve.tensor_reduce(norm[:, t % 2], sq[:], AX.X, ALU.add).then_inc(summed, 1)
                    if t >= 1:
                        dve.wait_ge(clipped, t)
                        dve.reciprocal(rn[:, (t - 1) % 2], rn[:, (t - 1) % 2]).then_inc(inverted, 1)
                    if t < NT:
                        times_sin(t)
                    if t >= 1:
                        r = t - 1
                        dve.wait_ge(inverted, r + 1)
                        dve.wait_ge(rotated, 2 * r + 1)
                        rnb = rn[:, r % 2, 1, :].rearrange("p (h o) -> p h o", o=1).to_broadcast([P, FF_HEADS, FF_HD])
                        dve.tensor_tensor(tc[:, r % 4, 1], tc[:, r % 4, 1], rnb, ALU.mult).then_inc(k_scaled, 1)

            @block.gpsimd
            def _(pool):
                pool.memset(kT[:, :, 0:FF_WIN], 0.0).then_inc(filled, 1)
                pool.memset(v_own[:, :, :, FF_HD:FF_HD + 1], 1.0).then_inc(filled, 1)
                pool.wait_ge(filled, 2)
                pool.memset(v_prev[0:FF_WIN, 0], 0.0).then_inc(filled, 1)
                pool.wait_ge(filled, 3)
                pool.memset(hT[64:P].rearrange("p (b n) -> p b n", n=SEQ)[:, :, 0:1], 0.0).then_inc(filled, 1)
                for t in range(NT + 1):
                    if t < NT:
                        pool.wait_ge(products, 3 * t + 3)
                        for i in (1, 0):
                            pool.tensor_tensor(tc[:, t % 4, i], tc[:, t % 4, i], ts_[:, i], ALU.add).then_inc(rotated, 1)
                    if t >= 1:
                        r = t - 1
                        pool.wait_ge(rotated, 2 * r + 2)
                        pool.wait_ge(inverted, r + 1)
                        rnb = rn[:, r % 2, 0, :].rearrange("p (h o) -> p h o", o=1).to_broadcast([P, FF_HEADS, FF_HD])
                        pool.tensor_tensor(tc[:, r % 4, 0], tc[:, r % 4, 0], rnb, ALU.mult).then_inc(q_scaled, 1)


def ffn_windows(nc, u, d, cst, layer, tag, mask, h, qT, kT, v_own, v_prev, wo):
    ident = cst["ident"]
    HB = FF_HEADS // 2
    with stage(nc, tag) as st:
        maskb = st.sb("maskb", [P, 2, HB, P], BF16)
        identb = st.sb("identb", [P, P], BF16)
        mx = st.sb("mx", [P, 2, FF_HEADS])
        less = st.sb("less", [P, 2, FF_HEADS, P])
        prob = st.sb("prob", [P, 2, FF_HEADS, P])
        probT = st.sb("probT", [P, 2, FF_HEADS, P])
        rinv = st.sb("rinv", [P, 2, FF_HEADS])
        o = st.sb("o", [P, 2, FF_HEADS, FF_HD])
        oT = st.sb("oT", [P, 2, FF_PAIRS, P])
        scores = st.ps("scores", [P, 2, 512])
        turned = st.ps("turned", [P, 2, 512])
        outp = st.ps("outp", [P, 2, 512])
        oTp = st.ps("oTp", [P, 512])
        projp = st.ps("projp", [P, 512])
        cast, h_clear, h_stored = st.sem("cast"), st.sem("h_clear"), st.sem("h_stored")
        scored, max_ready, lessened, probs_ready = (st.sem(n) for n in ("scored", "max_ready", "lessened", "probs_ready"))
        probs_turned, t_kept, pv_done, inverted, o_ready = (st.sem(n) for n in ("probs_turned", "t_kept", "pv_done", "inverted", "o_ready"))
        o_turned, oT_kept, projected, added = (st.sem(n) for n in ("o_turned", "oT_kept", "projected", "added"))
        with nc.Block() as block:

            @block.sync
            def _(sp):
                sp.wait_ge(h_clear, 1)
                n = 0
                for c in range(NCH):
                    sp.wait_ge(added, 4 * c + 4)
                    lo, end = 4 * c, 4 * c + 4
                    sp.dma_start(h[1:P, lo:end, 64:D], u[0:P - 1, lo:end, 64:D]).then_inc(h_stored, 16)
                    last = end if end % QT else end - 1
                    sp.dma_start(h[0:1, lo + 1:last + 1, 64:D], u[P - 1:P, lo:last, 64:D]).then_inc(h_stored, 16)
                    n += 2
                sp.wait_ge(h_stored, 16 * n)

            @block.gpsimd
            def _(pool):
                first = h[0:1].rearrange("p (b t) c -> p b t c", b=BATCH)[:, :, 0, 64:D]
                pool.memset(first, 0.0).then_inc(h_clear, 1)
                for t in range(NT):
                    pool.wait_ge(added, t + 1)
                    pool.tensor_copy(h[:, t, 0:64], u[:, t, 0:64])

            @block.tensor
            def _(pe):
                def score(t):
                    if t >= 1:
                        pe.wait_ge(lessened, 2 * t)
                    which = 1 if t % QT == 0 else 0
                    for b in range(2):
                        pe.matmul(scores[:, b, :], identb[:], maskb[:, which].rearrange("p h n -> p (h n)"),
                                  start=True, stop=False, skip_group_check=True)
                        for h4 in range(HB):
                            rows, pair = slice(b * 64, b * 64 + 64), h4
                            for w in range(2):
                                k0 = t * P + w * FF_WIN
                                mm = pe.matmul(scores[w * 64:w * 64 + 64, b, h4 * P:(h4 + 1) * P],
                                               qT[rows, pair, t * P + w * 64:t * P + w * 64 + 64],
                                               kT[rows, pair, k0:k0 + P], start=False,
                                               stop=h4 == HB - 1, skip_group_check=True)
                    mm.then_inc(scored, 1)

                def turn(t):
                    pe.wait_ge(probs_ready, t + 1)
                    if t >= 1:
                        pe.wait_ge(t_kept, t)
                    for h in range(FF_HEADS):
                        mm = pe.transpose(turned[:, h // HB, h % HB * P:(h % HB + 1) * P], prob[:, t % 2, h, :], ident[:])
                    mm.then_inc(probs_turned, 1)

                def times_v(t):
                    pe.wait_ge(t_kept, t + 1)
                    since(pe, o_ready, 2 * t)
                    for h in range(FF_HEADS):
                        slot = h % 2 * HB + h // 2
                        for w, v in ((0, v_prev), (1, v_own)):
                            mm = pe.matmul(outp[w * 64:w * 64 + 64, h // HB, h % HB * 65:h % HB * 65 + 65],
                                           probT[:, t % 2, slot, w * 64:w * 64 + 64], v[:, t, h, :], start=True, stop=True)
                    mm.then_inc(pv_done, 1)

                def turn_o(t):
                    pe.wait_ge(o_ready, 2 * t + 2)
                    since(pe, oT_kept, t)
                    of = o[:, t % 2].rearrange("p h e -> p (h e)")
                    for c in range(FF_PAIRS):
                        mm = pe.transpose(oTp[:, c * P:(c + 1) * P], of[:, c * P:(c + 1) * P], ident[:])
                    mm.then_inc(o_turned, 1)

                def project(t):
                    pe.wait_ge(oT_kept, t + 1)
                    since(pe, added, t)
                    for c in range(FF_PAIRS):
                        mm = pe.matmul(projp[:, 0:D], oT[:, t % 2, c, :], wo[:, c, :], start=c == 0, stop=c == FF_PAIRS - 1)
                    mm.then_inc(projected, 1)

                pe.wait_ge(cast, 2)
                for t in range(NT + 4):
                    if t < NT:
                        score(t)
                    if 2 <= t < NT + 2:
                        times_v(t - 2)
                    if 1 <= t <= NT:
                        turn(t - 1)
                    if 3 <= t < NT + 3:
                        turn_o(t - 3)
                    if 4 <= t:
                        project(t - 4)

            @block.scalar
            def _(act):
                def keep(t):
                    act.wait_ge(probs_turned, t + 1)
                    since(act, pv_done, t - 1)
                    act.activation(probT[:, t % 2], turned[:].rearrange("p b (h n) -> p (b h) n", h=HB), ACT.Copy).then_inc(t_kept, 1)

                def keep_o(t):
                    act.wait_ge(o_turned, t + 1)
                    since(act, projected, t - 1)
                    act.activation(oT[:, t % 2].rearrange("p c n -> p (c n)"), oTp[:], ACT.Copy).then_inc(oT_kept, 1)

                for t in range(NT + 3):
                    if t < NT:
                        act.wait_ge(lessened, 2 * t + 2)
                        if t >= 2:
                            act.wait_ge(probs_turned, t - 1)
                        act.activation(prob[:, t % 2, :, :], less[:, t % 2, :, :], ACT.Exp, scale=8.0).then_inc(probs_ready, 1)
                    if 1 <= t <= NT:
                        keep(t - 1)
                    if 3 <= t:
                        keep_o(t - 3)

            @block.vector
            def _(dve):
                dve.tensor_copy(maskb[:], mask[:].rearrange("p k (o n) -> p k o n", o=1).to_broadcast([P, 2, HB, P])).then_inc(cast, 1)
                dve.tensor_copy(identb[:], ident[:]).then_inc(cast, 1)

                def normalise(t):
                    dve.wait_ge(pv_done, t + 1)
                    sums = outp[:, :, 0:HB * 65].rearrange("p b (h e) -> p b h e", e=65)
                    since(dve, o_ready, 2 * (t - 1))
                    since(dve, o_turned, t - 1)
                    dve.reciprocal(rinv[:, t % 2].rearrange("p (b h o) -> p b h o", b=2, o=1), sums[:, :, :, 64:65]).then_inc(inverted, 1)
                    dve.wait_ge(inverted, t + 1)
                    for b in range(2):
                        rb = rinv[:, t % 2, b * HB:(b + 1) * HB].rearrange("p (h o) -> p h o", o=1).to_broadcast([P, HB, FF_HD])
                        dve.tensor_tensor(o[:, t % 2, b * HB:(b + 1) * HB, :], sums[:, b, :, 0:FF_HD], rb, ALU.mult).then_inc(o_ready, 1)

                def add(t):
                    dve.wait_ge(projected, t + 1)
                    dve.tensor_tensor(u[:, t, :], u[:, t, :], projp[:, 0:D], ALU.add).then_inc(added, 1)

                for t in range(NT + 4):
                    if t < NT:
                        dve.wait_ge(scored, t + 1)
                        sv = scores[:].rearrange("p b (h n) -> p b h n", h=HB)
                        mxv = mx[:, t % 2, :].rearrange("p (b h) -> p b h", b=2)
                        dve.tensor_reduce(mxv, sv, AX.X, ALU.max).then_inc(max_ready, 1)
                        dve.wait_ge(max_ready, t + 1)
                        if t >= 2:
                            dve.wait_ge(probs_ready, t - 1)
                        for b in range(2):
                            mb = mx[:, t % 2, b * HB:(b + 1) * HB].rearrange("p (h o) -> p h o", o=1).to_broadcast([P, HB, P])
                            dve.tensor_tensor(less[:, t % 2, b * HB:(b + 1) * HB, :], sv[:, b], mb, ALU.subtract).then_inc(lessened, 1)
                    if 2 <= t < NT + 2:
                        normalise(t - 2)
                    if 4 <= t:
                        add(t - 4)


def ffn_glu(nc, u, d, cst, layer, tag, h):
    ident = cst["ident"]
    with stage(nc, tag) as st:
        hT = st.sb("hT", [D, TOK])
        w1 = st.sb("w1", [D, 2 * HID])
        w2 = st.sb("w2", [P, 3, D])
        b1 = st.sb("b1", [P, 6])
        b2 = st.sb("b2", [P, D])
        affine = st.sb("affine", [D, 2])
        act_g = st.sb("act_g", [P, 2, 3, 512])
        hid = st.sb("hid", [P, 2, 3, 512])
        banks = st.ps("banks", [P, 8, 512])
        loaded, affine_loaded, biased = st.sem("loaded"), st.sem("affine_loaded"), st.sem("biased")
        a_done, g_done, gelu_done, hid_done = (st.sem(n) for n in ("a_done", "g_done", "gelu_done", "hid_done"))
        down_done, added = st.sem("down_done"), st.sem("added")

        def load(sp):
            sp.dma_start(affine[:, 0:1], d["L0_ffn_ln_g"][layer].rearrange("(p o) -> p o", o=1)).then_inc(affine_loaded, 16)
            sp.dma_start(affine[:, 1:2], d["L0_ffn_ln_b"][layer].rearrange("(p o) -> p o", o=1)).then_inc(affine_loaded, 16)
            sp.dma_start(w1[:], d["L0_ffn_w1"][layer]).then_inc(loaded, 16)
            for j, (a, b) in enumerate(HID_CUT):
                sp.dma_start(w2[0:b - a, j, :], d["L0_ffn_w2"][layer][a:b, :]).then_inc(loaded, 16)
                for i in range(2):
                    src = d["L0_ffn_b1"][layer][i * HID + a:i * HID + b].rearrange("(p o) -> p o", o=1)
                    sp.dma_start(b1[0:b - a, 3 * i + j:3 * i + j + 1], src).then_inc(loaded, 16)
            sp.dma_start(b2[:], d["L0_ffn_b2"][bass.ts(layer, 1), :].to_broadcast([P, D])).then_inc(loaded, 16)

        ln = NormTurn(nc, st, h, h, hT, 1e-5, ident, banks[:, 6:8, :], affine, (affine_loaded, 32))
        with nc.Block() as block:

            @block.sync
            def _(sp):
                load(sp)

            @block.tensor
            def _(pe):
                def down(c):
                    pe.wait_ge(hid_done, 3 * c + 3)
                    for i in range(4):
                        for j, (a, b) in enumerate(HID_CUT):
                            mm = pe.matmul(banks[:, 7, i * P:(i + 1) * P], hid[0:b - a, c % 2, j, i * P:(i + 1) * P],
                                           w2[0:b - a, j, :], start=j == 0, stop=j == 2)
                    mm.then_inc(down_done, 1)

                for c in range(NCH):
                    ln.turn(pe, c)
                pe.wait_ge(loaded, 16 * 11)
                for c in range(NCH):
                    pe.wait_ge(ln.kept, c + 1)
                    for j, (a, b) in enumerate(HID_CUT):
                        if c >= 1:
                            pe.wait_ge(gelu_done, 3 * (c - 1) + j + 1)
                        pe.matmul(banks[0:b - a, 3 + j, :], w1[:, HID + a:HID + b], hT[:, c * 512:(c + 1) * 512],
                                  start=True, stop=True).then_inc(g_done, 1)
                        if c >= 1:
                            pe.wait_ge(hid_done, 3 * (c - 1) + j + 1)
                        pe.matmul(banks[0:b - a, j, :], w1[:, a:b], hT[:, c * 512:(c + 1) * 512],
                                  start=True, stop=True).then_inc(a_done, 1)
                    if c >= 1:
                        if c >= 2:
                            pe.wait_ge(added, c - 1)
                        else:
                            pe.wait_ge(ln.kept, NCH)
                        down(c - 1)
                pe.wait_ge(added, NCH - 1)
                down(NCH - 1)

            @block.gpsimd
            def _(pool):
                ln.norm.gpsimd(pool)
                pool.wait_ge(loaded, 16 * 11)
                b2v = b2[:].rearrange("p (o n) -> p o n", o=1).to_broadcast([P, NT, D])
                pool.tensor_tensor(u[:], u[:], b2v, ALU.add).then_inc(biased, 1)

            @block.scalar
            def _(act):
                ln.norm.scalar(act)
                for c in range(NCH):
                    ln.keep(act, c)
                act.wait_ge(loaded, 16 * 11)
                for c in range(NCH):
                    for j, (a, b) in enumerate(HID_CUT):
                        act.wait_ge(g_done, 3 * c + j + 1)
                        if c >= 2:
                            act.wait_ge(hid_done, 3 * (c - 2) + j + 1)
                        act.activation(act_g[0:b - a, c % 2, j, :], banks[0:b - a, 3 + j, :], ACT.Gelu,
                                       bias=b1[0:b - a, 3 + j:4 + j]).then_inc(gelu_done, 1)

            @block.vector
            def _(dve):
                ln.norm.vector(dve)
                dve.wait_ge(loaded, 16 * 11)

                def add(c):
                    dve.wait_ge(down_done, c + 1)
                    dve.wait_ge(biased, 1)
                    y = banks[:, 7, :].rearrange("p (t n) -> p t n", t=4)
                    dve.tensor_tensor(u[:, 4 * c:4 * c + 4, :], u[:, 4 * c:4 * c + 4, :], y, ALU.add).then_inc(added, 1)

                for c in range(NCH):
                    for j, (a, b) in enumerate(HID_CUT):
                        dve.wait_ge(a_done, 3 * c + j + 1)
                        dve.wait_ge(gelu_done, 3 * c + j + 1)
                        if c >= 2:
                            dve.wait_ge(down_done, c - 1)
                        dve.scalar_tensor_tensor(hid[0:b - a, c % 2, j, :], banks[0:b - a, j, :], b1[0:b - a, j:j + 1],
                                                 act_g[0:b - a, c % 2, j, :], ALU.add, ALU.mult).then_inc(hid_done, 1)
                    if c >= 1:
                        add(c - 1)
                add(NCH - 1)


NSTATE = 16


def attn_b(nc, x, d, cst):
    ident = cst["ident"]
    with stage(nc, "ab") as st:
        xn = st.sb("xn", [P, NT, D])
        xT = st.sb("xT", [D, TOK])
        banks = st.ps("banks", [P, 8, 512])
        z = st.sb("z", [D, TOK])
        dt = st.sb("dt", [D, TOK])
        dtx = st.sb("dtx", [D, TOK])
        y = st.sb("y", [D, TOK])
        attn_b_prepare(nc, x, d, cst, xn, xT, banks, z, dt, dtx)
        attn_b_scan(nc, d, xT, banks, dt, dtx, y)
        attn_b_finish(nc, x, d, banks, z, y)


def attn_b_prepare(nc, x, d, cst, xn, xT, banks, z, dt, dtx):
    with stage(nc, "bp") as st:
        w = st.sb("w", [D, 3, D])
        b = st.sb("b", [D, 3])
        pos = st.sb("pos", [D, TOK])
        loaded, projected = st.sem("loaded"), st.sem("projected")
        gate, dt_in, magnitude, decayed, plus_one, logged = (st.sem(n) for n in (
            "gate", "dt_in", "magnitude", "decayed", "plus_one", "logged"))
        positive, dt_ready, xs_ready, dtx_ready = (st.sem(n) for n in ("positive", "dt_ready", "xs_ready", "dtx_ready"))

        def load(sp):
            for i, name in enumerate(("z", "dt", "x")):
                sp.dma_start(w[:, i, :], d["L0_attn_b_W" + name]).then_inc(loaded, 16)
                sp.dma_start(b[:, i:i + 1], d["L0_attn_b_b" + name].rearrange("(p o) -> p o", o=1)).then_inc(loaded, 16)

        ln = NormTurn(nc, st, x, xn, xT, 1e-5, cst["ident"], banks[:, 6:8, :])
        with nc.Block() as block:

            @block.sync
            def _(sp):
                load(sp)

            @block.gpsimd
            def _(pool):
                ln.norm.gpsimd(pool)

            @block.tensor
            def _(pe):
                for c in range(NCH):
                    ln.turn(pe, c)
                pe.wait_ge(loaded, 96)
                for c in range(NCH):
                    pe.wait_ge(ln.kept, c + 1)
                    for i, used in enumerate((gate, dt_in, xs_ready)):
                        if c >= 2:
                            pe.wait_ge(used, c - 1)
                        pe.matmul(banks[:, 2 * i + c % 2, :], w[:, i, :], xT[:, c * 512:(c + 1) * 512], start=True,
                                  stop=True).then_inc(projected, 1)

            @block.scalar
            def _(act):
                ln.norm.scalar(act)
                for c in range(NCH):
                    ln.keep(act, c)
                for c in range(NCH):
                    act.wait_ge(projected, 3 * c + 1)
                    act.activation(z[:, c * 512:(c + 1) * 512], banks[:, c % 2, :], ACT.Sigmoid, bias=b[:, 0:1]).then_inc(gate, 1)
                act.wait_ge(positive, 1)
                act.activation(dt[:], dt[:], ACT.Abs).then_inc(magnitude, 1)
                act.wait_ge(magnitude, 1)
                act.activation(dt[:], dt[:], ACT.Exp, scale=-1.0).then_inc(decayed, 1)
                act.wait_ge(plus_one, 1)
                act.activation(dt[:], dt[:], ACT.Ln).then_inc(logged, 1)

            @block.vector
            def _(dve):
                ln.norm.vector(dve)
                dve.wait_ge(loaded, 96)
                for c in range(NCH):
                    cs = slice(c * 512, (c + 1) * 512)
                    dve.wait_ge(projected, 3 * c + 2)
                    dve.tensor_scalar(dt[:, cs], banks[:, 2 + c % 2, :], b[:, 1:2], None, ALU.add).then_inc(dt_in, 1)
                    dve.wait_ge(projected, 3 * c + 3)
                    dve.tensor_scalar(dtx[:, cs], banks[:, 4 + c % 2, :], b[:, 2:3], None, ALU.add).then_inc(xs_ready, 1)
                dve.wait_ge(dt_in, NCH)
                dve.tensor_scalar(pos[:], dt[:], 0.0, None, ALU.max).then_inc(positive, 1)
                dve.wait_ge(decayed, 1)
                dve.tensor_scalar(dt[:], dt[:], 1.0, None, ALU.add).then_inc(plus_one, 1)
                dve.wait_ge(logged, 1)
                dve.tensor_tensor(dt[:], dt[:], pos[:], ALU.add).then_inc(dt_ready, 1)
                dve.wait_ge(dt_ready, 1)
                dve.wait_ge(xs_ready, NCH)
                dve.tensor_tensor(dtx[:], dtx[:], dt[:], ALU.mult).then_inc(dtx_ready, 1)


def attn_b_scan(nc, d, xT, banks, dt, dtx, y):
    with stage(nc, "bs") as st:
        wrow = st.sb("wrow", [D, 2, NSTATE])
        wrep = st.sb("wrep", [D, 2, NSTATE, D])
        brow = st.sb("brow", [D, 2, NSTATE])
        a = st.sb("a", [D, NSTATE])
        decay = st.sb("decay", [D, 2, SEQ])
        inp = st.sb("inp", [D, 2, SEQ])
        h = st.sb("h", [D, 2, SEQ])
        hc = st.sb("hc", [D, 2, SEQ])
        loaded, repeated, a_exp, a_ready = (st.sem(n) for n in ("loaded", "repeated", "a_exp", "a_ready"))
        b_done, c_done, decay_ready, inp_ready, scanned, hc_ready, y_added, y_zero = (st.sem(n) for n in (
            "b_done", "c_done", "decay_ready", "inp_ready", "scanned", "hc_ready", "y_added", "y_zero"))
        N = BATCH * NSTATE
        with nc.Block() as block:

            @block.sync
            def _(sp):
                for i, name in enumerate("BC"):
                    sp.dma_start(wrow[:, i, :], d["L0_attn_b_W" + name]).then_inc(loaded, 16)
                    sp.dma_start(brow[:, i, :], row_of(d["L0_attn_b_b" + name], D)).then_inc(loaded, 16)
                sp.dma_start(a[:], d["L0_attn_b_A_log"]).then_inc(loaded, 16)

            @block.tensor
            def _(pe):
                pe.wait_ge(repeated, 2)

                def project(i, k, bank, sem):
                    for c in range(2):
                        tok = (k // NSTATE) * SEQ + c * 512
                        mm = pe.matmul(banks[:, bank + c, :], wrep[:, i, k % NSTATE, :], xT[:, tok:tok + 512],
                                       start=True, stop=True)
                    mm.then_inc(sem, 1)

                for k in range(N):
                    if k >= 2:
                        pe.wait_ge(inp_ready, k - 1)
                    project(0, k, 2 * (k % 2), b_done)
                    if k >= 2:
                        pe.wait_ge(hc_ready, k - 1)
                    project(1, k, 4 + 2 * (k % 2), c_done)

            @block.scalar
            def _(act):
                act.wait_ge(loaded, 80)
                act.activation(a[:], a[:], ACT.Exp).then_inc(a_exp, 1)
                act.wait_ge(a_ready, 1)
                for k in range(N):
                    if k >= 2:
                        act.wait_ge(scanned, k - 1)
                    tok = (k // NSTATE) * SEQ
                    act.activation(decay[:, k % 2, :], dt[:, tok:tok + SEQ], ACT.Exp,
                                   scale=a[:, k % NSTATE:k % NSTATE + 1]).then_inc(decay_ready, 1)

            @block.vector
            def _(dve):
                dve.wait_ge(loaded, 80)
                for i in range(2):
                    src = wrow[:, i, :].rearrange("p (n o) -> p n o", o=1).to_broadcast([D, NSTATE, D])
                    dve.tensor_copy(wrep[:, i, :, :], src).then_inc(repeated, 1)
                dve.wait_ge(a_exp, 1)
                dve.tensor_scalar(a[:], a[:], -1.0, None, ALU.mult).then_inc(a_ready, 1)

                def feed(k):
                    tok, n = (k // NSTATE) * SEQ, k % NSTATE
                    dve.wait_ge(b_done, k + 1)
                    bank = 2 * (k % 2)
                    if k >= 2:
                        dve.wait_ge(scanned, k - 1)
                    dve.scalar_tensor_tensor(inp[:, k % 2, :], banks[:, bank:bank + 2, :].rearrange("p b c -> p (b c)"),
                                             brow[:, 0, n:n + 1], dtx[:, tok:tok + SEQ], ALU.add, ALU.mult).then_inc(inp_ready, 1)

                def scan(k):
                    dve.wait_ge(decay_ready, k + 1)
                    dve.wait_ge(inp_ready, k + 1)
                    if k >= 2:
                        dve.wait_ge(hc_ready, k - 1)
                    dve.tensor_tensor_scan(h[:, k % 2, :], decay[:, k % 2, :], inp[:, k % 2, :], 0.0, ALU.mult,
                                           ALU.add).then_inc(scanned, 1)

                def weigh(k):
                    n = k % NSTATE
                    dve.wait_ge(c_done, k + 1)
                    dve.wait_ge(scanned, k + 1)
                    if k >= 2:
                        dve.wait_ge(y_added, k - 1)
                    bank = 4 + 2 * (k % 2)
                    dve.scalar_tensor_tensor(hc[:, k % 2, :], banks[:, bank:bank + 2, :].rearrange("p b c -> p (b c)"),
                                             brow[:, 1, n:n + 1], h[:, k % 2, :], ALU.add, ALU.mult).then_inc(hc_ready, 1)

                feed(0)
                for k in range(N):
                    scan(k)
                    if k + 1 < N:
                        feed(k + 1)
                    weigh(k)

            @block.gpsimd
            def _(pool):
                pool.memset(y[:], 0.0).then_inc(y_zero, 1)
                pool.wait_ge(y_zero, 1)
                for k in range(N):
                    tok = (k // NSTATE) * SEQ
                    pool.wait_ge(hc_ready, k + 1)
                    if k >= 1:
                        pool.wait_ge(y_added, k)
                    pool.tensor_tensor(y[:, tok:tok + SEQ], y[:, tok:tok + SEQ], hc[:, k % 2, :], ALU.add).then_inc(y_added, 1)


def attn_b_finish(nc, x, d, banks, z, y):
    with stage(nc, "bf") as st:
        w = st.sb("w", [D, D])
        b = st.sb("b", [P, D])
        loaded, gated, biased, projected, added = (st.sem(n) for n in ("loaded", "gated", "biased", "projected", "added"))
        with nc.Block() as block:

            @block.sync
            def _(sp):
                sp.dma_start(w[:], d["L0_attn_b_Wout"]).then_inc(loaded, 16)
                sp.dma_start(b[:], row_of(d["L0_attn_b_bout"], P)).then_inc(loaded, 16)

            @block.tensor
            def _(pe):
                pe.wait_ge(loaded, 32)
                for c in range(NCH):
                    pe.wait_ge(gated, c + 1)
                    for j in range(4):
                        t = 4 * c + j
                        mm = pe.matmul(banks[:, c, j * P:(j + 1) * P], y[:, t * P:(t + 1) * P], w[:], start=True, stop=True)
                    mm.then_inc(projected, 1)

            @block.vector
            def _(dve):
                for c in range(NCH):
                    cs = slice(c * 512, (c + 1) * 512)
                    dve.tensor_tensor(y[:, cs], y[:, cs], z[:, cs], ALU.mult).then_inc(gated, 1)
                dve.wait_ge(loaded, 32)
                bv = b[:].rearrange("p (o n) -> p o n", o=1).to_broadcast([P, NT, D])
                dve.tensor_tensor(x[:], x[:], bv, ALU.add).then_inc(biased, 1)
                dve.wait_ge(biased, 1)
                for c in range(NCH):
                    dve.wait_ge(projected, c + 1)
                    src = banks[:, c, :].rearrange("p (t n) -> p t n", t=4)
                    dve.tensor_tensor(x[:, 4 * c:4 * c + 4, :], x[:, 4 * c:4 * c + 4, :], src, ALU.add).then_inc(added, 1)


DF_HD = 8
DF_V = 2 * DF_HD
LAMBDA_INIT = 0.8
DF_STACK = len(Q_PARTS) * DF_HD


def diff(nc, x, d, cst):
    G = BATCH * HEADS
    with stage(nc, "df") as st:
        qh = st.dram("qh", (2 * G, DF_STACK, SEQ), BF16)
        kh = st.dram("kh", (2 * G, DF_STACK, SEQ), BF16)
        ctx = st.sb("ctx", [P, QT, G, DF_V])
        vh = st.sb("vh", [P, QT, G, DF_V])
        neglam = st.sb("neglam", [P, G])
        diff_prepare(nc, x, d, cst, qh, kh, vh, neglam)
        diff_heads(nc, cst, d, ctx, vh, qh, kh, neglam)
        diff_finish(nc, x, d, cst, ctx)


def diff_prepare(nc, x, d, cst, qh, kh, vh, neglam):
    ident = cst["ident"]
    WD = HEADS * DF_V
    with stage(nc, "dp") as st:
        banks = st.ps("banks", [P, 8, 512])
        w = st.sb("w", [D, 3, WD])
        lamrow = st.sb("lamrow", [P, 4, HEADS * DF_HD])
        lamprod = st.sb("lamprod", [P, 2, HEADS * DF_HD])
        lam = st.sb("lam", [P, 2, HEADS])
        xT = st.sb("xT", [D, TOK])
        xn = st.sb("xn", [P, NT, D])
        val = st.sb("val", [P, 2, TOK])
        rest = st.sb("rest", [P, 2, TOK])
        parts = st.sb("parts", [P, 2, 3, TOK], BF16)
        loaded, projected, evac = st.sem("loaded"), st.sem("projected"), st.sem("evac")
        high, less, mid, split = (st.sem(n) for n in ("high", "less", "mid", "split"))
        v_mm, v_ready, stored = st.sem("v_mm"), st.sem("v_ready"), [st.sem(f"stored{i}") for i in range(2)]
        lam_step, lam_exp = st.sem("lam_step"), st.sem("lam_exp")
        UNITS, NW = 4, BATCH * 3

        def load(sp):
            for i, name in enumerate("qkv"):
                sp.dma_start(w[:, i, :], d["L1_attn_a_W" + name]).then_inc(loaded, 16)
            for i, name in enumerate(("q1", "k1", "q2", "k2")):
                src = d["L1_attn_a_lambda_" + name].rearrange("(o h) e -> o (h e)", o=1).to_broadcast([P, HEADS * DF_HD])
                sp.dma_start(lamrow[:, i, :], src).then_inc(loaded, 16)

        ln = NormTurn(nc, st, x, xn, xT, 1e-5, ident, banks[:, 4:6, :])
        with nc.Block() as block:

            @block.sync
            def _(sp):
                load(sp)
                for r in range(UNITS):
                    sp.wait_ge(split, r + 1)
                    dst_all, order = ((qh, Q_PARTS), (kh, K_PARTS))[r // 2]
                    for b in range(BATCH):
                        g0 = b * HEADS + r % 2 * 8
                        rows = dst_all[2 * g0:2 * g0 + 16].rearrange("h (e r) c -> (h e) r c", e=DF_HD)
                        for dst, src in stacked(rows, parts[:, r % 2, :, b * SEQ:(b + 1) * SEQ], order):
                            sp.dma_start(dst, src).then_inc(stored[r % 2], 16)
                for i in range(2):
                    sp.wait_ge(stored[i], 16 * NW * 2)

            @block.gpsimd
            def _(pool):
                ln.norm.gpsimd(pool)

            @block.tensor
            def _(pe):
                for c in range(NCH):
                    ln.turn(pe, c)
                pe.wait_ge(loaded, 7 * 16)
                for r in range(UNITS):
                    for c in range(NCH):
                        if r == 0:
                            pe.wait_ge(ln.kept, c + 1)
                        if r >= 1 or c >= 2:
                            pe.wait_ge(evac, NCH * r + c - 1)
                        lhs = w[:, r // 2, r % 2 * P:(r % 2 + 1) * P]
                        pe.matmul(banks[:, c % 2, :], lhs, xT[:, c * 512:(c + 1) * 512], start=True,
                                  stop=True).then_inc(projected, 1)
                for t in range(NT // 2):
                    if t >= 2:
                        pe.wait_ge(v_ready, t - 1)
                    for j in range(2):
                        mm = pe.matmul(banks[:, 2 + t % 2, j * WD:(j + 1) * WD], xT[:, (2 * t + j) * P:(2 * t + j + 1) * P],
                                       w[:, 2, :], start=True, stop=True)
                    mm.then_inc(v_mm, 1)

            @block.scalar
            def _(act):
                ln.norm.scalar(act)
                for c in range(NCH):
                    ln.keep(act, c)
                act.wait_ge(lam_step, 3)
                act.activation(lam[:], lam[:], ACT.Exp).then_inc(lam_exp, 1)
                for r in range(UNITS):
                    act.wait_ge(evac, NCH * (r + 1))
                    if r >= 2:
                        act.wait_ge(stored[r % 2], 16 * NW)
                    act.activation(parts[:, r % 2, 0, :], val[:, r % 2, :], ACT.Copy).then_inc(high, 1)
                    act.wait_ge(less, r + 1)
                    act.activation(parts[:, r % 2, 1, :], rest[:, r % 2, :], ACT.Copy).then_inc(mid, 1)

            @block.vector
            def _(dve):
                ln.norm.vector(dve)
                dve.wait_ge(loaded, 7 * 16)
                for i in range(2):
                    dve.tensor_tensor(lamprod[:, i, :], lamrow[:, 2 * i, :], lamrow[:, 2 * i + 1, :], ALU.mult).then_inc(lam_step, 1)
                dve.wait_ge(lam_step, 2)
                dve.tensor_reduce(lam[:], lamprod[:].rearrange("p i (h e) -> p i h e", e=DF_HD), AX.X, ALU.add).then_inc(lam_step, 1)
                for r in range(UNITS):
                    for c in range(NCH):
                        dve.wait_ge(projected, NCH * r + c + 1)
                        if r >= 2 and c == 0:
                            dve.wait_ge(split, r - 1)
                        factor = 1.0 / math.sqrt(DF_HD) if r < 2 else 1.0
                        dve.tensor_scalar(val[:, r % 2, c * 512:(c + 1) * 512], banks[:, c % 2, :], factor, None,
                                          ALU.mult).then_inc(evac, 1)
                    dve.wait_ge(high, r + 1)
                    dve.tensor_tensor(rest[:, r % 2, :], val[:, r % 2, :], parts[:, r % 2, 0, :], ALU.subtract).then_inc(less, 1)
                    dve.wait_ge(mid, r + 1)
                    dve.tensor_tensor(parts[:, r % 2, 2, :], rest[:, r % 2, :], parts[:, r % 2, 1, :], ALU.subtract).then_inc(split, 1)
                for t in range(NT // 2):
                    dve.wait_ge(v_mm, t + 1)
                    b, k0 = 2 * t // QT, 2 * t % QT
                    dst = vh[:, k0:k0 + 2, b * HEADS:(b + 1) * HEADS, :].rearrange("p t g e -> p t (g e)")
                    dve.tensor_copy(dst, banks[:, 2 + t % 2, :].rearrange("p (t n) -> p t n", t=2)).then_inc(v_ready, 1)
                dve.wait_ge(lam_exp, 1)
                for b in range(BATCH):
                    dve.tensor_tensor(neglam[:, b * HEADS:(b + 1) * HEADS], lam[:, 1, :], lam[:, 0, :], ALU.subtract).then_inc(lam_step, 1)
                dve.wait_ge(lam_step, 5)
                dve.tensor_scalar(neglam[:], neglam[:], LAMBDA_INIT, None, ALU.subtract).then_inc(lam_step, 1)


def diff_heads(nc, cst, d, ctx, vh, qh, kh, neglam):
    ident = cst["ident"]
    G = BATCH * HEADS
    NSTEP = 2 * QT
    M2 = 64
    with stage(nc, "dh") as st:
        q_s = st.sb("q", [P, 2, SEQ], BF16)
        k_s = st.sb("k", [P, 2, SEQ], BF16)
        mask = st.sb("mask", [P, P])
        maskb = st.sb("maskb", [P, P], BF16)
        identb = st.sb("identb", [P, P], BF16)
        prob = st.sb("prob", [P, 2, 2, SEQ])
        both = st.sb("both", [P, 2, SEQ])
        probT = st.sb("probT", [P, 2, QT, P])
        v_s = st.sb("v", [P, 2, QT, VCOLS])
        outT = st.sb("outT", [P, 2, P])
        gather = st.sb("gather", [P, DF_V])
        negmax = st.sb("negmax", [P, 2, 2])
        rowsum = st.sb("rowsum", [P, 2, QT, 2])
        rinv = st.sb("rinv", [P, 2, QT, 2])
        coef = st.sb("coef", [P, 2])
        scores = st.ps("scores", [P, 2, 2, 512])
        turned = st.ps("turned", [P, QT, P])
        outp = st.ps("outp", [P, 512])
        ctxp = st.ps("ctxp", [P, QT, DF_V])
        mask_loaded, cast = st.sem("mask_loaded"), st.sem("cast")
        ops_loaded = [st.sem(f"ops_loaded{i}") for i in range(2)]
        scored = [st.sem(f"scored{m}") for m in range(2)]
        max_ready = [st.sem(f"max_ready{m}") for m in range(2)]
        probs_ready = [st.sem(f"probs_ready{m}") for m in range(2)]
        inverted, coef_ready, combined = st.sem("inverted"), st.sem("coef_ready"), st.sem("combined")
        probs_turned, turned_kept = st.sem("probs_turned"), st.sem("turned_kept")
        v_clear, v_placed = st.sem("v_clear"), st.sem("v_placed")
        pv_done, out_kept, gathered, ctx_kept = (st.sem(n) for n in ("pv_done", "out_kept", "gathered", "ctx_kept"))

        def passes(eng, run):
            run(0, True, False)
            with eng.Fori(1, G // 2 - 1) as i:
                run(i, False, False)
            run(G // 2 - 1, False, True)

        with nc.Block() as block:

            @block.sync
            def _(sp):
                def load_head(g, par):
                    for m in range(2):
                        rows = slice(m * M2, m * M2 + DF_STACK)
                        sp.dma_start(q_s[rows, par, :], qh[2 * g + m]).then_inc(ops_loaded[par], 16)
                        sp.dma_start(k_s[rows, par, :], kh[2 * g + m]).then_inc(ops_loaded[par], 16)

                def run(i, first, last):
                    for par in range(1 if last else 2):
                        g1 = 2 * i + par + 1
                        since(sp, scored[1], QT * (g1 - 1))
                        load_head(g1, 1 - par)

                sp.dma_start(mask[:], d["causal"]).then_inc(mask_loaded, 16)
                sp.dma_start(gather[:], cst["gather16"]).then_inc(mask_loaded, 16)
                load_head(0, 0)
                passes(sp, run)

            @block.tensor
            def _(pe):
                def score(n, s, first):
                    par, t = s // QT, s % QT
                    width = (t + 1) * P
                    for m in range(2):
                        if not (first and s < 1):
                            pe.wait_ge(probs_ready[m], n)
                        rows = slice(m * M2, m * M2 + DF_STACK)
                        for bank in range((width + 511) // 512):
                            b0, b1 = bank * 512, min(width, bank * 512 + 512)
                            diag = b1 == width
                            mm = pe.matmul(scores[:, m, bank, 0:b1 - b0], q_s[rows, par, t * P:(t + 1) * P],
                                           k_s[rows, par, b0:b1], start=True, stop=not diag, skip_group_check=True)
                            if diag:
                                mm = pe.matmul(scores[:, m, bank, b1 - P - b0:b1 - b0], identb[:], maskb[:],
                                               start=False, stop=True, skip_group_check=True)
                        mm.then_inc(scored[m], 1)

                def turn(n, s, g):
                    t = s % QT
                    pe.wait_ge(combined, n + 1)
                    since(pe, turned_kept, n)
                    for kt in range(t + 1):
                        mm = pe.transpose(turned[:, kt, :], both[:, s % 2, kt * P:(kt + 1) * P], ident[:])
                    mm.then_inc(probs_turned, 1)

                def times_v(n, s, g):
                    t = s % QT
                    if t == 0:
                        pe.wait_ge(v_placed, g + 1)
                    pe.wait_ge(turned_kept, n + 1)
                    since(pe, out_kept, n)
                    for kt in range(t + 1):
                        r = kt % 4 * 32
                        mm = pe.matmul(outp[r:r + VCOLS, 0:P], v_s[:, s // QT, kt, :], probT[:, s % 2, kt, :],
                                       start=kt < 4, stop=kt + 4 > t, tile_position=(0, r), skip_group_check=True)
                    mm.then_inc(pv_done, 1)

                def add_parts(n, s, g):
                    t = s % QT
                    rows = slice(0, 32 * min(t + 1, 4))
                    pe.wait_ge(out_kept, n + 1)
                    if t == 0:
                        since(pe, ctx_kept, g)
                    pe.matmul(ctxp[:, t, :], outT[rows, s % 2, :], gather[rows, :], start=True,
                              stop=True).then_inc(gathered, 1)

                def run(i, first, last):
                    for s in range(NSTEP):
                        n, par, t = NSTEP * i + s, s // QT, s % QT
                        if t == 0:
                            pe.wait_ge(ops_loaded[par], 64 * (i + 1))
                        score(n, s, first)
                        if not (first and s < 2):
                            turn(*back(i, s, 2, NSTEP))
                        if not (first and s < 3):
                            times_v(*back(i, s, 3, NSTEP))
                        if not (first and s < 4):
                            add_parts(*back(i, s, 4, NSTEP))

                pe.wait_ge(cast, 2)
                passes(pe, run)
                for k in range(4):
                    if k < 2:
                        turn(*back(G // 2, k, 2, NSTEP))
                    if k < 3:
                        times_v(*back(G // 2, k, 3, NSTEP))
                    add_parts(*back(G // 2, k, 4, NSTEP))

            @block.vector
            def _(dve):
                dve.wait_ge(mask_loaded, 32)
                dve.tensor_copy(maskb[:], mask[:]).then_inc(cast, 1)
                dve.tensor_copy(identb[:], ident[:]).then_inc(cast, 1)

                def invert(n, s, g):
                    dve.wait_ge(probs_ready[1], n + 1)
                    if s % QT == 0:
                        since(dve, ctx_kept, g - 1)
                    dve.reciprocal(rinv[:, s // QT, s % QT, :], rowsum[:, s // QT, s % QT, :]).then_inc(inverted, 1)

                def take_coef(n, s, g):
                    dve.wait_ge(inverted, n + 1)
                    since(dve, combined, n - 1)
                    dve.scalar_tensor_tensor(coef[:, s % 2:s % 2 + 1], rinv[:, s // QT, s % QT, 1:2],
                                             rowsum[:, s // QT, s % QT, 0:1], neglam[:, bass.ts(g, 1)],
                                             ALU.mult, ALU.mult).then_inc(coef_ready, 1)

                def combine(n, s, g):
                    width = (s % QT + 1) * P
                    dve.wait_ge(coef_ready, n + 1)
                    since(dve, probs_turned, n - 1)
                    dve.scalar_tensor_tensor(both[:, s % 2, 0:width], prob[:, s % 2, 1, 0:width], coef[:, s % 2:s % 2 + 1],
                                             prob[:, s % 2, 0, 0:width], ALU.mult, ALU.add).then_inc(combined, 1)

                def keep_out(n, s, g):
                    rows = slice(0, 32 * min(s % QT + 1, 4))
                    dve.wait_ge(pv_done, n + 1)
                    since(dve, gathered, n - 1)
                    dve.tensor_copy(outT[rows, s % 2, :], outp[rows, 0:P]).then_inc(out_kept, 1)

                def keep_ctx(g, par):
                    dve.wait_ge(gathered, QT * (g + 1))
                    over = rinv[:, par, :, 0:1].to_broadcast([P, QT, DF_V])
                    dve.tensor_tensor(ctx[:, :, g, :], ctxp[:], over, ALU.mult).then_inc(ctx_kept, 1)

                def run(i, first, last):
                    for s in range(NSTEP):
                        n, width = NSTEP * i + s, (s % QT + 1) * P

                        def take_max(m):
                            dve.wait_ge(scored[m], n + 1)
                            row = scores[:, m, :, :].rearrange("p b c -> p (b c)")[:, 0:width]
                            dve.tensor_reduce(negmax[:, s % 2, m:m + 1], row, AX.X, ALU.max, negate=True).then_inc(max_ready[m], 1)

                        if not (first and s < 4):
                            keep_out(*back(i, s, 4, NSTEP))
                        if s % QT == 4 and not (first and s < QT):
                            keep_ctx(2 * i + s // QT - 1, 1 - s // QT)
                        take_max(0)
                        if not (first and s < 1):
                            invert(*back(i, s, 1, NSTEP))
                        take_max(1)
                        if not (first and s < 1):
                            take_coef(*back(i, s, 1, NSTEP))
                            combine(*back(i, s, 1, NSTEP))

                passes(dve, run)
                for k in range(4):
                    keep_out(*back(G // 2, k, 4, NSTEP))
                    if k == 0:
                        invert(*back(G // 2, 0, 1, NSTEP))
                        take_coef(*back(G // 2, 0, 1, NSTEP))
                        combine(*back(G // 2, 0, 1, NSTEP))
                keep_ctx(G - 1, 1)

            @block.scalar
            def _(act):
                def keep_turned(n, s, g):
                    t = s % QT
                    act.wait_ge(probs_turned, n + 1)
                    since(act, pv_done, n - 1)
                    act.activation(probT[:, s % 2, 0:t + 1, :], turned[:, 0:t + 1, :], ACT.Copy).then_inc(turned_kept, 1)

                def run(i, first, last):
                    for s in range(NSTEP):
                        n, width = NSTEP * i + s, (s % QT + 1) * P
                        if not (first and s < 3):
                            keep_turned(*back(i, s, 3, NSTEP))
                        for m in range(2):
                            act.wait_ge(max_ready[m], n + 1)
                            if m == 0 and not (first and s < 2):
                                act.wait_ge(combined, n - 1)
                            if m == 0 and not (first and s < 4):
                                act.wait_ge(coef_ready, n - 3)
                            row = scores[:, m, :, :].rearrange("p b c -> p (b c)")[:, 0:width]
                            act.activation(prob[:, s % 2, m, 0:width], row, ACT.Exp, bias=negmax[:, s % 2, m:m + 1],
                                           accum_out=rowsum[:, s // QT, s % QT, m:m + 1]).then_inc(probs_ready[m], 1)

                passes(act, run)
                for k in range(3):
                    keep_turned(*back(G // 2, k, 3, NSTEP))

            @block.gpsimd
            def _(pool):
                def run(i, first, last):
                    for par in range(2):
                        place_v(pool, v_s, vh, DF_V, v_placed, pv_done, 2 * i + par, par, first)

                pool.memset(v_s[:], 0.0).then_inc(v_clear, 1)
                pool.wait_ge(v_clear, 1)
                passes(pool, run)


def diff_finish(nc, x, d, cst, ctx):
    ident = cst["ident"]
    G = BATCH * HEADS
    with stage(nc, "dz") as st:
        sq = st.sb("sq", [P, QT, G, DF_V])
        ms = st.sb("ms", [P, QT, G])
        scol = st.sb("scol", [P, 1])
        wo = st.sb("wo", [P, 2, D])
        oT = st.sb("oT", [P, 2, 2, P])
        banks = st.ps("banks", [P, 4, 512])
        loaded, squared, summed, meaned, rooted, inverted, s_ready, wo_ready, scaled = (st.sem(n) for n in (
            "loaded", "squared", "summed", "meaned", "rooted", "inverted", "s_ready", "wo_ready", "scaled"))
        turned, kept, projected, added = (st.sem(n) for n in ("turned", "kept", "projected", "added"))
        HALF = QT // 2
        with nc.Block() as block:

            @block.sync
            def _(sp):
                sp.dma_start(wo[:], d["L1_attn_a_Wo"].rearrange("(c p) n -> p c n", p=P)).then_inc(loaded, 16)
                sp.dma_start(scol[:], d["rms_scale_col"]).then_inc(loaded, 16)

            @block.gpsimd
            def _(pool):
                pool.wait_ge(loaded, 32)
                pool.tensor_scalar(scol[:], scol[:], 1.0 - LAMBDA_INIT, None, ALU.mult).then_inc(s_ready, 1)
                pool.wait_ge(s_ready, 1)
                pool.tensor_scalar(wo[:], wo[:], scol[:, 0:1], None, ALU.mult).then_inc(wo_ready, 1)

            @block.scalar
            def _(act):
                for k in range(2):
                    half = slice(k * HALF, (k + 1) * HALF)
                    act.activation(sq[:, half], ctx[:, half], ACT.Square).then_inc(squared, 1)
                for k in range(2):
                    act.wait_ge(meaned, k + 1)
                    act.activation(ms[:, k * HALF:(k + 1) * HALF], ms[:, k * HALF:(k + 1) * HALF], ACT.Sqrt).then_inc(rooted, 1)
                for t in range(NT):
                    act.wait_ge(turned, t + 1)
                    since(act, projected, t - 1)
                    act.activation(oT[:, t % 2, :, :], banks[:, t % 2, 0:2 * P].rearrange("p (c n) -> p c n", c=2),
                                   ACT.Copy).then_inc(kept, 1)

            @block.vector
            def _(dve):
                for k in range(2):
                    half = slice(k * HALF, (k + 1) * HALF)
                    dve.wait_ge(squared, k + 1)
                    dve.tensor_reduce(ms[:, half], sq[:, half], AX.X, ALU.add).then_inc(summed, 1)
                    dve.wait_ge(summed, k + 1)
                    dve.tensor_scalar(ms[:, half], ms[:, half], 1.0 / DF_V, 1e-5, ALU.mult, ALU.add).then_inc(meaned, 1)
                for k in range(2):
                    half = slice(k * HALF, (k + 1) * HALF)
                    dve.wait_ge(rooted, k + 1)
                    dve.reciprocal(ms[:, half], ms[:, half]).then_inc(inverted, 1)
                    dve.wait_ge(inverted, k + 1)
                    for qt in range(k * HALF, (k + 1) * HALF):
                        rb = ms[:, qt, :].rearrange("p (g o) -> p g o", o=1).to_broadcast([P, G, DF_V])
                        dve.tensor_tensor(ctx[:, qt], ctx[:, qt], rb, ALU.mult).then_inc(scaled, 1)
                for t in range(NT):
                    tile = t % BATCH * QT + t // BATCH
                    dve.wait_ge(projected, t + 1)
                    dve.tensor_tensor(x[:, tile, :], x[:, tile, :], banks[:, 2 + t % 2, 0:D], ALU.add).then_inc(added, 1)

            @block.tensor
            def _(pe):
                def turn(t):
                    b, qt = t % BATCH, t // BATCH
                    pe.wait_ge(scaled, qt + 1)
                    since(pe, kept, t - 1)
                    src = ctx[:, qt, b * HEADS:(b + 1) * HEADS, :].rearrange("p g e -> p (g e)")
                    for c in range(2):
                        mm = pe.transpose(banks[:, t % 2, c * P:(c + 1) * P], src[:, c * P:(c + 1) * P], ident[:])
                    mm.then_inc(turned, 1)

                turn(0)
                pe.wait_ge(wo_ready, 1)
                for t in range(NT):
                    if t + 1 < NT:
                        turn(t + 1)
                    pe.wait_ge(kept, t + 1)
                    since(pe, added, t - 1)
                    for c in range(2):
                        mm = pe.matmul(banks[:, 2 + t % 2, 0:D], oT[:, t % 2, c, :], wo[:, c, :], start=c == 0, stop=c == 1)
                    mm.then_inc(projected, 1)


SW_HID = 384
SW_CUT = SW_HID // P
DEQUANT = 1.0 / 127.0


def swiglu(nc, x, d, cst, tag):
    ident = cst["ident"]
    with stage(nc, tag) as st:
        xn = st.sb("xn", [P, NT, D])
        xT = st.sb("xT", [D, TOK])
        wi = st.sb("wi", [P, 3, SW_HID], I32)
        w = st.sb("w", [P, 3, SW_HID])
        act_g = st.sb("act_g", [P, 2, SW_CUT, 512])
        hid = st.sb("hid", [P, 2, SW_CUT, 512])
        banks = st.ps("banks", [P, 8, 512])
        loaded, w_ready = st.sem("loaded"), st.sem("w_ready")
        u_done, g_done, silu_done, hid_done = (st.sem(n) for n in ("u_done", "g_done", "silu_done", "hid_done"))
        down_done, added = st.sem("down_done"), st.sem("added")

        def load(sp):
            sp.dma_start(wi[:, 0, :], d["w_gateT"]).then_inc(loaded, 16)
            sp.dma_start(wi[:, 1, :], d["w_upT"]).then_inc(loaded, 16)
            sp.dma_start(wi[:, 2, :].rearrange("p (c n) -> p c n", n=D),
                         d["w_downT"].rearrange("(c p) n -> p c n", p=P)).then_inc(loaded, 16)

        ln = NormTurn(nc, st, x, xn, xT, 1e-5, ident, banks[:, 6:8, :])
        with nc.Block() as block:

            @block.sync
            def _(sp):
                load(sp)

            @block.gpsimd
            def _(pool):
                ln.norm.gpsimd(pool)

            @block.tensor
            def _(pe):
                def down(c):
                    pe.wait_ge(hid_done, SW_CUT * (c + 1))
                    for i in range(4):
                        for j in range(SW_CUT):
                            mm = pe.matmul(banks[:, 6 + c % 2, i * P:(i + 1) * P], hid[:, c % 2, j, i * P:(i + 1) * P],
                                           w[:, 2, j * D:(j + 1) * D], start=j == 0, stop=j == SW_CUT - 1)
                    mm.then_inc(down_done, 1)

                for c in range(NCH):
                    ln.turn(pe, c)
                pe.wait_ge(w_ready, 1)
                for c in range(NCH):
                    pe.wait_ge(ln.kept, c + 1)
                    for j in range(SW_CUT):
                        rhs = xT[:, c * 512:(c + 1) * 512]
                        if c >= 1:
                            pe.wait_ge(silu_done, SW_CUT * (c - 1) + j + 1)
                        pe.matmul(banks[:, j, :], w[:, 0, j * P:(j + 1) * P], rhs, start=True, stop=True).then_inc(g_done, 1)
                        if c >= 1:
                            pe.wait_ge(hid_done, SW_CUT * (c - 1) + j + 1)
                        pe.matmul(banks[:, 3 + j, :], w[:, 1, j * P:(j + 1) * P], rhs, start=True, stop=True).then_inc(u_done, 1)
                    if c >= 1:
                        if c >= 3:
                            pe.wait_ge(added, c - 2)
                        elif c == 1:
                            pe.wait_ge(ln.kept, NCH)
                        down(c - 1)
                pe.wait_ge(added, NCH - 2)
                down(NCH - 1)

            @block.scalar
            def _(act):
                ln.norm.scalar(act)
                for c in range(NCH):
                    ln.keep(act, c)
                for k in range(NCH * SW_CUT):
                    c, j = k // SW_CUT, k % SW_CUT
                    act.wait_ge(g_done, k + 1)
                    if c >= 2:
                        act.wait_ge(hid_done, k - 2 * SW_CUT + 1)
                    act.activation(act_g[:, c % 2, j, :], banks[:, j, :], ACT.Silu).then_inc(silu_done, 1)

            @block.vector
            def _(dve):
                ln.norm.vector(dve)
                dve.wait_ge(loaded, 48)
                dve.tensor_scalar(w[:], wi[:], DEQUANT, None, ALU.mult).then_inc(w_ready, 1)

                def add(c):
                    dve.wait_ge(down_done, c + 1)
                    y = banks[:, 6 + c % 2, :].rearrange("p (t n) -> p t n", t=4)
                    dve.tensor_tensor(x[:, 4 * c:4 * c + 4, :], x[:, 4 * c:4 * c + 4, :], y, ALU.add).then_inc(added, 1)

                for k in range(NCH * SW_CUT):
                    c, j = k // SW_CUT, k % SW_CUT
                    dve.wait_ge(u_done, k + 1)
                    dve.wait_ge(silu_done, k + 1)
                    if c >= 2:
                        dve.wait_ge(down_done, c - 1)
                    dve.tensor_tensor(hid[:, c % 2, j, :], banks[:, 3 + j, :], act_g[:, c % 2, j, :], ALU.mult).then_inc(hid_done, 1)
                    if j == SW_CUT - 1 and c >= 1:
                        add(c - 1)
                add(NCH - 1)


LN_DEPTH = 6


def linear(nc, x, d, cst):
    with stage(nc, "li") as st:
        y = st.sb("y", [P, NT, D])
        layer_norm(nc, st, x, y, 1e-5)
        with nc.Fori(0, LN_DEPTH) as layer:
            linear_layer(nc, y, d, cst, layer)
        added = st.sem("added")
        with nc.Block() as block:

            @block.vector
            def _(dve):
                dve.tensor_tensor(x[:], x[:], y[:], ALU.add).then_inc(added, 1)


def linear_layer(nc, y, d, cst, layer):
    ident = cst["ident"]
    with stage(nc, "ll") as st:
        h = st.sb("h", [P, NT, D])
        hT = st.sb("hT", [D, TOK])
        w = st.sb("w", [D, 3 * D])
        wo = st.sb("wo", [D, D])
        bo = st.sb("bo", [P, D])
        affine = st.sb("affine", [D, 2])
        qe = st.sb("qe", [D, 2, SEQ])
        q = st.sb("q", [P, 2, QT, D])
        k = st.sb("k", [P, 2, QT, D])
        vT = st.sb("vT", [D, 2, SEQ])
        qmax, qsum, qinv = st.sb("qmax", [D, 2]), st.sb("qsum", [D, 2]), st.sb("qinv", [D, 2])
        kmax, ksum = st.sb("kmax", [P, 2, QT]), st.sb("ksum", [P, 2, QT])
        mT, mw = st.sb("mT", [D, 2, D]), st.sb("mw", [D, 2, D])
        banks = st.ps("banks", [P, 8, 512])
        loaded, biased = st.sem("loaded"), st.sem("biased")
        q_done, q_max, q_exp, q_turned, q_kept, q_inv = (st.sem(n) for n in ("q_done", "q_max", "q_exp", "q_turned", "q_kept", "q_inv"))
        k_done, k_max, k_exp, k_inv, k_ready = (st.sem(n) for n in ("k_done", "k_max", "k_exp", "k_inv", "k_ready"))
        v_done, v_kept = st.sem("v_done"), st.sem("v_kept")
        m_done, m_kept, mw_done, mw_kept, out_done, added = (st.sem(n) for n in (
            "m_done", "m_kept", "mw_done", "mw_kept", "out_done", "added"))
        two = lambda ap: ap.rearrange("p b c -> p (b c)")

        def load(sp):
            sp.dma_start(affine[:, 0:1], d["L1_attn_b_gamma"][layer].rearrange("(p o) -> p o", o=1)).then_inc(loaded, 16)
            sp.dma_start(affine[:, 1:2], d["L1_attn_b_beta"][layer].rearrange("(p o) -> p o", o=1)).then_inc(loaded, 16)
            sp.dma_start(w[:], d["L1_attn_b_w_qkv"][layer]).then_inc(loaded, 16)
            sp.dma_start(wo[:], d["L1_attn_b_w_out"][layer]).then_inc(loaded, 16)
            sp.dma_start(bo[:], d["L1_attn_b_b_out"][bass.ts(layer, 1), :].to_broadcast([P, D])).then_inc(loaded, 16)

        ln = NormTurn(nc, st, y, h, hT, 1e-5, ident, banks[:, 6:8, :], affine, (loaded, 80))
        with nc.Block() as block:

            @block.sync
            def _(sp):
                load(sp)

            @block.gpsimd
            def _(pool):
                ln.norm.gpsimd(pool)
                ln.norm.wait_chunk(pool, NCH - 1)
                pool.wait_ge(loaded, 80)
                bv = bo[:].rearrange("p (o n) -> p o n", o=1).to_broadcast([P, NT, D])
                pool.tensor_tensor(y[:], y[:], bv, ALU.add).then_inc(biased, 1)

            @block.tensor
            def _(pe):
                def project(b):
                    pe.wait_ge(ln.kept, 2 * b + 2)
                    for c in range(2):
                        cs = slice(b * SEQ + c * 512, b * SEQ + (c + 1) * 512)
                        mm = pe.matmul(banks[:, c, :], w[:, 0:D], hT[:, cs], start=True, stop=True)
                    mm.then_inc(q_done, 1)
                    if b >= 1:
                        pe.wait_ge(k_exp, QT)
                    for t in range(QT):
                        tok = b * SEQ + t * P
                        mm = pe.matmul(banks[:, 2 + t // 4, t % 4 * P:(t % 4 + 1) * P], hT[:, tok:tok + P], w[:, D:2 * D],
                                       start=True, stop=True)
                    mm.then_inc(k_done, 1)
                    if b >= 1:
                        pe.wait_ge(v_kept, 1)
                    for c in range(2):
                        cs = slice(b * SEQ + c * 512, b * SEQ + (c + 1) * 512)
                        mm = pe.matmul(banks[:, 4 + c, :], w[:, 2 * D:], hT[:, cs], start=True, stop=True)
                    mm.then_inc(v_done, 1)

                def turn_q(b):
                    pe.wait_ge(q_exp, b + 1)
                    if b >= 1:
                        pe.wait_ge(q_kept, 1)
                    for t in range(QT):
                        mm = pe.transpose(banks[:, 6 + t // 4, t % 4 * P:(t % 4 + 1) * P], qe[:, b, t * P:(t + 1) * P], ident[:])
                    mm.then_inc(q_turned, 1)

                def mix(b):
                    pe.wait_ge(q_kept, b + 1)
                    pe.wait_ge(k_ready, b + 1)
                    for t in range(QT):
                        mm = pe.matmul(banks[:, 4, 0:D], q[:, b, t, :], k[:, b, t, :], start=t == 0, stop=t == QT - 1)
                    mm.then_inc(m_done, 1)
                    pe.wait_ge(m_kept, b + 1)
                    pe.matmul(banks[:, 5, 0:D], mT[:, b, :], wo[:], start=True, stop=True).then_inc(mw_done, 1)
                    pe.wait_ge(mw_kept, b + 1)
                    for t in range(QT):
                        mm = pe.matmul(banks[:, 2 * b + t // 4, t % 4 * P:(t % 4 + 1) * P], vT[:, b, t * P:(t + 1) * P],
                                       mw[:, b, :], start=True, stop=True)
                    mm.then_inc(out_done, 1)

                for c in range(NCH):
                    ln.turn(pe, c)
                pe.wait_ge(loaded, 80)
                project(0)
                pe.wait_ge(ln.kept, NCH)
                turn_q(0)
                project(1)
                turn_q(1)
                pe.wait_ge(v_kept, 2)
                pe.wait_ge(k_exp, 2 * QT)
                mix(0)
                mix(1)

            @block.scalar
            def _(act):
                ln.norm.scalar(act)
                for c in range(NCH):
                    ln.keep(act, c)
                for b in range(BATCH):
                    act.wait_ge(q_max, b + 1)
                    act.activation(qe[:, b, :], two(banks[:, 0:2, :]), ACT.Exp, bias=qmax[:, b:b + 1],
                                   accum_out=qsum[:, b:b + 1]).then_inc(q_exp, 1)
                    act.wait_ge(k_max, b + 1)
                    for t in range(QT):
                        src = banks[:, 2 + t // 4, t % 4 * P:(t % 4 + 1) * P]
                        act.activation(k[:, b, t, :], src, ACT.Exp, bias=kmax[:, b, t:t + 1],
                                       accum_out=ksum[:, b, t:t + 1]).then_inc(k_exp, 1)
                    act.wait_ge(v_done, b + 1)
                    act.activation(vT[:, b, :], two(banks[:, 4:6, :]), ACT.Copy).then_inc(v_kept, 1)
                    act.wait_ge(q_turned, b + 1)
                    act.activation(q[:, b].rearrange("p t n -> p (t n)"), two(banks[:, 6:8, :]), ACT.Copy).then_inc(q_kept, 1)
                for b in range(BATCH):
                    act.wait_ge(mw_done, b + 1)
                    act.activation(mw[:, b, :], banks[:, 5, 0:D], ACT.Copy).then_inc(mw_kept, 1)

            @block.vector
            def _(dve):
                ln.norm.vector(dve)
                for b in range(BATCH):
                    dve.wait_ge(q_done, b + 1)
                    dve.tensor_reduce(qmax[:, b:b + 1], two(banks[:, 0:2, :]), AX.X, ALU.max, negate=True).then_inc(q_max, 1)
                    dve.wait_ge(k_done, b + 1)
                    kp = two(banks[:, 2:4, :]).rearrange("p (t n) -> p t n", n=D)
                    dve.tensor_reduce(kmax[:, b, :], kp, AX.X, ALU.max, negate=True).then_inc(k_max, 1)
                    dve.wait_ge(q_exp, b + 1)
                    dve.reciprocal(qinv[:, b:b + 1], qsum[:, b:b + 1]).then_inc(q_inv, 1)
                for b in range(BATCH):
                    dve.wait_ge(k_exp, QT * (b + 1))
                    dve.reciprocal(ksum[:, b, :], ksum[:, b, :]).then_inc(k_inv, 1)
                    dve.wait_ge(k_inv, b + 1)
                    kb = ksum[:, b, :].rearrange("p (t o) -> p t o", o=1).to_broadcast([P, QT, D])
                    dve.tensor_tensor(k[:, b], k[:, b], kb, ALU.mult).then_inc(k_ready, 1)
                for b in range(BATCH):
                    dve.wait_ge(m_done, b + 1)
                    dve.wait_ge(q_inv, b + 1)
                    dve.tensor_scalar(mT[:, b, :], banks[:, 4, 0:D], qinv[:, b:b + 1], None, ALU.mult).then_inc(m_kept, 1)
                    dve.wait_ge(out_done, b + 1)
                    dve.wait_ge(biased, 1)
                    out = two(banks[:, 2 * b:2 * b + 2, :]).rearrange("p (t n) -> p t n", n=D)
                    ys = y[:, b * QT:(b + 1) * QT, :]
                    dve.tensor_tensor(ys, ys, out, ALU.add).then_inc(added, 1)


STAGES = ("attn_a", "ffn0", "attn_b", "ffn1", "diff", "swiglu0", "linear", "swiglu1")


def build_program(nc, d, stages=STAGES):
    with ExitStack() as stack:
        x = stack.enter_context(nc.sbuf_tensor("residual", [P, NT, D], F32))
        ident = stack.enter_context(nc.sbuf_tensor("ident_s", [P, P], F32))
        loaded = stack.enter_context(nc.semaphore("stream_loaded"))
        out_stored = stack.enter_context(nc.semaphore("out_stored"))
        cst = {"ident": ident, "mask_c": d["mask_c"], "mask_p": d["mask_p"],
               "gather8": d["gather8"], "gather16": d["gather16"]}
        with nc.Block() as block:

            @block.sync
            def _(sp):
                for b in range(BATCH):
                    src = d["x_in"][b * SEQ:(b + 1) * SEQ, :].rearrange("(t p) c -> p t c", p=P)
                    sp.dma_start(x[:, b * QT:(b + 1) * QT, :], src).then_inc(loaded, 16)
                sp.dma_start(ident[:], d["ident"]).then_inc(loaded, 16)
                sp.wait_ge(loaded, 48)
        for s in stages:
            if s == "attn_a":
                attn_a(nc, x, d, cst)
            if s in ("ffn0", "ffn1"):
                ffn(nc, x, d, cst, s)
            if s == "attn_b":
                attn_b(nc, x, d, cst)
            if s == "diff":
                diff(nc, x, d, cst)
            if s in ("swiglu0", "swiglu1"):
                swiglu(nc, x, d, cst, s)
            if s == "linear":
                linear(nc, x, d, cst)
        with nc.Block() as block:

            @block.sync
            def _(sp):
                sp.dma_start(d["out"].rearrange("(t p) c -> p t c", p=P), x[:]).then_inc(out_stored, 16)
                sp.wait_ge(out_stored, 16)


def layout(inputs):
    a = {k: np.ascontiguousarray(v) for k, v in inputs.items()}
    a["x_in"] = a.pop("L0_attn_a_hidden_states").reshape(TOK, D)
    a["relT"] = np.ascontiguousarray(a.pop("L0_attn_a_rel_embeddings").T)
    a["ident"] = np.eye(P, dtype=np.float32)
    a.update(attn_a_constants())
    a.update(ffn_constants())
    a["causal"] = np.where(np.arange(P)[None, :] <= np.arange(P)[:, None], 0.0, NEG).astype(np.float32)
    scale = a.pop("L1_attn_a_rms_scale")
    a["rms_scale_col"] = np.tile(scale, P // len(scale)).reshape(P, 1)
    for name in ("gate", "up", "down"):
        a[f"w_{name}T"] = np.ascontiguousarray(a.pop(f"L1_ffn_w_{name}").T)
    return a


def kernel(**inputs):
    import concourse.bacc as _bacc
    from concourse.bass_utils import run_bass_kernel_spmd as _run

    nc = _bacc.Bacc("TRN2", target_bir_lowering=False, num_devices=1)
    arrays, d = {}, {}
    for name, a in layout({k: np.asarray(v) for k, v in inputs.items()}).items():
        if name == "L0_attn_a_attention_mask":
            continue
        arrays[f"in_{name}"] = a
        d[name] = nc.dram_tensor(f"in_{name}", a.shape, mybir.dt.from_np(a.dtype), kind="ExternalInput").ap()
    d["out"] = nc.dram_tensor("out_0", (TOK, D), F32, kind="ExternalOutput").ap()
    build_program(nc, d)
    r = _run(nc, [arrays], core_ids=[0])
    return r.results[0]["out_0"].reshape(BATCH, SEQ, D)
```
